# Optimizing a Trainium2 kernel written in Bass

```python
import numpy as np
import jax
import jax.numpy as jnp

def _softmax(x, axis=-1):
    return jax.nn.softmax(x, axis=axis)

def _gelu(x):
    return jax.nn.gelu(x, approximate=True)

def _silu(x):
    return jax.nn.silu(x)

def _sigmoid(x):
    return jax.nn.sigmoid(x)

def _layernorm(x, axis=-1, eps=1e-05):
    m = jnp.mean(x, axis=axis, keepdims=True)
    v = jnp.var(x, axis=axis, keepdims=True)
    return (x - m) / jnp.sqrt(v + eps)

def _scatter_add(tgt, idx, src, axis=0):
    return tgt.at[idx].add(src)

def _segment_sum(src, seg, n):
    return jax.ops.segment_sum(src, seg, n)
kernel_name = 'mk_hybrid_d2_jaxref_r8_c00146'

def setup_inputs(seed: int=0):
    np.random.seed(seed)
    _w = jnp.asarray

    def _L0_attn_a_setup():
        import jax, jax.numpy as jnp
        import numpy as np
        import math
        D_MODEL = 512
        NUM_HEADS = 32
        NUM_KV_HEADS = 8
        HEAD_DIM = D_MODEL // NUM_HEADS
        GROUP = NUM_HEADS // NUM_KV_HEADS
        SEQ_LEN = 256
        BATCH = 2
        ROPE_THETA = 10000.0

        def apply_rope(x, start_pos=0):
            b, h, s, hd = x.shape
            inv_freq = 1.0 / ROPE_THETA ** (jnp.arange(0, hd, 2, dtype=jnp.float32) / hd)
            pos = jnp.arange(start_pos, start_pos + s, dtype=jnp.float32)
            ang = pos[:, None] * inv_freq[None, :]
            cos = jnp.cos(ang).astype(x.dtype)
            sin = jnp.sin(ang).astype(x.dtype)
            xr = x[..., 0::2]
            xi = x[..., 1::2]
            out_r = xr * cos - xi * sin
            out_i = xr * sin + xi * cos
            return jnp.stack([out_r, out_i], axis=-1).reshape(b, h, s, hd)
        key = jax.random.key(seed)
        ks = jax.random.split(key, 5)
        qkv_dim = HEAD_DIM * (NUM_HEADS + 2 * NUM_KV_HEADS)
        scale = 1.0 / math.sqrt(D_MODEL)
        return {'x': jax.random.normal(ks[0], (BATCH, SEQ_LEN, D_MODEL), jnp.float32), 'w_qkv': jax.random.normal(ks[1], (qkv_dim, D_MODEL), jnp.float32) * scale, 'b_qkv': jax.random.normal(ks[2], (qkv_dim,), jnp.float32) * 0.01, 'w_o': jax.random.normal(ks[3], (D_MODEL, D_MODEL), jnp.float32) * scale, 'b_o': jax.random.normal(ks[4], (D_MODEL,), jnp.float32) * 0.01}
    _L0_attn_a_in = _L0_attn_a_setup()

    def _L0_attn_b_setup():
        import jax, jax.numpy as jnp
        import numpy as np
        H_M, P_M, G_M, N_M, K_CONV, CHUNK = (128, 64, 8, 128, 4, 128)
        D_MODEL = 512
        D_INNER = H_M * P_M
        CONV_DIM = D_INNER + 2 * G_M * N_M
        PROJ_DIM = D_INNER + CONV_DIM + H_M
        EPS = 1e-05

        def segsum(x):
            l = x.shape[-1]
            xe = jnp.broadcast_to(x[..., None], x.shape + (l,))
            m1 = jnp.tril(jnp.ones((l, l), dtype=bool), -1)
            s = jnp.cumsum(jnp.where(m1, xe, 0.0), axis=-2)
            m2 = jnp.tril(jnp.ones((l, l), dtype=bool), 0)
            return jnp.where(m2, s, -jnp.inf)

        def causal_conv(x, w, bconv):
            k = w.shape[1]
            s = x.shape[1]
            xp = jnp.pad(x, ((0, 0), (k - 1, 0), (0, 0)))
            y = sum((xp[:, i:i + s, :] * w[:, i] for i in range(k)))
            return y + bconv
        key = jax.random.key(seed)
        ks = jax.random.split(key, 8)
        B_, S = (1, 256)
        sc = 0.02
        return {'x': jax.random.normal(ks[0], (B_, S, D_MODEL), dtype=jnp.float32), 'norm_w': jnp.ones((D_MODEL,), dtype=jnp.float32), 'in_proj_w': jax.random.normal(ks[1], (PROJ_DIM, D_MODEL), dtype=jnp.float32) * sc, 'conv_w': jax.random.normal(ks[2], (CONV_DIM, K_CONV), dtype=jnp.float32) * 0.2, 'conv_b': jnp.zeros((CONV_DIM,), dtype=jnp.float32), 'dt_bias': jax.random.uniform(ks[3], (H_M,), dtype=jnp.float32) * 0.1, 'A_log': jnp.log(1.0 + 15.0 * jax.random.uniform(ks[4], (H_M,), dtype=jnp.float32)), 'Dp': jnp.ones((H_M,), dtype=jnp.float32), 'gnorm_w': jnp.ones((D_INNER,), dtype=jnp.float32), 'out_proj_w': jax.random.normal(ks[5], (D_MODEL, D_INNER), dtype=jnp.float32) * sc}
    _L0_attn_b_in = _L0_attn_b_setup()

    def _L0_ffn_setup():
        import jax, jax.numpy as jnp
        import numpy as np
        D_MODEL = 512
        D_FF = 1376
        key = jax.random.key(seed)
        k1, k2, k3, k4 = jax.random.split(key, 4)
        x = jax.random.normal(k1, (2, 256, D_MODEL), dtype=jnp.float32)
        W_gate = jax.random.normal(k2, (D_FF, D_MODEL), dtype=jnp.float32) * D_MODEL ** (-0.5)
        W_up = jax.random.normal(k3, (D_FF, D_MODEL), dtype=jnp.float32) * D_MODEL ** (-0.5)
        W_down = jax.random.normal(k4, (D_MODEL, D_FF), dtype=jnp.float32) * D_FF ** (-0.5)
        return {'x': x, 'W_gate': W_gate, 'W_up': W_up, 'W_down': W_down}
    _L0_ffn_in = _L0_ffn_setup()

    def _L1_attn_a_setup():
        import jax, jax.numpy as jnp
        import numpy as np
        B, C, L = (64, 64, 512)
        key = jax.random.key(seed)
        x = jax.random.normal(key, (B, C, L), dtype=jnp.float32)
        return {'x': x}
    _L1_attn_a_in = _L1_attn_a_setup()

    def _L1_attn_b_setup():
        import jax, jax.numpy as jnp
        import numpy as np
        HIDDEN = 512
        N_HEADS = 32
        HEAD_DIM = HIDDEN // N_HEADS
        BATCH = 2
        SEQ = 256
        ROPE_BASE = 10000.0

        def _rope_cos_sin(seq_len, head_dim, dtype):
            inv_freq = 1.0 / ROPE_BASE ** (jnp.arange(0, head_dim, 2, dtype=jnp.float32) / head_dim)
            t = jnp.arange(seq_len, dtype=jnp.float32)
            freqs = t[:, None] * inv_freq[None, :]
            emb = jnp.concatenate([freqs, freqs], axis=-1)
            return (jnp.cos(emb).astype(dtype), jnp.sin(emb).astype(dtype))

        def _rotate_half(x):
            d = x.shape[-1] // 2
            return jnp.concatenate([-x[..., d:], x[..., :d]], axis=-1)
        key = jax.random.key(seed)
        ks = jax.random.split(key, 5)
        s = 1.0 / np.sqrt(HIDDEN)
        return {'hidden_states': jax.random.normal(ks[0], (BATCH, SEQ, HIDDEN), dtype=jnp.float32), 'Wq': jax.random.normal(ks[1], (HIDDEN, HIDDEN), dtype=jnp.float32) * s, 'Wk': jax.random.normal(ks[2], (HIDDEN, HIDDEN), dtype=jnp.float32) * s, 'Wv': jax.random.normal(ks[3], (HIDDEN, HIDDEN), dtype=jnp.float32) * s, 'Wo': jax.random.normal(ks[4], (HIDDEN, HIDDEN), dtype=jnp.float32) * s}
    _L1_attn_b_in = _L1_attn_b_setup()

    def _L1_ffn_setup():
        import jax, jax.numpy as jnp
        import numpy as np
        H = 512
        I = 1376
        R = 32
        NLEV = 16
        Q_ZERO = 7.5
        Q_STEP = 0.005
        LR_SCALE = 0.02

        def _qlinear(x, q, scale, A, Bm):
            w = (q.astype(jnp.float32) - Q_ZERO) * (scale * Q_STEP)[:, None]
            y = jnp.einsum('bsh,oh->bso', x, w)
            return y + LR_SCALE * (x @ A @ Bm)
        key = jax.random.key(seed)
        ks = jax.random.split(key, 13)
        B, S = (2, 256)
        inp = {'x': jax.random.normal(ks[0], (B, S, H), jnp.float32), 'gate_q': jax.random.randint(ks[1], (I, H), 0, NLEV, jnp.int32), 'gate_scale': jax.random.uniform(ks[2], (I,), jnp.float32), 'gate_A': jax.random.normal(ks[3], (H, R), jnp.float32), 'gate_B': jax.random.normal(ks[4], (R, I), jnp.float32), 'up_q': jax.random.randint(ks[5], (I, H), 0, NLEV, jnp.int32), 'up_scale': jax.random.uniform(ks[6], (I,), jnp.float32), 'up_A': jax.random.normal(ks[7], (H, R), jnp.float32), 'up_B': jax.random.normal(ks[8], (R, I), jnp.float32), 'down_q': jax.random.randint(ks[9], (H, I), 0, NLEV, jnp.int32), 'down_scale': jax.random.uniform(ks[10], (H,), jnp.float32), 'down_A': jax.random.normal(ks[11], (I, R), jnp.float32), 'down_B': jax.random.normal(ks[12], (R, H), jnp.float32)}
        return inp
    _L1_ffn_in = _L1_ffn_setup()
    _d = {'L0_attn_a_x': _L0_attn_a_in['x'], 'L0_attn_a_w_qkv': _L0_attn_a_in['w_qkv'], 'L0_attn_a_b_qkv': _L0_attn_a_in['b_qkv'], 'L0_attn_a_w_o': _L0_attn_a_in['w_o'], 'L0_attn_a_b_o': _L0_attn_a_in['b_o'], 'L0_attn_b_norm_w': _L0_attn_b_in['norm_w'], 'L0_attn_b_in_proj_w': _L0_attn_b_in['in_proj_w'], 'L0_attn_b_conv_w': _L0_attn_b_in['conv_w'], 'L0_attn_b_conv_b': _L0_attn_b_in['conv_b'], 'L0_attn_b_dt_bias': _L0_attn_b_in['dt_bias'], 'L0_attn_b_A_log': _L0_attn_b_in['A_log'], 'L0_attn_b_Dp': _L0_attn_b_in['Dp'], 'L0_attn_b_gnorm_w': _L0_attn_b_in['gnorm_w'], 'L0_attn_b_out_proj_w': _L0_attn_b_in['out_proj_w'], 'L0_ffn_W_gate': _L0_ffn_in['W_gate'], 'L0_ffn_W_up': _L0_ffn_in['W_up'], 'L0_ffn_W_down': _L0_ffn_in['W_down'], 'L1_attn_b_Wq': _L1_attn_b_in['Wq'], 'L1_attn_b_Wk': _L1_attn_b_in['Wk'], 'L1_attn_b_Wv': _L1_attn_b_in['Wv'], 'L1_attn_b_Wo': _L1_attn_b_in['Wo'], 'L1_ffn_gate_q': _L1_ffn_in['gate_q'], 'L1_ffn_gate_scale': _L1_ffn_in['gate_scale'], 'L1_ffn_gate_A': _L1_ffn_in['gate_A'], 'L1_ffn_gate_B': _L1_ffn_in['gate_B'], 'L1_ffn_up_q': _L1_ffn_in['up_q'], 'L1_ffn_up_scale': _L1_ffn_in['up_scale'], 'L1_ffn_up_A': _L1_ffn_in['up_A'], 'L1_ffn_up_B': _L1_ffn_in['up_B'], 'L1_ffn_down_q': _L1_ffn_in['down_q'], 'L1_ffn_down_scale': _L1_ffn_in['down_scale'], 'L1_ffn_down_A': _L1_ffn_in['down_A'], 'L1_ffn_down_B': _L1_ffn_in['down_B']}
    _x0 = _d['L0_attn_a_x']
    _d['L0_attn_a_x'] = jax.random.normal(jax.random.fold_in(jax.random.key(seed), 1), (4, 256, 512), dtype=_x0.dtype)
    del _x0
    return _d

def reference(L0_attn_a_x, L0_attn_a_w_qkv, L0_attn_a_b_qkv, L0_attn_a_w_o, L0_attn_a_b_o, L0_attn_b_norm_w, L0_attn_b_in_proj_w, L0_attn_b_conv_w, L0_attn_b_conv_b, L0_attn_b_dt_bias, L0_attn_b_A_log, L0_attn_b_Dp, L0_attn_b_gnorm_w, L0_attn_b_out_proj_w, L0_ffn_W_gate, L0_ffn_W_up, L0_ffn_W_down, L1_attn_b_Wq, L1_attn_b_Wk, L1_attn_b_Wv, L1_attn_b_Wo, L1_ffn_gate_q, L1_ffn_gate_scale, L1_ffn_gate_A, L1_ffn_gate_B, L1_ffn_up_q, L1_ffn_up_scale, L1_ffn_up_A, L1_ffn_up_B, L1_ffn_down_q, L1_ffn_down_scale, L1_ffn_down_A, L1_ffn_down_B):

    def _L0_attn_a_ref(x, w_qkv, b_qkv, w_o, b_o):
        import jax, jax.numpy as jnp
        import numpy as np
        import math
        D_MODEL = 512
        NUM_HEADS = 32
        NUM_KV_HEADS = 8
        HEAD_DIM = D_MODEL // NUM_HEADS
        GROUP = NUM_HEADS // NUM_KV_HEADS
        SEQ_LEN = 256
        BATCH = 2
        ROPE_THETA = 10000.0

        def apply_rope(x, start_pos=0):
            b, h, s, hd = x.shape
            inv_freq = 1.0 / ROPE_THETA ** (jnp.arange(0, hd, 2, dtype=jnp.float32) / hd)
            pos = jnp.arange(start_pos, start_pos + s, dtype=jnp.float32)
            ang = pos[:, None] * inv_freq[None, :]
            cos = jnp.cos(ang).astype(x.dtype)
            sin = jnp.sin(ang).astype(x.dtype)
            xr = x[..., 0::2]
            xi = x[..., 1::2]
            out_r = xr * cos - xi * sin
            out_i = xr * sin + xi * cos
            return jnp.stack([out_r, out_i], axis=-1).reshape(b, h, s, hd)
        bs, seq_len, d_model = x.shape
        qkv = x @ w_qkv.T + b_qkv
        q_dim = NUM_HEADS * HEAD_DIM
        kv_dim = NUM_KV_HEADS * HEAD_DIM
        q, k, v = jnp.split(qkv, [q_dim, q_dim + kv_dim], axis=-1)
        q = q.reshape(bs, seq_len, NUM_HEADS, HEAD_DIM).transpose(0, 2, 1, 3)
        k = k.reshape(bs, seq_len, NUM_KV_HEADS, HEAD_DIM).transpose(0, 2, 1, 3)
        v = v.reshape(bs, seq_len, NUM_KV_HEADS, HEAD_DIM).transpose(0, 2, 1, 3)
        q = apply_rope(q, 0)
        k = apply_rope(k, 0)
        k = jnp.repeat(k, GROUP, axis=1)
        v = jnp.repeat(v, GROUP, axis=1)
        scores = jnp.einsum('bhqd,bhkd->bhqk', q, k) / math.sqrt(HEAD_DIM)
        causal = jnp.tril(jnp.ones((seq_len, seq_len), dtype=bool))
        scores = jnp.where(causal[None, None, :, :], scores, jnp.float32(-1e+20))
        attn = jax.nn.softmax(scores, axis=-1)
        out = jnp.einsum('bhqk,bhkd->bhqd', attn, v)
        out = out.transpose(0, 2, 1, 3).reshape(bs, seq_len, d_model)
        return out @ w_o.T + b_o

    def _L0_attn_b_ref(x, norm_w, in_proj_w, conv_w, conv_b, dt_bias, A_log, Dp, gnorm_w, out_proj_w):
        import jax, jax.numpy as jnp
        import numpy as np
        H_M, P_M, G_M, N_M, K_CONV, CHUNK = (128, 64, 8, 128, 4, 128)
        D_MODEL = 512
        D_INNER = H_M * P_M
        CONV_DIM = D_INNER + 2 * G_M * N_M
        PROJ_DIM = D_INNER + CONV_DIM + H_M
        EPS = 1e-05

        def segsum(x):
            l = x.shape[-1]
            xe = jnp.broadcast_to(x[..., None], x.shape + (l,))
            m1 = jnp.tril(jnp.ones((l, l), dtype=bool), -1)
            s = jnp.cumsum(jnp.where(m1, xe, 0.0), axis=-2)
            m2 = jnp.tril(jnp.ones((l, l), dtype=bool), 0)
            return jnp.where(m2, s, -jnp.inf)

        def causal_conv(x, w, bconv):
            k = w.shape[1]
            s = x.shape[1]
            xp = jnp.pad(x, ((0, 0), (k - 1, 0), (0, 0)))
            y = sum((xp[:, i:i + s, :] * w[:, i] for i in range(k)))
            return y + bconv
        b, s, _ = x.shape
        residual = x
        h = x * jax.lax.rsqrt(jnp.mean(x * x, axis=-1, keepdims=True) + EPS) * norm_w
        proj = jnp.einsum('bsd,od->bso', h, in_proj_w)
        gate = proj[..., :D_INNER]
        hBC = proj[..., D_INNER:D_INNER + CONV_DIM]
        dt = proj[..., D_INNER + CONV_DIM:]
        hBC = jax.nn.silu(causal_conv(hBC, conv_w, conv_b))
        hid = hBC[..., :D_INNER].reshape(b, s, H_M, P_M)
        B = hBC[..., D_INNER:D_INNER + G_M * N_M].reshape(b, s, G_M, N_M)
        C = hBC[..., D_INNER + G_M * N_M:].reshape(b, s, G_M, N_M)
        dt = jax.nn.softplus(dt + dt_bias)
        A = -jnp.exp(A_log)
        pad = -s % CHUNK
        D_res = Dp[None, None, :, None] * hid
        hid_dt = hid * dt[..., None]
        A_full = A[None, None, :] * dt

        def padseq(t):
            return jnp.pad(t, [(0, 0), (0, pad)] + [(0, 0)] * (t.ndim - 2))
        hid_dt, A_full, Bp, Cp = (padseq(hid_dt), padseq(A_full), padseq(B), padseq(C))
        S = s + pad
        c, l = (S // CHUNK, CHUNK)
        hc = hid_dt.reshape(b, c, l, H_M, P_M)
        Ac = A_full.reshape(b, c, l, H_M).transpose(0, 3, 1, 2)
        rep = H_M // G_M
        Bh = jnp.repeat(Bp.reshape(b, c, l, G_M, N_M), rep, axis=3)
        Ch = jnp.repeat(Cp.reshape(b, c, l, G_M, N_M), rep, axis=3)
        A_cs = jnp.cumsum(Ac, axis=-1)
        L = jnp.exp(segsum(Ac))
        M = jnp.einsum('bcihn,bcjhn->bcijh', Ch, Bh) * jnp.transpose(L, (0, 2, 3, 4, 1))
        Y_diag = jnp.einsum('bcijh,bcjhp->bcihp', M, hc)
        decay_states = jnp.exp(A_cs[..., -1:] - A_cs)
        states = jnp.einsum('bclhn,bhcl,bclhp->bchpn', Bh, decay_states, hc)
        A_last = jnp.pad(A_cs[..., -1], ((0, 0), (0, 0), (1, 0)))
        decay_chunk = jnp.exp(segsum(A_last))
        states_cat = jnp.concatenate([jnp.zeros_like(states[:, :1]), states], axis=1)
        prev_states = jnp.einsum('bhij,bjhpn->bihpn', decay_chunk, states_cat)[:, :-1]
        Y_off = jnp.einsum('bclhn,bchpn,bhcl->bclhp', Ch, prev_states, jnp.exp(A_cs))
        y = (Y_diag + Y_off).reshape(b, S, H_M, P_M)[:, :s] + D_res
        y = y.reshape(b, s, D_INNER)
        yg = y * jax.nn.silu(gate)
        gsz = D_INNER // G_M
        ygr = yg.reshape(b, s, G_M, gsz)
        ygr = ygr * jax.lax.rsqrt(jnp.mean(ygr * ygr, axis=-1, keepdims=True) + EPS)
        y = ygr.reshape(b, s, D_INNER) * gnorm_w
        out = jnp.einsum('bsd,od->bso', y, out_proj_w)
        return residual + out

    def _L0_ffn_ref(x, W_gate, W_up, W_down):
        import jax, jax.numpy as jnp
        import numpy as np
        D_MODEL = 512
        D_FF = 1376
        out_shape = x.shape[:-1] + (W_down.shape[0],)
        xf = x.reshape(-1, x.shape[-1])
        up = jnp.einsum('td,fd->tf', xf, W_up)
        gate = jax.nn.silu(jnp.einsum('td,fd->tf', xf, W_gate))
        h = gate * up
        y = jnp.einsum('tf,df->td', h, W_down)
        return y.reshape(out_shape)

    def _L1_attn_a_ref(x):
        import jax, jax.numpy as jnp
        import numpy as np
        B, C, L = (64, 64, 512)
        b, c, l = x.shape
        q = jnp.transpose(x, (2, 0, 1))
        scale = jnp.asarray(c, x.dtype) ** 0.5
        scores = jnp.einsum('lnc,lmc->lnm', q, q) / scale
        prob = jax.nn.softmax(scores, axis=-1)
        msg = jnp.einsum('lnm,lmc->lnc', prob, q)
        return x + jnp.transpose(msg, (1, 2, 0))

    def _L1_attn_b_ref(hidden_states, Wq, Wk, Wv, Wo):
        import jax, jax.numpy as jnp
        import numpy as np
        HIDDEN = 512
        N_HEADS = 32
        HEAD_DIM = HIDDEN // N_HEADS
        BATCH = 2
        SEQ = 256
        ROPE_BASE = 10000.0

        def _rope_cos_sin(seq_len, head_dim, dtype):
            inv_freq = 1.0 / ROPE_BASE ** (jnp.arange(0, head_dim, 2, dtype=jnp.float32) / head_dim)
            t = jnp.arange(seq_len, dtype=jnp.float32)
            freqs = t[:, None] * inv_freq[None, :]
            emb = jnp.concatenate([freqs, freqs], axis=-1)
            return (jnp.cos(emb).astype(dtype), jnp.sin(emb).astype(dtype))

        def _rotate_half(x):
            d = x.shape[-1] // 2
            return jnp.concatenate([-x[..., d:], x[..., :d]], axis=-1)
        b, s, _ = hidden_states.shape
        q = hidden_states @ Wq.T
        k = hidden_states @ Wk.T
        v = hidden_states @ Wv.T
        q = q.reshape(b, s, N_HEADS, HEAD_DIM).transpose(0, 2, 1, 3)
        k = k.reshape(b, s, N_HEADS, HEAD_DIM).transpose(0, 2, 1, 3)
        v = v.reshape(b, s, N_HEADS, HEAD_DIM).transpose(0, 2, 1, 3)
        cos, sin = _rope_cos_sin(s, HEAD_DIM, hidden_states.dtype)
        cos = cos[None, None]
        sin = sin[None, None]
        q = q * cos + _rotate_half(q) * sin
        k = k * cos + _rotate_half(k) * sin
        scores = jnp.einsum('bhqd,bhkd->bhqk', q, k) / np.sqrt(HEAD_DIM).astype(np.float32)
        attn = jax.nn.softmax(scores, axis=-1)
        out = jnp.einsum('bhqk,bhkd->bhqd', attn, v)
        out = out.transpose(0, 2, 1, 3).reshape(b, s, HIDDEN)
        return out @ Wo.T

    def _L1_ffn_ref(x, gate_q, gate_scale, gate_A, gate_B, up_q, up_scale, up_A, up_B, down_q, down_scale, down_A, down_B):
        import jax, jax.numpy as jnp
        import numpy as np
        H = 512
        I = 1376
        R = 32
        NLEV = 16
        Q_ZERO = 7.5
        Q_STEP = 0.005
        LR_SCALE = 0.02

        def _qlinear(x, q, scale, A, Bm):
            w = (q.astype(jnp.float32) - Q_ZERO) * (scale * Q_STEP)[:, None]
            y = jnp.einsum('bsh,oh->bso', x, w)
            return y + LR_SCALE * (x @ A @ Bm)
        g = _qlinear(x, gate_q, gate_scale, gate_A, gate_B)
        u = _qlinear(x, up_q, up_scale, up_A, up_B)
        h = jax.nn.silu(g) * u
        return _qlinear(h, down_q, down_scale, down_A, down_B)
    x = L0_attn_a_x
    x = x + _L0_attn_a_ref(_layernorm(x, axis=-1), L0_attn_a_w_qkv, L0_attn_a_b_qkv, L0_attn_a_w_o, L0_attn_a_b_o)
    x = x + _L0_ffn_ref(_layernorm(x, axis=-1), L0_ffn_W_gate, L0_ffn_W_up, L0_ffn_W_down)
    x = x + _L0_attn_b_ref(_layernorm(x, axis=-1), L0_attn_b_norm_w, L0_attn_b_in_proj_w, L0_attn_b_conv_w, L0_attn_b_conv_b, L0_attn_b_dt_bias, L0_attn_b_A_log, L0_attn_b_Dp, L0_attn_b_gnorm_w, L0_attn_b_out_proj_w)
    x = x + _L0_ffn_ref(_layernorm(x, axis=-1), L0_ffn_W_gate, L0_ffn_W_up, L0_ffn_W_down)
    x = x + _L1_attn_a_ref(_layernorm(x, axis=-1))
    x = x + _L1_ffn_ref(_layernorm(x, axis=-1), L1_ffn_gate_q, L1_ffn_gate_scale, L1_ffn_gate_A, L1_ffn_gate_B, L1_ffn_up_q, L1_ffn_up_scale, L1_ffn_up_A, L1_ffn_up_B, L1_ffn_down_q, L1_ffn_down_scale, L1_ffn_down_A, L1_ffn_down_B)
    x = x + _L1_attn_b_ref(_layernorm(x, axis=-1), L1_attn_b_Wq, L1_attn_b_Wk, L1_attn_b_Wv, L1_attn_b_Wo)
    x = x + _L1_ffn_ref(_layernorm(x, axis=-1), L1_ffn_gate_q, L1_ffn_gate_scale, L1_ffn_gate_A, L1_ffn_gate_B, L1_ffn_up_q, L1_ffn_up_scale, L1_ffn_up_A, L1_ffn_up_B, L1_ffn_down_q, L1_ffn_down_scale, L1_ffn_down_A, L1_ffn_down_B)
    return x

_drawn_inputs = setup_inputs


def setup_inputs(seed=0):
    import zlib

    import numpy as np

    out = dict(_drawn_inputs(seed))
    spreads = {'L0_attn_b_norm_w': (1.0, 0.2),
     'L0_attn_b_conv_b': (0.0, 0.1),
     'L0_attn_b_Dp': (1.0, 0.2),
     'L0_attn_b_gnorm_w': (1.0, 0.2)}
    factors = {'L0_attn_a_b_o': 2.706,
     'L0_attn_b_dt_bias': 8.0,
     'L0_attn_b_A_log': 5.27,
     'L1_attn_b_Wq': 6.44,
     'L1_attn_b_Wk': 6.438,
     'L1_attn_b_Wv': 5.52,
     'L1_attn_b_Wo': 5.31}
    for name, (base, spread) in spreads.items():
        noise = np.random.default_rng([zlib.crc32(name.encode()), seed]).standard_normal(out[name].shape)
        drawn = base * np.exp(spread * noise) if base else spread * noise
        out[name] = jnp.asarray(drawn.astype(out[name].dtype))
    for name, factor in factors.items():
        out[name] = (out[name] * factor).astype(out[name].dtype)
    return out
```

```python
from contextlib import ExitStack

import numpy as np

import concourse.bass as bass
from concourse import mybir

F32 = mybir.dt.float32
BF16 = mybir.dt.bfloat16
I32 = mybir.dt.int32
ALU = mybir.AluOpType
ACT = mybir.ActivationFunctionType
AX = mybir.AxisListType

P = 128
BATCH, SEQ, D = 4, 256, 512
TOK = BATCH * SEQ
NT = TOK // P
KD = D // P
BT = SEQ // P
HALF = 512
EPS = 1e-5

HEADS, KV_HEADS, HD = 32, 8, 16
HPT = P // HD
F_FF = 1376
FT = -(-F_FF // P)
F_PAD = FT * P
RANK = 32
Q_ZERO, Q_STEP, LR_SCALE = 7.5, 0.005, 0.02

MH, MP, MG, MN, TAPS = 128, 64, 8, 128, 4
D_INNER = MH * MP
GF = D_INNER // MG
GM = GF // P
GH = MH // MG
STEPS = 2 * GM
NCOL = (GM + 2) * (TAPS + 1) + 2 * GM
MASKED = -1e20

C_ID, C_HM, C_COS, C_SIN, C_TRI = 0, P, P + HPT, P + HPT + BT * HD, P + HPT + 2 * BT * HD
NCONST = C_TRI + P


class Core:

    def __init__(self, nc, ctx):
        self.nc = nc
        sb = lambda name, shape, dt=F32: ctx.enter_context(nc.sbuf_tensor(name, shape, dt))
        self.x = sb("x_res", [P, NT, D])
        self.xT = sb("xT", [P, KD, TOK])
        self.consts = sb("consts", [P, NCONST])
        self.identb = sb("identb", [P, P], BF16)
        self.tri4 = sb("tri4", [P, 4, P], BF16)
        self.tri_right = sb("tri_right", [P, 2, 2, P], BF16)
        self.ident = self.consts[:, C_ID:C_ID + P]
        sem = lambda name: ctx.enter_context(nc.semaphore(name))
        self.ln = {n: sem("ln_" + n) for n in ("stats", "chain", "var", "std", "xn", "turned", "evac", "added")}
        self.ln_runs = 0
        self.ln_links = 0
        self.ln_std = 0


def phase_semaphores(nc, ctx, prefix):
    taken = []

    def clear():
        nc.clear_and_free_semaphores(taken)
        nc.all_engine_barrier(sem_only=True)

    ctx.callback(clear)

    def sem(name):
        taken.append(nc.alloc_semaphore(prefix + name))
        return taken[-1]

    return sem


def load_phase(nc, core, x_dram, const_dram):
    with ExitStack() as ctx:
        loaded, cst, made = (ctx.enter_context(nc.semaphore(n)) for n in ("in_loaded", "const_loaded", "const_made"))
        block = ctx.enter_context(nc.Block())

        @block.sync
        def _(sp):
            sp.dma_start(core.consts[:], const_dram).then_inc(cst, 16)
            sp.dma_start(core.x[:], x_dram.rearrange("(t p) d -> p t d", p=P)).then_inc(loaded, 16)
            sp.wait_ge(loaded, 16)

        @block.vector
        def _(dve):
            dve.wait_ge(cst, 16)
            dve.tensor_copy(core.identb[:], core.ident)
            tri = core.consts[:, C_TRI:C_TRI + P]
            dve.tensor_copy(core.tri4[:], tri.unsqueeze(1).broadcast_to((P, 4, P)))
            dve.memset(core.tri_right[:], 0.0).then_inc(made, 1)
            dve.wait_ge(made, 1)
            for h in range(2):
                dve.tensor_copy(core.tri_right[:, h, 1, :], tri)


def store_phase(nc, core, out_dram):
    with ExitStack() as ctx:
        stored = ctx.enter_context(nc.semaphore("stored"))
        block = ctx.enter_context(nc.Block())

        @block.sync
        def _(sp):
            sp.dma_start(out_dram.rearrange("(t p) d -> p t d", p=P), core.x[:]).then_inc(stored, 16)
            sp.wait_ge(stored, 16)


def norm_phase(nc, core, name, add=False, rms_col=None):
    run, s = core.ln_runs, core.ln
    core.ln_runs += 1
    links = [core.ln_links]
    with ExitStack() as ctx:
        sb = lambda n, shape, dt=F32: ctx.enter_context(nc.sbuf_tensor(name + n, shape, dt))
        st = sb("st", [P, NT, 6])
        v = sb("v", [P, 10, NT])
        xn = sb("xn", [P, NT, D])
        hn = sb("hn", [P, NT, D]) if rms_col is not None else xn
        wcol = sb("wcol", [P, KD]) if rms_col is not None else None
        ps = ctx.enter_context(nc.psum_tensor(name + "ps", [P, 2, KD, HALF], F32))
        wsem = ctx.enter_context(nc.semaphore(name + "w")) if rms_col is not None else None
        block = ctx.enter_context(nc.Block())
        MEAN2, DIFF, VSUM, DSQ, VAR, MEAN, STD, RSTD, MS, RMS = (v[:, i, :] for i in range(10))
        n_std = 2 if rms_col is not None else 1

        def evac(eng, half, f):
            out = core.xT[:, f, half * HALF:(half + 1) * HALF]
            src = ps[:, half, f, :]
            if eng is nc.scalar:
                if wcol is None:
                    eng.activation(out, src, ACT.Copy)
                else:
                    eng.activation(out, src, ACT.Copy, scale=wcol[:, f:f + 1])
            elif wcol is None:
                eng.tensor_copy(out, src)
            else:
                eng.tensor_scalar(out, src, wcol[:, f:f + 1], None, ALU.mult)

        @block.sync
        def _(sp):
            if wcol is not None:
                sp.dma_start(wcol[:], rms_col).then_inc(wsem, 16)

        @block.vector
        def _(dve):
            def link(ins):
                links[0] += 1
                ins.then_inc(s["chain"], 1)
                dve.wait_ge(s["chain"], links[0])

            with dve.Fori(0, NT) as t:
                dve.bn_stats(st[:, t, :], core.x[:, t, :]).then_inc(s["stats"], 1)
            dve.wait_ge(s["stats"], NT * (run + 1))
            dve.tensor_tensor(DIFF, st[:, :, 1], st[:, :, 4], ALU.subtract)
            dve.tensor_tensor(VSUM, st[:, :, 2], st[:, :, 5], ALU.add)
            link(dve.tensor_tensor(MEAN2, st[:, :, 1], st[:, :, 4], ALU.add))
            dve.tensor_scalar(MEAN, MEAN2, 0.5, None, ALU.mult)
            link(dve.scalar_tensor_tensor(out=DSQ, in0=DIFF, scalar=0.25, in1=DIFF, op0=ALU.mult, op1=ALU.mult))
            link(dve.scalar_tensor_tensor(out=VAR, in0=VSUM, scalar=1.0 / D, in1=DSQ, op0=ALU.mult, op1=ALU.add))
            dve.tensor_scalar(DSQ, VAR, EPS, None, ALU.add).then_inc(s["var"], 1)
            dve.wait_ge(s["std"], core.ln_std + 1)
            link(dve.reciprocal(RSTD, STD))
            if n_std == 2:
                link(dve.tensor_tensor(MS, RSTD, RSTD, ALU.mult))
                link(dve.tensor_tensor(MS, MS, VAR, ALU.mult))
                dve.tensor_scalar(DSQ, MS, EPS, None, ALU.add).then_inc(s["var"], 1)
                dve.wait_ge(s["std"], core.ln_std + 2)
                link(dve.reciprocal(RMS, STD))
            for t in range(NT):
                ins = dve.tensor_scalar(xn[:, t, :], core.x[:, t, :], MEAN[:, t:t + 1], RSTD[:, t:t + 1],
                                        ALU.subtract, ALU.mult)
                if n_std == 2:
                    link(ins)
                    ins = dve.tensor_scalar(hn[:, t, :], xn[:, t, :], RMS[:, t:t + 1], None, ALU.mult)
                ins.then_inc(s["xn"], 1)
            if wcol is not None:
                dve.wait_ge(wsem, 16)
            for half in range(2):
                dve.wait_ge(s["turned"], NT * run + 4 * (half + 1))
                for f in (0, 1):
                    evac(nc.vector, half, f)

        @block.gpsimd
        def _(pool):
            if add:
                for t in range(NT):
                    pool.wait_ge(s["xn"], NT * run + t + 1)
                    pool.tensor_tensor(core.x[:, t, :], core.x[:, t, :], xn[:, t, :], ALU.add)

        @block.scalar
        def _(act):
            for i in range(n_std):
                act.wait_ge(s["var"], core.ln_std + i + 1)
                act.activation(STD, DSQ, ACT.Sqrt).then_inc(s["std"], 1)
            if wcol is not None:
                act.wait_ge(wsem, 16)
            for half in range(2):
                act.wait_ge(s["turned"], NT * run + 4 * (half + 1))
                for f in (2, 3):
                    evac(nc.scalar, half, f)

        @block.tensor
        def _(pe):
            for t in range(NT):
                pe.wait_ge(s["xn"], NT * run + t + 1)
                for f in range(KD):
                    ins = pe.transpose(ps[:, t // 4, f, (t % 4) * P:(t % 4 + 1) * P],
                                       hn[:, t, f * P:(f + 1) * P], core.ident)
                ins.then_inc(s["turned"], 1)
    core.ln_links = links[0]
    core.ln_std += n_std


def ffn_phase(nc, core, name, w_gu, w_down, quant=None):
    wdt = I32 if quant else F32
    LAST = 2 * FT
    with ExitStack() as ctx:
        sb = lambda n, shape, dt=F32: ctx.enter_context(nc.sbuf_tensor(name + n, shape, dt))
        pb = lambda n, shape: ctx.enter_context(nc.psum_tensor(name + n, shape, F32))
        sem = phase_semaphores(nc, ctx, name)
        wgu_raw = sb("wgu_raw", [P, 2, 2, KD, P], wdt)
        wd_raw = sb("wd_raw", [P, 2, D], wdt)
        wgu = sb("wgu", [P, 2, 2, KD, P]) if quant else wgu_raw
        wd = sb("wd", [P, 2, D]) if quant else wd_raw
        sil = sb("sil", [P, 2, HALF])
        hT = sb("hT", [P, 2, HALF])
        ps_gu = pb("psgu", [P, 2, HALF])
        acc = pb("acc", [P, 4, D])
        gu_loaded = [sem(f"gu_loaded{i}") for i in range(2)]
        d_loaded = [sem(f"d_loaded{i}") for i in range(2)]
        gate_ready, up_ready, silu_done, h_ready, down_done, acc_ready, acc_added = (
            sem(n) for n in ("gate_ready", "up_ready", "silu_done", "h_ready", "down_done", "acc_ready", "acc_added"))
        if quant:
            ps_l = pb("psl", [P, HALF])
            low_in = sb("low_in", [P, 2, KD, RANK])
            low_da = sb("low_da", [P, FT, RANK])
            low_b = sb("low_b", [RANK, 2, F_PAD])
            low_db = sb("low_db", [RANK, D])
            scale_gu = sb("scale_gu", [P, 2, F_PAD])
            scale_d = sb("scale_d", [P, D])
            b_slot = sb("b_slot", [RANK, 2, 2, P])
            da_slot = sb("da_slot", [P, 2, RANK])
            lowx = sb("lowx", [RANK, 2, TOK])
            lowh = sb("lowh", [RANK, HALF])
            (small_loaded, scaled, gu_deq, d_deq, b_copied, lowx_ready, lowx_kept, lowh_ready, lowh_kept) = (
                sem(n) for n in ("small_loaded", "scaled", "gu_deq", "d_deq", "b_copied", "lowx_ready", "lowx_kept",
                                 "lowh_ready", "lowh_kept"))
        block = ctx.enter_context(nc.Block())

        def steps(eng, half, body):
            for f in range(2):
                body(f, FT * half + f, (half + f) % 2)
            with eng.Fori(0, (FT - 2) // 2) as i:
                for j in range(2):
                    body(2 + 2 * i + j, FT * half + 2 + 2 * i + j, (half + j) % 2)
            for f in range(FT - FT % 2, FT):
                body(f, FT * half + f, (half + f) % 2)

        def landed(step, slot):
            return 8 * (step - slot) + 16

        @block.sync
        def _(sp):
            if quant:
                for dst, src in ((low_in, quant["a"]), (low_da, quant["da"]), (low_b, quant["b"]),
                                 (low_db, quant["db"])):
                    sp.dma_start(dst[:], src).then_inc(small_loaded, 16)
                sp.dma_start(scale_gu[:], quant["s_gu"].partition_broadcast(P)).then_inc(small_loaded, 16)
                sp.dma_start(scale_d[:], quant["s_d"].partition_broadcast(P)).then_inc(small_loaded, 16)
            for half in range(2):
                def load(f, step, slot):
                    if not (isinstance(step, int) and step < 2):
                        sp.wait_ge(gu_deq if quant else up_ready, step - 1)
                    sp.dma_start(wgu_raw[:, slot], w_gu[f]).then_inc(gu_loaded[slot], 16)
                    if not (isinstance(step, int) and step < 2):
                        sp.wait_ge(d_deq if quant else down_done, step - 1)
                    sp.dma_start(wd_raw[:, slot], w_down[f]).then_inc(d_loaded[slot], 16)
                steps(sp, half, load)

        @block.tensor
        def _(pe):
            if quant:
                pe.wait_ge(small_loaded, 16 * 6)
                for n in range(4):
                    half, w = n // 2, n % 2
                    if n:
                        pe.wait_ge(lowx_kept, n)
                    for k in range(KD):
                        ins = pe.matmul(ps_l[0:RANK, :], low_in[:, w, k, :],
                                        core.xT[:, k, half * HALF:(half + 1) * HALF], start=k == 0, stop=k == KD - 1)
                    ins.then_inc(lowx_ready, 1)
                pe.wait_ge(lowx_kept, 4)
            for half in range(2):
                tok = slice(half * HALF, (half + 1) * HALF)

                def gate_up(step, slot):
                    if quant:
                        pe.wait_ge(gu_deq, step + 1)
                        pe.wait_ge(b_copied, step + 1)
                    else:
                        pe.wait_ge(gu_loaded[slot], landed(step, slot))
                    for w, ready, used in ((0, gate_ready, silu_done), (1, up_ready, h_ready)):
                        if not (isinstance(step, int) and step == 0):
                            pe.wait_ge(used, step)
                        for k in range(KD):
                            ins = pe.matmul(ps_gu[:, w, :], wgu[:, slot, w, k, :], core.xT[:, k, tok],
                                            start=k == 0, stop=k == KD - 1 and not quant)
                        if quant:
                            ins = pe.matmul(ps_gu[:, w, :], b_slot[:, slot, w, :], lowx[:, w, tok],
                                            start=False, stop=True)
                        ins.then_inc(ready, 1)

                def down(step, slot, first, last):
                    pe.wait_ge(h_ready, step + 1)
                    if quant:
                        pe.wait_ge(d_deq, step + 1)
                    else:
                        pe.wait_ge(d_loaded[slot], landed(step, slot))
                    if first and half:
                        pe.wait_ge(acc_added, 4)
                    for t in range(4):
                        ins = pe.matmul(acc[:, t, :], hT[:, slot, t * P:(t + 1) * P], wd[:, slot, :],
                                        start=first, stop=last and not quant, skip_group_check=True)
                    if quant:
                        ins = pe.matmul(ps_l[0:RANK, :], da_slot[:, slot, :], hT[:, slot, :],
                                        start=first, stop=last, skip_group_check=True)
                    ins.then_inc(down_done, 1)
                    if last and quant:
                        pe.wait_ge(lowh_kept, half + 1)
                        for t in range(4):
                            ins = pe.matmul(acc[:, t, :], lowh[:, t * P:(t + 1) * P], low_db[:],
                                            start=False, stop=True, skip_group_check=True)
                        ins.then_inc(acc_ready, 1)

                def both(f, step, slot):
                    gate_up(step, slot)
                    if not (isinstance(f, int) and f == 0):
                        down(step - 1, 1 - slot, isinstance(f, int) and f == 1, False)

                steps(pe, half, both)
                down(FT * (half + 1) - 1, (FT * (half + 1) - 1) % 2, False, True)

        @block.scalar
        def _(act):
            if quant:
                for n in range(4):
                    half, w = n // 2, n % 2
                    act.wait_ge(lowx_ready, n + 1)
                    act.activation(lowx[:, w, half * HALF:(half + 1) * HALF], ps_l[0:RANK, :], ACT.Copy,
                                   scale=LR_SCALE).then_inc(lowx_kept, 1)
            for half in range(2):
                def silu(f, step, slot):
                    if quant:
                        act.activation(b_slot[:, slot, :, :], low_b[:, :, bass.ts(f, P)],
                                       ACT.Copy).then_inc(b_copied, 1)
                    act.wait_ge(gate_ready, step + 1)
                    if not (isinstance(step, int) and step < 2):
                        act.wait_ge(h_ready, step - 1)
                    act.activation(sil[:, slot, :], ps_gu[:, 0, :], ACT.Silu).then_inc(silu_done, 1)
                steps(act, half, silu)
                if quant:
                    act.wait_ge(down_done, FT * (half + 1))
                    act.activation(lowh[:], ps_l[0:RANK, :], ACT.Copy, scale=LR_SCALE).then_inc(lowh_kept, 1)

        @block.vector
        def _(dve):
            def product(step, slot):
                dve.wait_ge(silu_done, step + 1)
                dve.wait_ge(up_ready, step + 1)
                if not (isinstance(step, int) and step < 2):
                    dve.wait_ge(down_done, step - 1)
                dve.tensor_tensor(hT[:, slot, :], ps_gu[:, 1, :], sil[:, slot, :], ALU.mult).then_inc(h_ready, 1)

            def add_to_residual(half):
                if quant:
                    dve.wait_ge(acc_ready, half + 1)
                else:
                    dve.wait_ge(down_done, FT * (half + 1))
                for t in range(4):
                    xt = core.x[:, 4 * half + t, :]
                    dve.tensor_tensor(xt, acc[:, t, :], xt, ALU.add).then_inc(acc_added, 1)

            if not quant:
                for half in range(2):
                    steps(dve, half, lambda f, step, slot: product(step, slot))
                    add_to_residual(half)
                return

            dve.wait_ge(small_loaded, 16 * 6)
            dve.tensor_scalar(scale_gu[:], scale_gu[:], Q_STEP, None, ALU.mult).then_inc(scaled, 1)
            dve.tensor_scalar(scale_d[:], scale_d[:], Q_STEP, None, ALU.mult).then_inc(scaled, 1)
            dve.wait_ge(scaled, 2)

            def dequantise(f, step, slot):
                dve.wait_ge(gu_loaded[slot], landed(step, slot))
                for w in range(2):
                    s = scale_gu[:, w, bass.ts(f, P)].unsqueeze(1).broadcast_to((P, KD, P))
                    ins = dve.scalar_tensor_tensor(out=wgu[:, slot, w], in0=wgu_raw[:, slot, w], scalar=-Q_ZERO,
                                                   in1=s, op0=ALU.add, op1=ALU.mult)
                ins.then_inc(gu_deq, 1)
                if not (isinstance(step, int) and step == 0):
                    product(step - 1, 1 - slot)
                if isinstance(step, int) and step == FT:
                    add_to_residual(0)
                if not (isinstance(step, int) and step < 2):
                    dve.wait_ge(down_done, step - 1)
                dve.wait_ge(d_loaded[slot], landed(step, slot))
                dve.tensor_copy(da_slot[:, slot, :], low_da[:, f, :])
                dve.scalar_tensor_tensor(out=wd[:, slot, :], in0=wd_raw[:, slot, :], scalar=-Q_ZERO, in1=scale_d[:],
                                         op0=ALU.add, op1=ALU.mult).then_inc(d_deq, 1)

            for half in range(2):
                steps(dve, half, dequantise)
            product(LAST - 1, (LAST - 1) % 2)
            add_to_residual(1)


def across_batch_phase(nc, core):
    B2 = BATCH * BATCH
    with ExitStack() as ctx:
        sb = lambda n, shape, dt=F32: ctx.enter_context(nc.sbuf_tensor("ab_" + n, shape, dt))
        sem = phase_semaphores(nc, ctx, "ab_")
        sc = sb("sc", [P, KD, BATCH, BATCH])
        junk = sb("junk", [P, SEQ])
        mx = sb("mx", [P, KD * BATCH])
        ex = sb("ex", [P, KD * BATCH, BATCH])
        sm = sb("sm", [P, KD * BATCH])
        msg = sb("msg", [P, KD, TOK])
        ps = ctx.enter_context(nc.psum_tensor("ab_ps", [P, NT, D], F32))
        chain, max_done, exp_done, msg_ready, turned = (
            sem(n) for n in ("chain", "max_done", "exp_done", "msg_ready", "turned"))
        block = ctx.enter_context(nc.Block())
        xv = core.xT[:, :, :].rearrange("p k (b s) -> p k b s", b=BATCH)
        mv = msg[:, :, :].rearrange("p k (b s) -> p k b s", b=BATCH)

        @block.vector
        def _(dve):
            n_chain = [0]

            def link(ins):
                n_chain[0] += 1
                ins.then_inc(chain, 1)
                dve.wait_ge(chain, n_chain[0])

            for k in range(KD):
                for n in range(BATCH):
                    for m in range(n, BATCH):
                        ins = dve.tensor_tensor_reduce(junk[:], xv[:, k, n, :], xv[:, k, m, :], 1.0, 0.0, ALU.mult,
                                                       ALU.add, sc[:, k, n, m:m + 1])
                        link(ins)
            for n in range(BATCH):
                for m in range(n):
                    ins = dve.tensor_copy(sc[:, :, n, m], sc[:, :, m, n])
            link(ins)
            rows = sc[:, :, :, :].rearrange("p k n m -> p (k n) m")
            link(dve.tensor_reduce(mx[:], rows, AX.X, ALU.max))
            dve.tensor_tensor(ex[:], rows, mx[:].unsqueeze(2).broadcast_to((P, KD * BATCH, BATCH)),
                              ALU.subtract).then_inc(max_done, 1)
            dve.wait_ge(exp_done, 1)
            link(dve.tensor_reduce(sm[:], ex[:], AX.X, ALU.add))
            link(dve.reciprocal(mx[:], sm[:]))
            link(dve.tensor_tensor(ex[:], ex[:], mx[:].unsqueeze(2).broadcast_to((P, KD * BATCH, BATCH)), ALU.mult))
            for k in range(KD):
                for m in range(BATCH):
                    for n in range(BATCH):
                        ins = dve.scalar_tensor_tensor(
                            out=mv[:, k, n, :], in0=xv[:, k, m, :], scalar=ex[:, k * BATCH + n, m:m + 1],
                            in1=xv[:, k, n, :] if m == 0 else mv[:, k, n, :], op0=ALU.mult, op1=ALU.add)
                    if m < BATCH - 1:
                        link(ins)
                ins.then_inc(msg_ready, 1)
            for t in range(NT):
                dve.wait_ge(turned, (KD - 1) * NT + t + 1)
                xt = core.x[:, t, :]
                dve.tensor_tensor(xt, ps[:, t, :], xt, ALU.add)

        @block.scalar
        def _(act):
            act.wait_ge(max_done, 1)
            act.activation(ex[:], ex[:], ACT.Exp, scale=1.0 / float(SEQ) ** 0.5).then_inc(exp_done, 1)

        @block.tensor
        def _(pe):
            for k in range(KD):
                pe.wait_ge(msg_ready, k + 1)
                for t in range(NT):
                    pe.transpose(ps[:, t, k * P:(k + 1) * P], msg[:, k, t * P:(t + 1) * P],
                                 core.ident).then_inc(turned, 1)


def attention_phase(nc, core, name, w_qkv, w_o, kv_heads, causal, b_qkv=None, b_o=None):
    kv_t = kv_heads * HD // P
    KW, VW = kv_t * P, kv_heads * HD
    QUADS = HPT // 4
    JOBS = KD * QUADS * BT
    jobs = [(c, gq, t) for c in range(KD) for gq in range(QUADS) for t in range(BT)]
    n_small = 2 + (2 if b_qkv is not None else 0)
    with ExitStack() as ctx:
        sb = lambda n, shape, dt=F32: ctx.enter_context(nc.sbuf_tensor(name + n, shape, dt))
        pb = lambda n, shape: ctx.enter_context(nc.psum_tensor(name + n, shape, F32))
        sem = phase_semaphores(nc, ctx, name)
        wq = sb("wq", [P, KD, D + KW + VW])
        wo = sb("wo", [P, KD, D])
        bq = sb("bq", [P, D + KW + VW]) if b_qkv is not None else None
        bo = sb("bo", [P, D]) if b_o is not None else None
        xb = sb("xb", [P, KD, SEQ])
        raw = sb("raw", [P, BT, D + KW])
        cosd = sb("cosd", [P, BT, D + KW])
        roped = sb("roped", [P, BT, D + KW])
        v = sb("v", [P, BT, VW])
        qT = sb("qT", [P, KD, SEQ])
        kT = sb("kT", [P, kv_t, HPT, SEQ])
        nm = sb("nm", [P, 2, 4])
        rows = sb("rows", [P, BT, HEADS])
        rec = sb("rec", [P, BT, HEADS])
        pr = sb("pr", [P, 2, 4, SEQ])
        pT = sb("pT", [P, 2, BT, 4, P])
        o = sb("o", [P, BT, D])
        oT = sb("oT", [P, KD, SEQ])
        ps_s = [pb(f"ps_s{i}", [P, 2, HALF]) for i in range(2)]
        ps_p = pb("ps_p", [P, 2, HALF])
        ps_o = pb("ps_o", [P, BT, D])
        (w_loaded, xb_ready, qkv_ready, raw_ready, v_ready, cosd_ready, rotated, roped_ready, qkT_ready, qT_ready,
         k_dve, k_act, scores_ready, max_ready, probs_ready, pT_ready, pT_kept, pv_done, rec_ready, o_ready, oT_ready,
         oT_kept, out_ready, biased) = (
            sem(n) for n in ("w_loaded", "xb_ready", "qkv_ready", "raw_ready", "v_ready", "cosd_ready", "rotated",
                             "roped_ready", "qkT_ready", "qT_ready", "k_dve", "k_act", "scores_ready", "max_ready",
                             "probs_ready", "pT_ready", "pT_kept", "pv_done", "rec_ready", "o_ready", "oT_ready",
                             "oT_kept", "out_ready", "biased"))
        block = ctx.enter_context(nc.Block())
        ps_qT = ps_o[:, :, :].rearrange("p a (c s) -> p (a c) s", s=SEQ)
        ps_kT = ps_s[0][:, :, :].rearrange("p a (c s) -> p (a c) s", s=SEQ)
        NH = (D + KW) // HD
        k_of_dve = min(kv_t, 2)

        def n_keys(t):
            return t + 1 if causal else BT

        def scores_view(slot, t):
            kw = n_keys(t) * P
            return ps_s[slot][:, :, :].rearrange("p a n -> p (a n)")[:, 0:4 * kw].rearrange("p (h k) -> p h k", k=kw)

        @block.sync
        def _(sp):
            sp.dma_start(wq[:], w_qkv).then_inc(w_loaded, 16)
            sp.dma_start(wo[:], w_o).then_inc(w_loaded, 16)
            if bq is not None:
                sp.dma_start(bq[:], b_qkv.partition_broadcast(P)).then_inc(w_loaded, 16)
                sp.dma_start(bo[:], b_o.partition_broadcast(P)).then_inc(w_loaded, 16)

        @block.tensor
        def _(pe):
            pe.wait_ge(w_loaded, 16 * n_small)
            with pe.Fori(0, BATCH) as b:
                pe.wait_ge(xb_ready, b + 1)
                for t in range(BT):
                    for dst, at, width in ((ps_s[t][:, 0, :], 0, D), (ps_s[t][:, 1, 0:KW], D, KW),
                                           (ps_p[:, t, 0:VW], D + KW, VW)):
                        for k in range(KD):
                            ins = pe.matmul(dst, xb[:, k, t * P:(t + 1) * P], wq[:, k, at:at + width],
                                            start=k == 0, stop=k == KD - 1)
                    ins.then_inc(qkv_ready, 1)
                for t in range(BT):
                    pe.wait_ge(roped_ready, 2 * b + t + 1)
                    if t == 0:
                        pe.wait_ge(raw_ready, 2 * b + 2)
                    for c in range(KD):
                        ins = pe.transpose(ps_qT[:, c, t * P:(t + 1) * P], roped[:, t, c * P:(c + 1) * P], core.ident)
                    for c in range(kv_t):
                        ins = pe.transpose(ps_kT[:, c, t * P:(t + 1) * P],
                                           roped[:, t, D + c * P:D + (c + 1) * P], core.ident)
                    ins.then_inc(qkT_ready, 1)
                pe.wait_ge(qT_ready, b + 1)
                pe.wait_ge(k_dve, b + 1)
                if kv_t > k_of_dve:
                    pe.wait_ge(k_act, b + 1)
                pe.wait_ge(v_ready, 2 * b + 2)

                def scores(n):
                    c, gq, t = jobs[n]
                    kc = c if kv_t > 1 else 0
                    if n >= 2:
                        pe.wait_ge(probs_ready, JOBS * b + (n - 1))
                    view = scores_view(n % 2, t)
                    q = qT[:, c, t * P:(t + 1) * P]
                    per = HALF // (n_keys(t) * P)
                    for h in range(0, 4, per):
                        if causal:
                            mask = core.tri4[:] if t == 0 else core.tri_right[:].rearrange("p a b c -> p a (b c)")
                            pe.matmul(view[:, h:h + per, :], core.identb[:], mask, start=True, stop=False)
                        ins = pe.matmul(view[:, h:h + per, :], q,
                                        kT[:, kc, 4 * gq + h:4 * gq + h + per, 0:n_keys(t) * P],
                                        start=not causal, stop=True)
                    ins.then_inc(scores_ready, 1)

                scores(0)
                scores(1)
                for n in range(JOBS):
                    c, gq, t = jobs[n]
                    pe.wait_ge(probs_ready, JOBS * b + (n + 1))
                    if n:
                        pe.wait_ge(pT_kept, JOBS * b + n)
                    for kt in range(n_keys(t)):
                        for h in range(4):
                            ins = pe.transpose(ps_p[:, kt, h * P:(h + 1) * P],
                                               pr[:, n % 2, h, kt * P:(kt + 1) * P], core.ident)
                    ins.then_inc(pT_ready, 1)
                    if n + 2 < JOBS:
                        scores(n + 2)
                    pe.wait_ge(pT_kept, JOBS * b + (n + 1))
                    for h in range(4):
                        g = 4 * gq + h
                        head = HPT * c + g
                        kv = head if kv_t > 1 else g
                        for kt in range(n_keys(t)):
                            ins = pe.matmul(ps_o[:, t, head * HD:(head + 1) * HD], pT[:, n % 2, kt, h, :],
                                            v[:, kt, kv * HD:(kv + 1) * HD], start=kt == 0, stop=kt == n_keys(t) - 1)
                    ins.then_inc(pv_done, 1)
                for t in range(BT):
                    pe.wait_ge(o_ready, 2 * b + t + 1)
                    for c in range(KD):
                        ins = pe.transpose(ps_kT[:, c, t * P:(t + 1) * P], o[:, t, c * P:(c + 1) * P], core.ident)
                    ins.then_inc(oT_ready, 1)
                pe.wait_ge(oT_kept, b + 1)
                for t in range(BT):
                    for k in range(KD):
                        ins = pe.matmul(ps_s[1][:, t, :], oT[:, k, t * P:(t + 1) * P], wo[:, k, :],
                                        start=k == 0, stop=k == KD - 1)
                    ins.then_inc(out_ready, 1)

        @block.vector
        def _(dve):
            dve.wait_ge(w_loaded, 16 * n_small)
            with dve.Fori(0, BATCH) as b:
                dve.tensor_copy(xb[:], core.xT[:, :, bass.ts(b, SEQ)]).then_inc(xb_ready, 1)
                for t in range(BT):
                    dve.wait_ge(qkv_ready, 2 * b + t + 1)
                    if bq is None:
                        dve.tensor_copy(raw[:, t, 0:D], ps_s[t][:, 0, :])
                        dve.tensor_copy(raw[:, t, D:D + KW], ps_s[t][:, 1, 0:KW]).then_inc(raw_ready, 1)
                        dve.tensor_copy(v[:, t, :], ps_p[:, t, 0:VW]).then_inc(v_ready, 1)
                    else:
                        dve.tensor_tensor(raw[:, t, 0:D], ps_s[t][:, 0, :], bq[:, 0:D], ALU.add)
                        dve.tensor_tensor(raw[:, t, D:D + KW], ps_s[t][:, 1, 0:KW], bq[:, D:D + KW],
                                          ALU.add).then_inc(raw_ready, 1)
                        dve.tensor_tensor(v[:, t, :], ps_p[:, t, 0:VW], bq[:, D + KW:], ALU.add).then_inc(v_ready, 1)
                for t in range(BT):
                    dve.wait_ge(raw_ready, 2 * b + t + 1)
                    r = raw[:, t, :].rearrange("p (h two d) -> p h two d", two=2, d=HD // 2)
                    out = roped[:, t, :].rearrange("p (h two d) -> p h two d", two=2, d=HD // 2)
                    for part in range(2):
                        s0 = C_SIN + t * HD + part * HD // 2
                        sin = core.consts[:, s0:s0 + HD // 2].unsqueeze(1).broadcast_to((P, NH, HD // 2))
                        ins = dve.tensor_tensor(out[:, :, part, :], r[:, :, 1 - part, :], sin, ALU.mult)
                    ins.then_inc(rotated, 1)
                    dve.wait_ge(rotated, 2 * b + t + 1)
                    dve.wait_ge(cosd_ready, 2 * b + t + 1)
                    dve.tensor_tensor(roped[:, t, :], roped[:, t, :], cosd[:, t, :], ALU.add).then_inc(roped_ready, 1)
                dve.wait_ge(qkT_ready, 2 * b + 2)
                for g in range(HPT):
                    ins = dve.tensor_scalar(kT[:, 0:k_of_dve, g, :], ps_kT[:, 0:k_of_dve, :],
                                            core.consts[:, C_HM + g:C_HM + g + 1], None, ALU.mult)
                ins.then_inc(k_dve, 1)

                def maximum(n):
                    t = jobs[n][2]
                    dve.wait_ge(scores_ready, JOBS * b + (n + 1))
                    dve.tensor_reduce(nm[:, n % 2, :], scores_view(n % 2, t), AX.X, ALU.max,
                                      negate=True).then_inc(max_ready, 1)

                maximum(0)
                maximum(1)
                for n in range(JOBS):
                    t = jobs[n][2]
                    dve.wait_ge(pT_ready, JOBS * b + (n + 1))
                    if n >= 2:
                        dve.wait_ge(pv_done, JOBS * b + (n - 1))
                    kt = n_keys(t)
                    dve.tensor_copy(pT[:, n % 2, 0:kt].rearrange("p k h q -> p k (h q)"),
                                    ps_p[:, 0:kt, :]).then_inc(pT_kept, 1)
                    if n + 2 < JOBS:
                        maximum(n + 2)
                dve.wait_ge(probs_ready, JOBS * b + JOBS)
                dve.reciprocal(rec[:], rows[:]).then_inc(rec_ready, 1)
                dve.wait_ge(rec_ready, b + 1)
                dve.wait_ge(pv_done, JOBS * b + JOBS)
                for t in range(BT):
                    dve.tensor_tensor(o[:, t, :].rearrange("p (h d) -> p h d", d=HD),
                                      ps_o[:, t, :].rearrange("p (h d) -> p h d", d=HD),
                                      rec[:, t, :].unsqueeze(2).broadcast_to((P, HEADS, HD)),
                                      ALU.mult).then_inc(o_ready, 1)
                for t in range(BT):
                    dve.wait_ge(out_ready, 2 * b + t + 1)
                    xt = core.x[:, 2 * b + t, :]
                    if bo is not None:
                        if t == 0:
                            dve.wait_ge(biased, b + 1)
                    dve.tensor_tensor(xt, ps_s[1][:, t, :], xt, ALU.add)

        @block.gpsimd
        def _(pool):
            pool.wait_ge(w_loaded, 16 * n_small)
            with pool.Fori(0, BATCH) as b:
                for t in range(BT):
                    pool.wait_ge(raw_ready, 2 * b + t + 1)
                    c0 = C_COS + t * HD
                    cos = core.consts[:, c0:c0 + HD].unsqueeze(1).broadcast_to((P, NH, HD))
                    pool.tensor_tensor(cosd[:, t, :].rearrange("p (h d) -> p h d", d=HD),
                                       raw[:, t, :].rearrange("p (h d) -> p h d", d=HD), cos,
                                       ALU.mult).then_inc(cosd_ready, 1)
                if bo is not None:
                    for t in range(BT):
                        ins = pool.tensor_tensor(core.x[:, 2 * b + t, :], core.x[:, 2 * b + t, :], bo[:], ALU.add)
                    ins.then_inc(biased, 1)

        @block.scalar
        def _(act):
            with act.Fori(0, BATCH) as b:
                act.wait_ge(qkT_ready, 2 * b + 2)
                act.activation(qT[:], ps_qT, ACT.Copy, scale=1.0 / float(HD) ** 0.5).then_inc(qT_ready, 1)
                if kv_t > k_of_dve:
                    for g in range(HPT):
                        ins = act.activation(kT[:, k_of_dve:, g, :], ps_kT[:, k_of_dve:kv_t, :], ACT.Copy,
                                             scale=core.consts[:, C_HM + g:C_HM + g + 1])
                    ins.then_inc(k_act, 1)
                for n in range(JOBS):
                    c, gq, t = jobs[n]
                    act.wait_ge(max_ready, JOBS * b + (n + 1))
                    if n >= 2:
                        act.wait_ge(pT_ready, JOBS * b + (n - 1))
                    for h in range(4):
                        head = HPT * c + 4 * gq + h
                        ins = act.activation(pr[:, n % 2, h, 0:n_keys(t) * P], scores_view(n % 2, t)[:, h, :],
                                             ACT.Exp, bias=nm[:, n % 2, h:h + 1],
                                             accum_out=rows[:, t, head:head + 1])
                    ins.then_inc(probs_ready, 1)
                act.wait_ge(oT_ready, 2 * b + 2)
                act.activation(oT[:], ps_kT, ACT.Copy).then_inc(oT_kept, 1)


def dt_phase(nc, core, mem, dram):
    with ExitStack() as ctx:
        sb = lambda n, shape, dt=F32: ctx.enter_context(nc.sbuf_tensor("dt_" + n, shape, dt))
        sem = phase_semaphores(nc, ctx, "dt_")
        w = sb("w", [P, KD, MH])
        col = sb("col", [P, 3])
        z, e, dtT, dec = (sb(n, [P, TOK]) for n in ("z", "e", "dtT", "dec"))
        ps = ctx.enter_context(nc.psum_tensor("dt_ps", [P, 2, HALF], F32))
        ps_t = ctx.enter_context(nc.psum_tensor("dt_pst", [P, NT, MH], F32))
        loaded, proj, chain, a_exp, minus_abs, log_done, dt_done, decayed, turned = (
            sem(n) for n in ("loaded", "proj", "chain", "a_exp", "minus_abs", "log_done", "dt_done", "decayed",
                             "turned"))
        expd = sem("expd")
        block = ctx.enter_context(nc.Block())

        @block.sync
        def _(sp):
            sp.dma_start(w[:], dram["m_wdt"]).then_inc(loaded, 16)
            sp.dma_start(col[:, 0:1], dram["m_dtb"]).then_inc(loaded, 16)
            sp.dma_start(col[:, 1:2], dram["m_alog"]).then_inc(loaded, 16)
            sp.dma_start(mem.cols[:], dram["m_cols"]).then_inc(loaded, 16)
            sp.wait_ge(loaded, 64)

        @block.tensor
        def _(pe):
            pe.wait_ge(loaded, 64)
            for half in range(2):
                for k in range(KD):
                    ins = pe.matmul(ps[:, half, :], w[:, k, :], core.xT[:, k, half * HALF:(half + 1) * HALF],
                                    start=k == 0, stop=k == KD - 1)
            ins.then_inc(proj, 1)
            pe.wait_ge(dt_done, 1)
            for t in range(NT):
                ins = pe.transpose(ps_t[:, t, :], dtT[:, t * P:(t + 1) * P], core.ident)
            ins.then_inc(turned, 1)

        @block.scalar
        def _(act):
            act.wait_ge(loaded, 64)
            act.activation(col[:, 2:3], col[:, 1:2], ACT.Exp).then_inc(a_exp, 1)
            act.wait_ge(minus_abs, 1)
            act.activation(e[:], e[:], ACT.Exp).then_inc(expd, 1)
            act.wait_ge(expd, 1)
            act.activation(e[:], e[:], ACT.Ln, bias=1.0).then_inc(log_done, 1)
            act.wait_ge(dt_done, 1)
            act.activation(dec[:], dtT[:], ACT.Exp, scale=col[:, 2:3]).then_inc(decayed, 1)

        @block.vector
        def _(dve):
            n_chain = [0]

            def link(ins):
                n_chain[0] += 1
                ins.then_inc(chain, 1)
                dve.wait_ge(chain, n_chain[0])

            dve.wait_ge(a_exp, 1)
            link(dve.tensor_scalar(col[:, 2:3], col[:, 2:3], -1.0, None, ALU.mult))
            dve.wait_ge(proj, 1)
            link(dve.tensor_scalar(z[:], ps[:, :, :].rearrange("p a n -> p (a n)"), col[:, 0:1], None, ALU.add))
            dve.scalar_tensor_tensor(out=e[:], in0=z[:], scalar=-1.0, in1=z[:], op0=ALU.mult,
                                     op1=ALU.min).then_inc(minus_abs, 1)
            dve.wait_ge(log_done, 1)
            dve.scalar_tensor_tensor(out=dtT[:], in0=z[:], scalar=0.0, in1=e[:], op0=ALU.max,
                                     op1=ALU.add).then_inc(dt_done, 1)
            dve.wait_ge(decayed, 1)
            link(dve.memset(dec[:, :].rearrange("p (b s) -> p b s", b=BATCH)[:, :, 0:1], 0.0))
            link(dve.tensor_copy(mem.dec[:, 0, :], dec[:]))
            link(dve.tensor_tensor(dec[:], dec[:], mem.dec[:, 0, :], ALU.subtract))
            link(dve.tensor_copy(mem.dec[:, 1, :], dec[:]))
            link(dve.tensor_tensor(dec[:], dec[:], mem.dec[:, 1, :], ALU.subtract))
            dve.tensor_copy(mem.dec[:, 2, :], dec[:])
            link(dve.memset(mem.start[:], 0.0))
            for b in range(2):
                dve.tensor_copy(mem.start[:, b * SEQ:b * SEQ + P], core.ident)
            dve.memset(mem.ones[:], 1.0)
            dve.wait_ge(turned, 1)
            dve.tensor_copy(mem.dt[:], ps_t[:])


def mix_phase(nc, core, mem, dram):
    with ExitStack() as ctx:
        sb = lambda n, shape, dt=F32: ctx.enter_context(nc.sbuf_tensor("mx_" + n, shape, dt))
        pb = lambda n, shape: ctx.enter_context(nc.psum_tensor("mx_" + n, shape, F32))
        sem = phase_semaphores(nc, ctx, "mx_")
        w = sb("w", [P, 2, 2, KD, P])
        wbc = sb("wbc", [P, 2, KD, P])
        wout = sb("wout", [P, GM, D])
        cols = sb("cols", [P, NCOL])
        sel = sb("sel", [P, GH, P], BF16)
        cacc = sb("cacc", [P, 2, HALF])
        bT, cT = sb("bT", [P, TOK]), sb("cT", [P, TOK])
        G = sb("G", [P, BATCH, SEQ + P])
        hidT = sb("hidT", [P, 2, HALF])
        gateT = sb("gateT", [P, 2, HALF])
        hid = sb("hid", [P, 2, 4, P])
        L = sb("L", [P, 2, 2 * SEQ + 2 * P])
        M = sb("M", [P, 2, 2, 2 * SEQ + 2 * P])
        y2 = sb("y2", [P, HALF])
        yg = sb("yg", [P, 2, HALF])
        yw = sb("yw", [P, GM, TOK])
        sq = sb("sq", [P, 2, HALF])
        sqsum = sb("sqsum", [P, TOK])
        rms = sb("rms", [P, 3, NT])
        ps_hid = [pb(f"ps_hid{i}", [P, HALF]) for i in range(2)]
        ps_gate, ps_turn, ps_y, ps_misc = (pb(n, [P, HALF]) for n in ("ps_gate", "ps_turn", "ps_y", "ps_misc"))
        ps_dec = [pb(f"ps_dec{i}", [P, HALF]) for i in range(2)]
        w_loaded = [sem(f"w_loaded{i}") for i in range(2)]
        AHEAD = {"conv_done": 2, "scanned": 2, "m_ready": 2, "gate_kept": 1, "gate_ready": 3, "values_kept": 1,
                 "y2_done": 2, "yg_done": 2, "yw_done": 2, "sq_added": 2, "out_added": 2, "out_ready": 1,
                 "g_ready": 4, "hidT_ready": 2, "sq_ready": 2}
        plain = ("wbc_loaded wout_loaded cols_ready hid_ready tap_done conv_chain g_kept turned dec_ready "
                 "y_ready sum_ready var_ready std_ready chain").split()
        s = {n: sem(n) for n in [*plain, *AHEAD]}
        block = ctx.enter_context(nc.Block())
        CONVS = STEPS + 4
        T1 = TAPS + 1

        def done(name, count):
            return AHEAD.get(name, 0) + count

        def col(i):
            return cols[:, i:i + 1]

        def column(i):
            return cols[:, bass.ds(i, 1)]

        def group_steps(eng, body):
            for q in range(4):
                body(q // 2, q, q)
            with eng.Fori(1, STEPS // 4 - 1) as i:
                for q in range(4):
                    body(2 * i + q // 2, 4 * i + q, q)
            for q in range(4):
                body(GM - 2 + q // 2, STEPS - 4 + q, q)

        def is_first(step):
            return isinstance(step, int) and step == 0

        def is_last(step):
            return isinstance(step, int) and step == STEPS - 1

        @block.sync
        def _(sp):
            with sp.Fori(0, MG) as g:
                sp.wait_ge(s["g_ready"], done("g_ready", 4 * (g - 1) + 1))
                sp.dma_start(wbc[:], dram["m_wbc"][g]).then_inc(s["wbc_loaded"], 16)
                with sp.Fori(0, GM // 2) as i:
                    for j in range(2):
                        tile = GM * g + 2 * i + j
                        sp.wait_ge(s["gate_ready"], done("gate_ready", 2 * (tile - 1)))
                        sp.dma_start(w[:, j], dram["m_w"][g, 2 * i + j]).then_inc(w_loaded[j], 16)
                sp.wait_ge(s["out_ready"], done("out_ready", NT * g))
                sp.dma_start(wout[:], dram["m_wout"][g]).then_inc(s["wout_loaded"], 16)

        @block.tensor
        def _(pe):
            with pe.Fori(0, MG) as g:
                def project(ps, weights, half):
                    for k in range(KD):
                        ins = pe.matmul(ps[:], weights[:, k, :], core.xT[:, k, half * HALF:(half + 1) * HALF],
                                        start=k == 0, stop=k == KD - 1)
                    return ins

                pe.wait_ge(s["wbc_loaded"], 16 * (g + 1))
                for n in range(4):
                    pe.wait_ge(s["conv_done"], done("conv_done", CONVS * g + n - 1))
                    project(ps_hid[n % 2], wbc[:, n // 2], n % 2).then_inc(s["hid_ready"], 1)

                def values_and_gate(tile, step, q):
                    half, slot = q % 2, q // 2
                    if half == 0:
                        pe.wait_ge(w_loaded[slot], 8 * (GM * g + tile - slot) + 16)
                    pe.wait_ge(s["conv_done"], done("conv_done", CONVS * g + 4 + step - 1))
                    project(ps_hid[half], w[:, slot, 0], half).then_inc(s["hid_ready"], 1)
                    pe.wait_ge(s["gate_kept"], done("gate_kept", STEPS * g + step))
                    project(ps_gate, w[:, slot, 1], half).then_inc(s["gate_ready"], 1)

                def decays(tile, step, q):
                    half = q % 2
                    for hh in range(2):
                        pe.wait_ge(s["scanned"], done("scanned", 2 * (STEPS * g + step - 1) + hh + 1))
                        for part in range(3):
                            ins = pe.matmul(ps_dec[hh][:], sel[:, 2 * tile + hh, :],
                                            mem.dec[:, part, half * HALF:(half + 1) * HALF],
                                            start=part == 0, stop=part == 2)
                        ins.then_inc(s["dec_ready"], 1)

                def turn_values(step, q):
                    half = q % 2
                    pe.wait_ge(s["hidT_ready"], done("hidT_ready", CONVS * g + 4 + step + 1))
                    pe.wait_ge(s["values_kept"], done("values_kept", STEPS * g + step))
                    for t in range(4):
                        ins = pe.transpose(ps_turn[:, t * P:(t + 1) * P], hidT[:, half, t * P:(t + 1) * P],
                                           core.ident)
                    ins.then_inc(s["turned"], 1)

                def sums(step, q):
                    half = q % 2
                    pe.wait_ge(s["m_ready"], done("m_ready", 2 * (STEPS * g + step) + 2))
                    pe.wait_ge(s["values_kept"], done("values_kept", STEPS * g + step + 1))
                    pe.wait_ge(s["y2_done"], done("y2_done", STEPS * g + step))
                    for hh in range(2):
                        rows = slice(hh * MP, (hh + 1) * MP)
                        for b in range(2):
                            pe.matmul(ps_y[rows, b * SEQ:(b + 1) * SEQ], hid[:, half, 2 * b, rows],
                                      M[:, half, hh, b * SEQ:(b + 1) * SEQ], start=True, stop=False)
                            ins = pe.matmul(ps_y[rows, b * SEQ + P:(b + 1) * SEQ], hid[:, half, 2 * b + 1, rows],
                                            M[:, half, hh, 2 * SEQ + b * P:2 * SEQ + (b + 1) * P],
                                            start=False, stop=True)
                    ins.then_inc(s["y_ready"], 1)

                values_and_gate(0, 0, 0)
                pe.wait_ge(s["cols_ready"], g + 1)
                decays(0, 0, 0)
                pe.wait_ge(s["hidT_ready"], done("hidT_ready", CONVS * g + 4))
                pe.wait_ge(s["out_added"], done("out_added", NT * g))
                for b in range(BATCH):
                    if b >= 2:
                        pe.wait_ge(s["g_kept"], BATCH * g + b - 1)
                    ps = (ps_misc, ps_turn)[b % 2]
                    pe.matmul(ps[:, 0:SEQ], bT[:, b * SEQ:b * SEQ + P], cT[:, b * SEQ:(b + 1) * SEQ],
                              start=True, stop=True)
                    pe.matmul(ps[:, SEQ:SEQ + P], bT[:, b * SEQ + P:(b + 1) * SEQ],
                              cT[:, b * SEQ + P:(b + 1) * SEQ], start=True, stop=True).then_inc(s["g_ready"], 1)
                pe.wait_ge(s["g_kept"], BATCH * (g + 1))

                def step_of(tile, step, q):
                    if not is_first(step):
                        sums(step - 1, (q + 3) % 4)
                    turn_values(step, q)
                    if not is_last(step):
                        nxt = (tile if q % 2 == 0 else tile + 1, step + 1, (q + 1) % 4)
                        values_and_gate(*nxt)
                        decays(*nxt)

                group_steps(pe, step_of)
                sums(STEPS - 1, 3)

                pe.wait_ge(s["sq_added"], done("sq_added", STEPS * (g + 1)))
                pe.wait_ge(s["y2_done"], done("y2_done", STEPS * (g + 1)))
                for t in range(NT):
                    ins = pe.matmul(ps_y[:, t:t + 1], sqsum[:, t * P:(t + 1) * P], mem.ones[:], start=True, stop=True)
                ins.then_inc(s["sum_ready"], 1)
                pe.wait_ge(s["wout_loaded"], 16 * (g + 1))
                pe.wait_ge(s["yw_done"], done("yw_done", STEPS * (g + 1)))
                for t in range(NT):
                    pe.wait_ge(s["out_added"], done("out_added", NT * g + t - 1))
                    for m in range(GM):
                        ins = pe.matmul((ps_misc, ps_turn)[t % 2][:], yw[:, m, t * P:(t + 1) * P], wout[:, m, :],
                                        start=m == 0, stop=m == GM - 1)
                    ins.then_inc(s["out_ready"], 1)

        @block.scalar
        def _(act):
            with act.Fori(0, MG) as g:
                act.wait_ge(s["cols_ready"], g + 1)

                def first_tap(tile, unit, half):
                    act.wait_ge(s["hid_ready"], CONVS * g + unit + 1)
                    act.wait_ge(s["hidT_ready"], done("hidT_ready", CONVS * g + unit - 1))
                    act.activation(cacc[:, half, :], ps_hid[half][:], ACT.Identity, scale=col(T1 * tile + TAPS - 1),
                                   bias=col(T1 * tile + TAPS)).then_inc(s["tap_done"], 1)

                def silu_of_conv(out, unit, half):
                    act.wait_ge(s["conv_done"], done("conv_done", CONVS * g + unit + 1))
                    act.activation(out, cacc[:, half, :], ACT.Silu).then_inc(s["hidT_ready"], 1)

                for n in range(4):
                    first_tap(GM + n // 2, n, n % 2)
                    if n:
                        m = n - 1
                        silu_of_conv((bT, cT)[m // 2][:, (m % 2) * HALF:(m % 2 + 1) * HALF], m, m % 2)
                silu_of_conv(cT[:, HALF:], 3, 1)

                def weigh_and_square(tile, step, q):
                    half = q % 2
                    act.wait_ge(s["yg_done"], done("yg_done", STEPS * g + step + 1))
                    act.activation(yw[:, tile, half * HALF:(half + 1) * HALF], yg[:, half, :], ACT.Copy,
                                   scale=col(T1 * (GM + 2) + GM + tile)).then_inc(s["yw_done"], 1)
                    act.wait_ge(s["sq_added"], done("sq_added", STEPS * g + step - 1))
                    act.activation(sq[:, half, :], yg[:, half, :], ACT.Square).then_inc(s["sq_ready"], 1)

                def step_of(tile, step, q):
                    half = q % 2
                    first_tap(tile, 4 + step, half)
                    if is_first(step):
                        for b in range(BATCH):
                            act.wait_ge(s["g_ready"], done("g_ready", BATCH * g + b + 1))
                            act.activation(G[:, b, :], (ps_misc, ps_turn)[b % 2][:, 0:SEQ + P],
                                           ACT.Copy).then_inc(s["g_kept"], 1)
                    act.wait_ge(s["gate_ready"], done("gate_ready", STEPS * g + step + 1))
                    act.wait_ge(s["yg_done"], done("yg_done", STEPS * g + step - 1))
                    act.activation(gateT[:, half, :], ps_gate[:], ACT.Silu).then_inc(s["gate_kept"], 1)
                    silu_of_conv(hidT[:, half, :], 4 + step, half)
                    if not is_first(step):
                        weigh_and_square(tile if q % 2 else tile - 1, step - 1, (q + 3) % 4)

                for step in range(STEPS):
                    step_of(step // 2, step, step % 4)
                weigh_and_square(GM - 1, STEPS - 1, 3)
                act.wait_ge(s["var_ready"], g + 1)
                act.activation(rms[:, 1, :], rms[:, 0, :], ACT.Sqrt).then_inc(s["std_ready"], 1)

        @block.gpsimd
        def _(pool):
            for name, count in AHEAD.items():
                pool.sem_inc(s[name], count)
            with pool.Fori(0, MG) as g:
                pool.wait_ge(s["g_kept"], BATCH * (g + 1))
                pool.wait_ge(s["cols_ready"], g + 1)

                def add_squares(step, q):
                    half = q % 2
                    total = sqsum[:, half * HALF:(half + 1) * HALF]
                    pool.wait_ge(s["sq_ready"], done("sq_ready", STEPS * g + step + 1))
                    pool.wait_ge(s["sq_added"], done("sq_added", STEPS * g + step - 1))
                    pool.tensor_tensor(total, total, sq[:, half, :], ALU.add).then_inc(s["sq_added"], 1)

                def step_of(tile, step, q):
                    half = q % 2
                    for hh in range(2):
                        pool.wait_ge(s["scanned"], done("scanned", 2 * (STEPS * g + step) + hh + 1))
                        for lo, n, g0 in ((0, SEQ, 0), (2 * SEQ, P, SEQ)):
                            ins = pool.tensor_tensor(
                                M[:, half, hh, lo:lo + 2 * n].rearrange("p (b i) -> p b i", b=2),
                                L[:, hh, lo:lo + 2 * n].rearrange("p (b i) -> p b i", b=2),
                                G[:, 2 * half:2 * half + 2, g0:g0 + n], ALU.mult)
                        ins.then_inc(s["m_ready"], 1)
                    if not is_first(step):
                        add_squares(step - 1, (q + 3) % 4)

                group_steps(pool, step_of)
                add_squares(STEPS - 1, 3)

        @block.vector
        def _(dve):
            with dve.Fori(0, MG) as g:
                dve.tensor_copy(cols[:], mem.cols[:, g, :])
                dve.memset(sqsum[:], 0.0)
                dve.tensor_copy(sel[:], core.identb[:, bass.ts(g, GH)].unsqueeze(2).broadcast_to(
                    (P, GH, P))).then_inc(s["cols_ready"], 1)
                dve.wait_ge(s["cols_ready"], g + 1)

                def conv(tile, unit, half):
                    pick = col if isinstance(tile, int) else column
                    acc = cacc[:, half, :].rearrange("p (b s) -> p b s", b=2)
                    src = ps_hid[half][:, :].rearrange("p (b s) -> p b s", b=2)
                    dve.wait_ge(s["tap_done"], CONVS * g + unit + 1)
                    for back in range(1, TAPS):
                        if back > 1:
                            dve.wait_ge(s["conv_chain"], 2 * (CONVS * g + unit) + back - 1)
                        ins = dve.scalar_tensor_tensor(
                            out=acc[:, :, back:], in0=src[:, :, 0:SEQ - back], scalar=pick(T1 * tile + TAPS - 1 - back),
                            in1=acc[:, :, back:], op0=ALU.mult, op1=ALU.add)
                        ins.then_inc(s["conv_chain" if back < TAPS - 1 else "conv_done"], 1)

                for n in range(4):
                    conv(GM + n // 2, n, n % 2)

                def scans(step, q):
                    for hh in range(2):
                        dve.wait_ge(s["dec_ready"], 2 * (STEPS * g + step) + hh + 1)
                        dve.wait_ge(s["m_ready"], done("m_ready", 2 * (STEPS * g + step - 1) + hh + 1))
                        dve.tensor_tensor_scan(L[:, hh, 0:2 * SEQ], ps_dec[hh][:], mem.start[:], 0.0,
                                               ALU.mult, ALU.add)
                        for b in range(2):
                            ins = dve.tensor_tensor_scan(L[:, hh, 2 * SEQ + b * P:2 * SEQ + (b + 1) * P],
                                                         ps_dec[hh][:, b * SEQ + P:(b + 1) * SEQ], core.ident, 0.0,
                                                         ALU.mult, ALU.add)
                        ins.then_inc(s["scanned"], 1)

                def gated(tile, step, q):
                    half = q % 2
                    pick = col if isinstance(tile, int) else column
                    dve.wait_ge(s["y_ready"], STEPS * g + step + 1)
                    dve.wait_ge(s["yg_done"], done("yg_done", STEPS * g + step))
                    dve.scalar_tensor_tensor(out=y2[:], in0=hidT[:, half, :], scalar=pick(T1 * (GM + 2) + tile),
                                             in1=ps_y[:], op0=ALU.mult, op1=ALU.add).then_inc(s["y2_done"], 1)
                    dve.wait_ge(s["y2_done"], done("y2_done", STEPS * g + step + 1))
                    dve.wait_ge(s["gate_kept"], done("gate_kept", STEPS * g + step + 1))
                    dve.wait_ge(s["sq_ready"], done("sq_ready", STEPS * g + step - 1))
                    dve.tensor_tensor(yg[:, half, :], y2[:], gateT[:, half, :], ALU.mult).then_inc(s["yg_done"], 1)

                def keep_values(tile, step, q):
                    half = q % 2
                    dve.wait_ge(s["turned"], STEPS * g + step + 1)
                    dts = mem.dt[:, 4 * half:4 * half + 4, bass.ds(GH * g + 2 * tile, 2)]
                    dve.tensor_tensor(hid[:, half].rearrange("p t (h d) -> p t h d", h=2),
                                      ps_turn[:, :].rearrange("p (t h d) -> p t h d", t=4, h=2),
                                      dts.unsqueeze(3).broadcast_to((P, 4, 2, MP)), ALU.mult).then_inc(
                                          s["values_kept"], 1)

                def step_of(tile, step, q):
                    conv(tile, 4 + step, q % 2)
                    scans(step, q)
                    if not is_first(step):
                        gated(tile if q % 2 else tile - 1, step - 1, (q + 3) % 4)
                    keep_values(tile, step, q)

                group_steps(dve, step_of)
                gated(GM - 1, STEPS - 1, 3)
                dve.wait_ge(s["sum_ready"], g + 1)
                dve.tensor_scalar(rms[:, 0, :], ps_y[:, 0:NT], 1.0 / (GM * P), EPS, ALU.mult,
                                  ALU.add).then_inc(s["var_ready"], 1)
                dve.wait_ge(s["std_ready"], g + 1)
                dve.reciprocal(rms[:, 2, :], rms[:, 1, :]).then_inc(s["chain"], 1)
                dve.wait_ge(s["chain"], g + 1)
                for t in range(NT):
                    dve.wait_ge(s["out_ready"], done("out_ready", NT * g + t + 1))
                    xt = core.x[:, t, :]
                    dve.scalar_tensor_tensor(out=xt, in0=(ps_misc, ps_turn)[t % 2][:], scalar=rms[:, 2, t:t + 1],
                                             in1=xt, op0=ALU.mult, op1=ALU.add).then_inc(s["out_added"], 1)


class MixerArrays:

    def __init__(self, nc, ctx):
        sb = lambda n, shape, dt=F32: ctx.enter_context(nc.sbuf_tensor("m_" + n, shape, dt))
        self.cols = sb("cols", [P, MG, NCOL])
        self.dec = sb("dec", [P, 3, TOK], BF16)
        self.dt = sb("dt", [P, NT, MH])
        self.start = sb("start", [P, 2 * SEQ])
        self.ones = sb("ones", [P, 1])


def mamba_phase(nc, core, dram):
    with ExitStack() as ctx:
        mem = MixerArrays(nc, ctx)
        dt_phase(nc, core, mem, dram)
        mix_phase(nc, core, mem, dram)


def program(nc, dram, out, parts=None):
    with ExitStack() as ctx:
        core = Core(nc, ctx)
        load_phase(nc, core, dram["x"], dram["consts"])
        for part in parts or ("attn0", "ffn0", "mamba", "ffn0", "across", "ffn1", "attn1", "ffn1"):
            if part == "attn0":
                norm_phase(nc, core, "na0")
                attention_phase(nc, core, "a0", dram["a0_w"], dram["a0_wo"], KV_HEADS, True,
                                dram["a0_b"], dram["a0_bo"])
            elif part == "attn1":
                norm_phase(nc, core, "na1")
                attention_phase(nc, core, "a1", dram["a1_w"], dram["a1_wo"], HEADS, False)
            elif part == "ffn0":
                norm_phase(nc, core, f"nf{core.ln_runs}")
                ffn_phase(nc, core, f"f{core.ln_runs}", dram["f0_gu"], dram["f0_down"])
            elif part == "ffn1":
                norm_phase(nc, core, f"nf{core.ln_runs}")
                quant = {k: dram["f1_" + k] for k in ("a", "da", "b", "db", "s_gu", "s_d")}
                ffn_phase(nc, core, f"f{core.ln_runs}", dram["f1_gu"], dram["f1_down"], quant)
            elif part == "across":
                norm_phase(nc, core, "nab")
                across_batch_phase(nc, core)
            elif part == "mamba":
                norm_phase(nc, core, "nm", add=True, rms_col=dram["m_norm"])
                mamba_phase(nc, core, dram)
        store_phase(nc, core, out)


def rope_tables():
    inv = (1.0 / np.float32(10000.0) ** (np.arange(0, HD, 2, dtype=np.float32) / np.float32(HD))).astype(np.float32)
    ang = np.arange(SEQ, dtype=np.float32)[:, None] * inv[None, :]
    cos, sin = np.cos(ang).astype(np.float32), np.sin(ang).astype(np.float32)
    return np.concatenate([cos, cos], 1), np.concatenate([-sin, sin], 1)


def constants():
    c = np.zeros((P, NCONST), np.float32)
    c[:, C_ID:C_ID + P] = np.eye(P, dtype=np.float32)
    c[:, C_HM:C_HM + HPT] = np.arange(P)[:, None] // HD == np.arange(HPT)[None, :]
    cos, sin = rope_tables()
    c[:, C_COS:C_COS + BT * HD] = cos.reshape(BT, P, HD).transpose(1, 0, 2).reshape(P, BT * HD)
    c[:, C_SIN:C_SIN + BT * HD] = sin.reshape(BT, P, HD).transpose(1, 0, 2).reshape(P, BT * HD)
    c[:, C_TRI:C_TRI + P] = np.where(np.arange(P)[None, :] > np.arange(P)[:, None], MASKED, 0.0)
    return c


def k_major(w):
    return np.ascontiguousarray(w.T.reshape(w.shape[1] // P, P, w.shape[0]).transpose(1, 0, 2))


def pad_to(a, n, axis):
    shape = list(a.shape)
    shape[axis] = n - shape[axis]
    return np.concatenate([a, np.zeros(shape, a.dtype)], axis)


def ffn_tiles(gate, up, down):
    g, u = (pad_to(w, F_PAD, 0).reshape(FT, P, KD, P).transpose(0, 3, 2, 1) for w in (gate, up))
    return (np.ascontiguousarray(np.stack([g, u], 2)),
            np.ascontiguousarray(pad_to(down, F_PAD, 1).T.reshape(FT, P, D)))


def layout(i):
    a = {k: np.asarray(v) for k, v in i.items()}
    d = {"x": a["L0_attn_a_x"].reshape(TOK, D), "consts": constants()}
    w, b = a["L0_attn_a_w_qkv"], a["L0_attn_a_b_qkv"]
    halves = np.concatenate([np.arange(0, HD, 2), np.arange(1, HD, 2)])
    group = HEADS // KV_HEADS
    q_rows = (np.arange(D).reshape(KV_HEADS, group, HD).transpose(1, 0, 2)[:, :, halves]).reshape(-1)
    k_rows = D + np.arange(KV_HEADS * HD).reshape(KV_HEADS, HD)[:, halves].reshape(-1)
    v_rows = D + KV_HEADS * HD + np.arange(KV_HEADS * HD)
    rows = np.concatenate([q_rows, k_rows, v_rows])
    d["a0_w"] = k_major(w[rows])
    d["a0_b"] = b[rows]
    o_cols = np.arange(D).reshape(KV_HEADS, group, HD).transpose(1, 0, 2).reshape(-1)
    d["a0_wo"] = k_major(a["L0_attn_a_w_o"][:, o_cols])
    d["a0_bo"] = a["L0_attn_a_b_o"]
    d["a1_w"] = k_major(np.concatenate([a["L1_attn_b_" + n] for n in ("Wq", "Wk", "Wv")], 0))
    d["a1_wo"] = k_major(a["L1_attn_b_Wo"])
    d["f0_gu"], d["f0_down"] = ffn_tiles(a["L0_ffn_W_gate"], a["L0_ffn_W_up"], a["L0_ffn_W_down"])
    q = {k[7:]: v for k, v in a.items() if k.startswith("L1_ffn_")}
    d["f1_gu"], d["f1_down"] = ffn_tiles(q["gate_q"], q["up_q"], q["down_q"])
    d["f1_a"] = np.ascontiguousarray(
        np.stack([q[n].reshape(KD, P, RANK).transpose(1, 0, 2) for n in ("gate_A", "up_A")], 1))
    d["f1_da"] = np.ascontiguousarray(pad_to(q["down_A"], F_PAD, 0).reshape(FT, P, RANK).transpose(1, 0, 2))
    d["f1_b"] = np.ascontiguousarray(np.stack([pad_to(q[n], F_PAD, 1) for n in ("gate_B", "up_B")], 1))
    d["f1_db"] = q["down_B"]
    d["f1_s_gu"] = np.stack([pad_to(q[n], F_PAD, 0) for n in ("gate_scale", "up_scale")], 0)
    d["f1_s_d"] = q["down_scale"]
    w = a["L0_attn_b_in_proj_w"]
    gate = w[:D_INNER].reshape(MG, GM, P, KD, P)
    hid = w[D_INNER:2 * D_INNER].reshape(MG, GM, P, KD, P)
    d["m_w"] = np.ascontiguousarray(np.stack([hid, gate], 2).transpose(0, 1, 5, 2, 4, 3))
    bc = w[2 * D_INNER:2 * D_INNER + 2 * MG * MN].reshape(2, MG, P, KD, P)
    d["m_wbc"] = np.ascontiguousarray(bc.transpose(1, 4, 0, 3, 2))
    d["m_wdt"] = k_major(w[2 * D_INNER + 2 * MG * MN:])
    d["m_wout"] = np.ascontiguousarray(a["L0_attn_b_out_proj_w"].T.reshape(MG, GM, P, D).transpose(0, 2, 1, 3))
    taps = np.concatenate([a["L0_attn_b_conv_w"], a["L0_attn_b_conv_b"][:, None]], 1)
    t_hid = taps[:D_INNER].reshape(MG, GM, P, TAPS + 1)
    t_bc = taps[D_INNER:].reshape(2, MG, P, TAPS + 1).transpose(1, 0, 2, 3)
    cols = np.concatenate([t_hid, t_bc], 1).transpose(2, 0, 1, 3).reshape(P, MG, -1)
    per_feature = lambda v: v.reshape(MG, GM, P).transpose(2, 0, 1)
    dp = per_feature(np.repeat(a["L0_attn_b_Dp"], MP))
    d["m_cols"] = np.ascontiguousarray(np.concatenate([cols, dp, per_feature(a["L0_attn_b_gnorm_w"])], 2))
    d["m_dtb"] = a["L0_attn_b_dt_bias"][:, None]
    d["m_alog"] = a["L0_attn_b_A_log"][:, None]
    d["m_norm"] = np.ascontiguousarray(a["L0_attn_b_norm_w"].reshape(KD, P).T)
    return {k: np.ascontiguousarray(v) for k, v in d.items()}


def kernel(**inputs):
    import concourse.bacc as _bacc
    from concourse.bass_utils import run_bass_kernel_spmd as _run

    nc = _bacc.Bacc("TRN2", target_bir_lowering=False, num_devices=1)
    arrays = layout(inputs)
    dram = {k: nc.dram_tensor(f"in_{k}", v.shape, mybir.dt.from_np(v.dtype), kind="ExternalInput").ap()
            for k, v in arrays.items()}
    out = nc.dram_tensor("out_x", (TOK, D), F32, kind="ExternalOutput").ap()
    program(nc, dram, out)
    r = _run(nc, [{f"in_{k}": v for k, v in arrays.items()}], core_ids=[0])
    return r.results[0]["out_x"].reshape(BATCH, SEQ, D)
```

```python
from contextlib import ExitStack

import numpy as np

import concourse.bass as bass
from concourse import mybir

F32 = mybir.dt.float32
F32R = mybir.dt.float32r
BF16 = mybir.dt.bfloat16
I32 = mybir.dt.int32
ALU = mybir.AluOpType
ACT = mybir.ActivationFunctionType
AX = mybir.AxisListType

P = 128
BATCH, SEQ, D = 4, 256, 512
TOK = BATCH * SEQ
NT = TOK // P
KD = D // P
BT = SEQ // P
HALF = 512
EPS = 1e-5

HEADS, KV_HEADS, HD = 32, 8, 16
HPT = P // HD
F_FF = 1376
FT = -(-F_FF // P)
F_PAD = FT * P
RANK = 32
Q_ZERO, Q_STEP, LR_SCALE = 7.5, 0.005, 0.02

MH, MP, MG, MN, TAPS = 128, 64, 8, 128, 4
D_INNER = MH * MP
GF = D_INNER // MG
GM = GF // P
GH = MH // MG
STEPS = 2 * GM
NCOL = (GM + 2) * (TAPS + 1) + 2 * GM
MASKED = -1e20

C_ID, C_HM, C_COS, C_SIN, C_TRI = 0, P, P + HPT, P + HPT + BT * HD, P + HPT + 2 * BT * HD
NCONST = C_TRI + P


class Core:

    def __init__(self, nc, ctx):
        self.nc = nc
        sb = lambda name, shape, dt=F32: ctx.enter_context(nc.sbuf_tensor(name, shape, dt))
        self.x = sb("x_res", [P, NT, D])
        self.xh = sb("xh", [P, KD, TOK], F32R)
        self.xl = sb("xl", [P, KD, TOK], F32R)
        self.consts = sb("consts", [P, NCONST])
        self.identb = sb("identb", [P, P], BF16)
        self.tri4 = sb("tri4", [P, 4, P], BF16)
        self.tri_right = sb("tri_right", [P, 2, 2, P], BF16)
        self.ident = self.consts[:, C_ID:C_ID + P]
        sem = lambda name: ctx.enter_context(nc.semaphore(name))
        self.ln = {n: sem("ln_" + n) for n in ("stats", "chain", "var", "std", "xn", "turned", "evac", "added")}
        self.ln_runs = 0
        self.ln_links = 0
        self.ln_std = 0


def phase_semaphores(nc, ctx, prefix):
    taken = []

    def clear():
        nc.clear_and_free_semaphores(taken)
        nc.all_engine_barrier(sem_only=True)

    ctx.callback(clear)

    def sem(name):
        taken.append(nc.alloc_semaphore(prefix + name))
        return taken[-1]

    return sem


def load_phase(nc, core, x_dram, const_dram):
    with ExitStack() as ctx:
        loaded, cst, made = (ctx.enter_context(nc.semaphore(n)) for n in ("in_loaded", "const_loaded", "const_made"))
        block = ctx.enter_context(nc.Block())

        @block.sync
        def _(sp):
            sp.dma_start(core.consts[:], const_dram).then_inc(cst, 16)
            sp.dma_start(core.x[:], x_dram.rearrange("(t p) d -> p t d", p=P)).then_inc(loaded, 16)
            sp.wait_ge(loaded, 16)

        @block.vector
        def _(dve):
            dve.wait_ge(cst, 16)
            dve.tensor_copy(core.identb[:], core.ident)
            tri = core.consts[:, C_TRI:C_TRI + P]
            dve.tensor_copy(core.tri4[:], tri.unsqueeze(1).broadcast_to((P, 4, P)))
            dve.memset(core.tri_right[:], 0.0).then_inc(made, 1)
            dve.wait_ge(made, 1)
            for h in range(2):
                dve.tensor_copy(core.tri_right[:, h, 1, :], tri)


def store_phase(nc, core, out_dram):
    with ExitStack() as ctx:
        stored = ctx.enter_context(nc.semaphore("stored"))
        block = ctx.enter_context(nc.Block())

        @block.sync
        def _(sp):
            sp.dma_start(out_dram.rearrange("(t p) d -> p t d", p=P), core.x[:]).then_inc(stored, 16)
            sp.wait_ge(stored, 16)


def split_product(pe, out, wh, wl, xh, xl, start, stop):
    pe.matmul(out, wh, xh, start=start, stop=False, skip_group_check=True)
    ins = pe.matmul(out, wh, xl, start=False, stop=stop and wl is None, skip_group_check=True)
    if wl is not None:
        ins = pe.matmul(out, wl, xh, start=False, stop=stop, skip_group_check=True)
    return ins


def norm_phase(nc, core, name, add=False, rms_col=None, whole=None):
    run, s = core.ln_runs, core.ln
    core.ln_runs += 1
    links = [core.ln_links]
    with ExitStack() as ctx:
        sb = lambda n, shape, dt=F32: ctx.enter_context(nc.sbuf_tensor(name + n, shape, dt))
        st = sb("st", [P, NT, 6])
        v = sb("v", [P, 10, NT])
        xn = sb("xn", [P, NT, D])
        hn = sb("hn", [P, NT, D]) if rms_col is not None else xn
        wcol = sb("wcol", [P, KD]) if rms_col is not None else None
        ps = ctx.enter_context(nc.psum_tensor(name + "ps", [P, 2, KD, HALF], F32))
        wsem = ctx.enter_context(nc.semaphore(name + "w")) if rms_col is not None else None
        block = ctx.enter_context(nc.Block())
        MEAN2, DIFF, VSUM, DSQ, VAR, MEAN, STD, RSTD, MS, RMS = (v[:, i, :] for i in range(10))
        n_std = 2 if rms_col is not None else 1

        high = whole if whole is not None else core.xh

        def evac(eng, half, f):
            out = high[:, f, half * HALF:(half + 1) * HALF]
            src = ps[:, half, f, :]
            if eng is nc.scalar:
                return eng.activation(out, src, ACT.Copy, scale=1.0 if wcol is None else wcol[:, f:f + 1])
            if wcol is None:
                return eng.tensor_copy(out, src)
            return eng.tensor_scalar(out, src, wcol[:, f:f + 1], None, ALU.mult)

        def low_part(half, f):
            tok = slice(half * HALF, (half + 1) * HALF)
            src, hi, out = ps[:, half, f, :], core.xh[:, f, tok], core.xl[:, f, tok]
            if wcol is None:
                nc.vector.tensor_tensor(out, src, hi, ALU.subtract)
            else:
                nc.vector.scalar_tensor_tensor(out=out, in0=src, scalar=wcol[:, f:f + 1], in1=hi, op0=ALU.mult,
                                               op1=ALU.subtract)

        @block.sync
        def _(sp):
            if wcol is not None:
                sp.dma_start(wcol[:], rms_col).then_inc(wsem, 16)

        @block.vector
        def _(dve):
            def link(ins):
                links[0] += 1
                ins.then_inc(s["chain"], 1)
                dve.wait_ge(s["chain"], links[0])

            with dve.Fori(0, NT) as t:
                dve.bn_stats(st[:, t, :], core.x[:, t, :]).then_inc(s["stats"], 1)
            dve.wait_ge(s["stats"], NT * (run + 1))
            dve.tensor_tensor(DIFF, st[:, :, 1], st[:, :, 4], ALU.subtract)
            dve.tensor_tensor(VSUM, st[:, :, 2], st[:, :, 5], ALU.add)
            link(dve.tensor_tensor(MEAN2, st[:, :, 1], st[:, :, 4], ALU.add))
            dve.tensor_scalar(MEAN, MEAN2, 0.5, None, ALU.mult)
            link(dve.scalar_tensor_tensor(out=DSQ, in0=DIFF, scalar=0.25, in1=DIFF, op0=ALU.mult, op1=ALU.mult))
            link(dve.scalar_tensor_tensor(out=VAR, in0=VSUM, scalar=1.0 / D, in1=DSQ, op0=ALU.mult, op1=ALU.add))
            dve.tensor_scalar(DSQ, VAR, EPS, None, ALU.add).then_inc(s["var"], 1)
            dve.wait_ge(s["std"], core.ln_std + 1)
            link(dve.reciprocal(RSTD, STD))
            if n_std == 2:
                link(dve.tensor_tensor(MS, RSTD, RSTD, ALU.mult))
                link(dve.tensor_tensor(MS, MS, VAR, ALU.mult))
                dve.tensor_scalar(DSQ, MS, EPS, None, ALU.add).then_inc(s["var"], 1)
                dve.wait_ge(s["std"], core.ln_std + 2)
                link(dve.reciprocal(RMS, STD))
            for t in range(NT):
                ins = dve.tensor_scalar(xn[:, t, :], core.x[:, t, :], MEAN[:, t:t + 1], RSTD[:, t:t + 1],
                                        ALU.subtract, ALU.mult)
                if n_std == 2:
                    link(ins)
                    ins = dve.tensor_scalar(hn[:, t, :], xn[:, t, :], RMS[:, t:t + 1], None, ALU.mult)
                ins.then_inc(s["xn"], 1)
            if wcol is not None:
                dve.wait_ge(wsem, 16)
            for half in range(2):
                dve.wait_ge(s["turned"], NT * run + 4 * (half + 1))
                for f in (0, 1):
                    ins = evac(nc.vector, half, f)
                if whole is None:
                    link(ins)
                    for f in (0, 1):
                        low_part(half, f)
                    dve.wait_ge(s["evac"], 2 * run + half + 1)
                    for f in (2, 3):
                        low_part(half, f)

        @block.gpsimd
        def _(pool):
            if add:
                for t in range(NT):
                    pool.wait_ge(s["xn"], NT * run + t + 1)
                    pool.tensor_tensor(core.x[:, t, :], core.x[:, t, :], xn[:, t, :], ALU.add)

        @block.scalar
        def _(act):
            for i in range(n_std):
                act.wait_ge(s["var"], core.ln_std + i + 1)
                act.activation(STD, DSQ, ACT.Sqrt).then_inc(s["std"], 1)
            if wcol is not None:
                act.wait_ge(wsem, 16)
            for half in range(2):
                act.wait_ge(s["turned"], NT * run + 4 * (half + 1))
                for f in (2, 3):
                    ins = evac(nc.scalar, half, f)
                ins.then_inc(s["evac"], 1)

        @block.tensor
        def _(pe):
            for t in range(NT):
                pe.wait_ge(s["xn"], NT * run + t + 1)
                for f in range(KD):
                    ins = pe.transpose(ps[:, t // 4, f, (t % 4) * P:(t % 4 + 1) * P],
                                       hn[:, t, f * P:(f + 1) * P], core.ident)
                ins.then_inc(s["turned"], 1)
    core.ln_links = links[0]
    core.ln_std += n_std


def slice_steps(eng, half, body):
    for f in range(2):
        body(f, FT * half + f, (half * FT + f) % 2)
    with eng.Fori(0, (FT - 2) // 2) as i:
        for j in range(2):
            body(2 + 2 * i + j, FT * half + 2 + 2 * i + j, (half * FT + j) % 2)
    for f in range(FT - FT % 2, FT):
        body(f, FT * half + f, (half * FT + f) % 2)


def early(step, n):
    return isinstance(step, int) and step < n


def landed(step, slot):
    return 8 * (step - slot) + 16


def ffn_phase(nc, core, name, w_gu, w_down):
    LAST = 2 * FT
    with ExitStack() as ctx:
        sb = lambda n, shape, dt=F32: ctx.enter_context(nc.sbuf_tensor(name + n, shape, dt))
        pb = lambda n, shape: ctx.enter_context(nc.psum_tensor(name + n, shape, F32))
        sem = phase_semaphores(nc, ctx, name)
        wgu = sb("wgu", [P, 2, 2, KD, P])
        wd = sb("wd", [P, 2, D])
        wgu_h, wgu_l = (sb(n, [P, 2, 2, KD, P], F32R) for n in ("wgu_h", "wgu_l"))
        wd_h, wd_l = (sb(n, [P, 2, D], F32R) for n in ("wd_h", "wd_l"))
        sil = sb("sil", [P, 2, HALF])
        hT = sb("hT", [P, 2, HALF])
        hT_h, hT_l = (sb(n, [P, 2, HALF], F32R) for n in ("hT_h", "hT_l"))
        ps_gu = pb("psgu", [P, 2, HALF])
        acc = pb("acc", [P, 4, D])
        gu_loaded = [sem(f"gu_loaded{i}") for i in range(2)]
        d_loaded = [sem(f"d_loaded{i}") for i in range(2)]
        (gu_high, gu_low, d_high, d_low, gate_ready, up_ready, silu_done, h_ready, h_high, h_low, down_done,
         acc_added) = (sem(n) for n in ("gu_high", "gu_low", "d_high", "d_low", "gate_ready", "up_ready", "silu_done",
                                        "h_ready", "h_high", "h_low", "down_done", "acc_added"))
        block = ctx.enter_context(nc.Block())

        @block.sync
        def _(sp):
            for half in range(2):
                def load(f, step, slot):
                    if not early(step, 2):
                        sp.wait_ge(gu_low, step - 1)
                    sp.dma_start(wgu[:, slot], w_gu[f]).then_inc(gu_loaded[slot], 16)
                    if not early(step, 2):
                        sp.wait_ge(d_low, step - 1)
                    sp.dma_start(wd[:, slot], w_down[f]).then_inc(d_loaded[slot], 16)
                slice_steps(sp, half, load)

        @block.tensor
        def _(pe):
            for half in range(2):
                tok = slice(half * HALF, (half + 1) * HALF)

                def gate_up(step, slot):
                    pe.wait_ge(gu_low, step + 1)
                    for w, ready, used in ((0, gate_ready, silu_done), (1, up_ready, h_ready)):
                        if not early(step, 1):
                            pe.wait_ge(used, step)
                        for k in range(KD):
                            ins = split_product(pe, ps_gu[:, w, :], wgu_h[:, slot, w, k, :], wgu_l[:, slot, w, k, :],
                                                core.xh[:, k, tok], core.xl[:, k, tok], k == 0, k == KD - 1)
                        ins.then_inc(ready, 1)

                def down(step, slot, first, last):
                    pe.wait_ge(d_low, step + 1)
                    if first and half:
                        pe.wait_ge(acc_added, 4)
                    pe.wait_ge(h_high, step + 1)
                    for t in range(4):
                        hi = hT_h[:, slot, t * P:(t + 1) * P]
                        pe.matmul(acc[:, t, :], hi, wd_h[:, slot, :], start=first, stop=False, skip_group_check=True)
                        pe.matmul(acc[:, t, :], hi, wd_l[:, slot, :], start=False, stop=False, skip_group_check=True)
                    pe.wait_ge(h_low, step + 1)
                    for t in range(4):
                        ins = pe.matmul(acc[:, t, :], hT_l[:, slot, t * P:(t + 1) * P], wd_h[:, slot, :],
                                        start=False, stop=last, skip_group_check=True)
                    ins.then_inc(down_done, 1)

                def both(f, step, slot):
                    gate_up(step, slot)
                    if not early(f, 1):
                        down(step - 1, 1 - slot, early(f, 2), False)

                slice_steps(pe, half, both)
                down(FT * (half + 1) - 1, (FT * (half + 1) - 1) % 2, False, True)

        @block.scalar
        def _(act):
            def silu_and_round(step, slot):
                act.wait_ge(gate_ready, step + 1)
                if not early(step, 2):
                    act.wait_ge(h_ready, step - 1)
                act.activation(sil[:, slot, :], ps_gu[:, 0, :], ACT.Silu).then_inc(silu_done, 1)
                act.wait_ge(h_ready, step + 1)
                act.activation(hT_h[:, slot, :], hT[:, slot, :], ACT.Copy).then_inc(h_high, 1)

            def work(f, step, slot):
                act.wait_ge(gu_loaded[slot], landed(step, slot))
                if not early(step, 2):
                    act.wait_ge(up_ready, step - 1)
                act.activation(wgu_h[:, slot], wgu[:, slot], ACT.Copy).then_inc(gu_high, 1)
                if not early(step, 1):
                    silu_and_round(step - 1, 1 - slot)
                act.wait_ge(d_loaded[slot], landed(step, slot))
                if not early(step, 2):
                    act.wait_ge(down_done, step - 1)
                act.activation(wd_h[:, slot], wd[:, slot], ACT.Copy).then_inc(d_high, 1)

            for half in range(2):
                slice_steps(act, half, work)
            silu_and_round(LAST - 1, (LAST - 1) % 2)

        @block.gpsimd
        def _(pool):
            def rests(f, step, slot):
                pool.wait_ge(gu_high, step + 1)
                pool.tensor_tensor(wgu_l[:, slot], wgu[:, slot], wgu_h[:, slot], ALU.subtract).then_inc(gu_low, 1)
                pool.wait_ge(d_high, step + 1)
                pool.tensor_tensor(wd_l[:, slot], wd[:, slot], wd_h[:, slot], ALU.subtract).then_inc(d_low, 1)

            for half in range(2):
                slice_steps(pool, half, rests)

        @block.vector
        def _(dve):
            def product(step, slot):
                dve.wait_ge(silu_done, step + 1)
                dve.wait_ge(up_ready, step + 1)
                if not early(step, 2):
                    dve.wait_ge(down_done, step - 1)
                dve.tensor_tensor(hT[:, slot, :], ps_gu[:, 1, :], sil[:, slot, :], ALU.mult).then_inc(h_ready, 1)
                dve.wait_ge(h_high, step + 1)
                dve.tensor_tensor(hT_l[:, slot, :], hT[:, slot, :], hT_h[:, slot, :],
                                  ALU.subtract).then_inc(h_low, 1)

            for half in range(2):
                slice_steps(dve, half, lambda f, step, slot: product(step, slot))
                dve.wait_ge(down_done, FT * (half + 1))
                for t in range(4):
                    xt = core.x[:, 4 * half + t, :]
                    dve.tensor_tensor(xt, acc[:, t, :], xt, ALU.add).then_inc(acc_added, 1)


def quant_ffn_phase(nc, core, name, w_gu, w_down, small):
    LAST = 2 * FT
    with ExitStack() as ctx:
        sb = lambda n, shape, dt=F32: ctx.enter_context(nc.sbuf_tensor(name + n, shape, dt))
        pb = lambda n, shape: ctx.enter_context(nc.psum_tensor(name + n, shape, F32))
        sem = phase_semaphores(nc, ctx, name)
        codes_gu = sb("codes_gu", [P, 2, 2, KD, P], I32)
        codes_d = sb("codes_d", [P, 2, D], I32)
        cgu = sb("cgu", [P, 2, 2, KD, P], F32R)
        cd = sb("cd", [P, 2, D], F32R)
        low_in = sb("low_in", [P, 2, KD, RANK])
        low_da = sb("low_da", [P, FT, RANK])
        low_b = sb("low_b", [RANK, 2, F_PAD])
        low_db = sb("low_db", [RANK, D])
        scale_gu = sb("scale_gu", [P, 2, FT])
        scale_d = sb("scale_d", [P, D])
        b_slot = sb("b_slot", [RANK, 2, 2, P])
        da_slot = sb("da_slot", [P, 2, RANK])
        whole_x = sb("whole_x", [P, KD, TOK])
        lowx = sb("lowx", [RANK, 2, TOK])
        lowh = sb("lowh", [RANK, HALF])
        low = sb("low", [P, 2, HALF])
        gate = sb("gate", [P, HALF])
        up = sb("up", [P, HALF])
        sil = sb("sil", [P, HALF])
        hT = sb("hT", [P, 2, HALF])
        hT_h, hT_l = (sb(n, [P, 2, HALF], F32R) for n in ("hT_h", "hT_l"))
        scaled_acc = sb("scaled_acc", [P, 4, D])
        ps_gu = pb("psgu", [P, 2, HALF])
        ps_low = pb("pslow", [P, HALF])
        ps_lowh = pb("pslowh", [P, HALF])
        acc = pb("acc", [P, 4, D])
        gu_loaded = [sem(f"gu_loaded{i}") for i in range(2)]
        d_loaded = [sem(f"d_loaded{i}") for i in range(2)]
        whole_ready = [sem(f"whole_ready{i}") for i in range(2)]
        (small_loaded, scaled, lowx_ready, lowx_kept, gu_ready, d_ready, b_copied, gate_ready, up_ready,
         low_ready, low_kept, gate_kept, up_kept, silu_done, h_ready, h_high, h_low, down_done, lowh_kept, acc_scaled, rank_ready,
         x_added, acc_added) = (
            sem(n) for n in ("small_loaded", "scaled", "lowx_ready", "lowx_kept", "gu_ready",
                             "d_ready", "b_copied", "gate_ready", "up_ready", "low_ready", "low_kept", "gate_kept", "up_kept", "silu_done",
                             "h_ready", "h_high", "h_low", "down_done", "lowh_kept", "acc_scaled", "rank_ready",
                             "x_added", "acc_added"))
        block = ctx.enter_context(nc.Block())

        @block.sync
        def _(sp):
            for dst, src in ((low_in, small["a"]), (low_da, small["da"]), (low_b, small["b"]),
                             (low_db, small["db"]), (scale_gu, small["s_gu"])):
                sp.dma_start(dst[:], src).then_inc(small_loaded, 16)
            sp.dma_start(scale_d[:], small["s_d"].partition_broadcast(P)).then_inc(small_loaded, 16)
            for half in range(2):
                def load(f, step, slot):
                    if not early(step, 2):
                        sp.wait_ge(gu_ready, step - 1)
                    sp.dma_start(codes_gu[:, slot], w_gu[f]).then_inc(gu_loaded[slot], 16)
                    if not early(step, 2):
                        sp.wait_ge(d_ready, step - 1)
                    sp.dma_start(codes_d[:, slot], w_down[f]).then_inc(d_loaded[slot], 16)
                slice_steps(sp, half, load)

        @block.tensor
        def _(pe):
            pe.wait_ge(small_loaded, 16 * 6)
            for half in range(2):
                pe.wait_ge(whole_ready[half], 1)
                if half:
                    pe.wait_ge(lowx_kept, 2)
                for w, ps in ((0, ps_low), (1, ps_lowh)):
                    for k in range(KD):
                        ins = pe.matmul(ps[0:RANK, :], low_in[:, w, k, :], whole_x[:, k, half * HALF:(half + 1) * HALF],
                                        start=k == 0,
                                        stop=k == KD - 1)
                    ins.then_inc(lowx_ready, 1)
            pe.wait_ge(lowx_kept, 4)
            for half in range(2):
                tok = slice(half * HALF, (half + 1) * HALF)

                def codes_and_low(w, step, slot, ready, kept):
                    if w or not early(step, 1):
                        pe.wait_ge(low_kept, 2 * step + w)
                    pe.matmul(ps_low[:], b_slot[:, slot, w, :], lowx[:, w, tok], start=True,
                              stop=True).then_inc(low_ready, 1)
                    if not early(step, 1):
                        pe.wait_ge(kept, step)
                    for k in range(KD):
                        ins = split_product(pe, ps_gu[:, w, :], cgu[:, slot, w, k, :], None, core.xh[:, k, tok],
                                            core.xl[:, k, tok], k == 0, k == KD - 1)
                    ins.then_inc(ready, 1)

                def down(step, slot, first, last):
                    pe.wait_ge(d_ready, step + 1)
                    pe.wait_ge(h_ready, step + 1)
                    if first and half:
                        pe.wait_ge(acc_added, 4)
                    pe.matmul(ps_lowh[0:RANK, :], da_slot[:, slot, :], hT[:, slot, :], start=first, stop=last,
                              skip_group_check=True)
                    pe.wait_ge(h_high, step + 1)
                    for t in range(4):
                        pe.matmul(acc[:, t, :], hT_h[:, slot, t * P:(t + 1) * P], cd[:, slot, :], start=first,
                                  stop=False, skip_group_check=True)
                    pe.wait_ge(h_low, step + 1)
                    for t in range(4):
                        ins = pe.matmul(acc[:, t, :], hT_l[:, slot, t * P:(t + 1) * P], cd[:, slot, :], start=False,
                                        stop=last, skip_group_check=True)
                    ins.then_inc(down_done, 1)

                def both(f, step, slot):
                    pe.wait_ge(gu_ready, step + 1)
                    pe.wait_ge(b_copied, step + 1)
                    codes_and_low(0, step, slot, gate_ready, gate_kept)
                    if not early(f, 1):
                        down(step - 1, 1 - slot, early(f, 2), False)
                    codes_and_low(1, step, slot, up_ready, up_kept)

                slice_steps(pe, half, both)
                down(FT * (half + 1) - 1, (FT * (half + 1) - 1) % 2, False, True)
                pe.wait_ge(lowh_kept, half + 1)
                for t in range(4):
                    pe.wait_ge(acc_scaled, 4 * half + t + 1)
                    pe.matmul(acc[:, t, :], lowh[:, t * P:(t + 1) * P], low_db[:], start=True,
                              stop=True).then_inc(rank_ready, 1)

        @block.scalar
        def _(act):
            for n in range(4):
                half, w = n // 2, n % 2
                act.wait_ge(lowx_ready, n + 1)
                act.activation(lowx[:, w, half * HALF:(half + 1) * HALF], (ps_low, ps_lowh)[w][0:RANK, :], ACT.Copy,
                               scale=LR_SCALE).then_inc(lowx_kept, 1)

            def copy_b(f, slot):
                act.activation(b_slot[:, slot, :, :], low_b[:, :, bass.ts(f, P)], ACT.Copy).then_inc(b_copied, 1)

            def keep_low(w, step):
                act.wait_ge(low_ready, 2 * step + w + 1)
                if not early(step, 1):
                    act.wait_ge((gate_kept, up_kept)[w], step)
                act.activation(low[:, w, :], ps_low[:], ACT.Copy).then_inc(low_kept, 1)

            def round_h(step, slot):
                act.wait_ge(h_ready, step + 1)
                act.activation(hT_h[:, slot, :], hT[:, slot, :], ACT.Copy).then_inc(h_high, 1)

            def work(f, step, slot):
                if isinstance(step, int) and step == FT:
                    round_h(step - 1, 1 - slot)
                    keep_lowh(0)
                    keep_low(0, step)
                else:
                    keep_low(0, step)
                    if not early(step, 1):
                        round_h(step - 1, 1 - slot)
                act.wait_ge(gate_kept, step + 1)
                act.activation(sil[:], gate[:], ACT.Silu).then_inc(silu_done, 1)
                keep_low(1, step)
                if isinstance(f, int) and f == FT - 1:
                    if step < LAST - 1:
                        copy_b(0, 1 - slot)
                else:
                    copy_b(f + 1, 1 - slot)

            def keep_lowh(half):
                act.wait_ge(down_done, FT * (half + 1))
                act.activation(lowh[:], ps_lowh[0:RANK, :], ACT.Copy, scale=LR_SCALE).then_inc(lowh_kept, 1)

            copy_b(0, 0)
            for half in range(2):
                slice_steps(act, half, work)
            round_h(LAST - 1, (LAST - 1) % 2)
            keep_lowh(1)

        @block.gpsimd
        def _(pool):
            pool.tensor_tensor(whole_x[:, :, HALF:], core.xh[:, :, HALF:], core.xl[:, :, HALF:],
                               ALU.add).then_inc(whole_ready[1], 1)

            def hidden(step, slot):
                pool.wait_ge(up_kept, step + 1)
                pool.wait_ge(silu_done, step + 1)
                if not early(step, 2):
                    pool.wait_ge(down_done, step - 1)
                pool.tensor_tensor(hT[:, slot, :], up[:], sil[:], ALU.mult).then_inc(h_ready, 1)
                pool.wait_ge(h_high, step + 1)
                pool.tensor_tensor(hT_l[:, slot, :], hT[:, slot, :], hT_h[:, slot, :],
                                   ALU.subtract).then_inc(h_low, 1)

            for half in range(2):
                slice_steps(pool, half, lambda f, step, slot: hidden(step, slot))

        @block.vector
        def _(dve):
            dve.tensor_tensor(whole_x[:, :, 0:HALF], core.xh[:, :, 0:HALF], core.xl[:, :, 0:HALF],
                              ALU.add).then_inc(whole_ready[0], 1)
            dve.wait_ge(small_loaded, 16 * 6)
            dve.tensor_scalar(scale_gu[:], scale_gu[:], Q_STEP, None, ALU.mult).then_inc(scaled, 1)
            dve.tensor_scalar(scale_d[:], scale_d[:], Q_STEP, None, ALU.mult).then_inc(scaled, 1)
            dve.wait_ge(scaled, 2)

            def scale_and_add(w, f, step, dst):
                dve.wait_ge(low_kept, 2 * step + w + 1)
                col = scale_gu[:, w, f:f + 1] if isinstance(f, int) else scale_gu[:, w, bass.ds(f, 1)]
                return dve.scalar_tensor_tensor(out=dst[:], in0=ps_gu[:, w, :], scalar=col, in1=low[:, w, :],
                                                op0=ALU.mult, op1=ALU.add)

            def keep_gate(f, step):
                dve.wait_ge(gate_ready, step + 1)
                if not early(step, 1):
                    dve.wait_ge(silu_done, step)
                scale_and_add(0, f, step, gate).then_inc(gate_kept, 1)

            def keep_up(f, step):
                dve.wait_ge(up_ready, step + 1)
                if not early(step, 1):
                    dve.wait_ge(h_ready, step)
                scale_and_add(1, f, step, up).then_inc(up_kept, 1)

            def centre(f, step, slot):
                dve.wait_ge(gu_loaded[slot], landed(step, slot))
                if not early(step, 2):
                    dve.wait_ge(up_ready, step - 1)
                dve.tensor_scalar(cgu[:, slot], codes_gu[:, slot], -Q_ZERO, None, ALU.add).then_inc(gu_ready, 1)

            def work(f, step, slot):
                if early(step, 1):
                    centre(f, step, slot)
                dve.wait_ge(d_loaded[slot], landed(step, slot))
                if not early(step, 2):
                    dve.wait_ge(down_done, step - 1)
                dve.tensor_copy(da_slot[:, slot, :], low_da[:, f, :])
                dve.tensor_scalar(cd[:, slot, :], codes_d[:, slot, :], -Q_ZERO, None, ALU.add).then_inc(d_ready, 1)
                keep_gate(f, step)
                if not (isinstance(step, int) and step == LAST - 1):
                    centre(f, step + 1, 1 - slot)
                keep_up(f, step)

            for half in range(2):
                slice_steps(dve, half, work)
                dve.wait_ge(down_done, FT * (half + 1))
                for t in range(4):
                    dve.tensor_tensor(scaled_acc[:, t, :], acc[:, t, :], scale_d[:],
                                      ALU.mult).then_inc(acc_scaled, 1)
                for t in range(4):
                    xt = core.x[:, 4 * half + t, :]
                    dve.wait_ge(acc_scaled, 4 * half + t + 1)
                    dve.tensor_tensor(xt, scaled_acc[:, t, :], xt, ALU.add).then_inc(x_added, 1)
                for t in range(4):
                    xt = core.x[:, 4 * half + t, :]
                    dve.wait_ge(x_added, 4 * half + t + 1)
                    dve.wait_ge(rank_ready, 4 * half + t + 1)
                    dve.tensor_tensor(xt, acc[:, t, :], xt, ALU.add).then_inc(acc_added, 1)


def across_batch_phase(nc, core, xT):
    B2 = BATCH * BATCH
    with ExitStack() as ctx:
        sb = lambda n, shape, dt=F32: ctx.enter_context(nc.sbuf_tensor("ab_" + n, shape, dt))
        sem = phase_semaphores(nc, ctx, "ab_")
        sc = sb("sc", [P, KD, BATCH, BATCH])
        junk = sb("junk", [P, SEQ])
        mx = sb("mx", [P, KD * BATCH])
        ex = sb("ex", [P, KD * BATCH, BATCH])
        sm = sb("sm", [P, KD * BATCH])
        msg = sb("msg", [P, KD, TOK])
        ps = ctx.enter_context(nc.psum_tensor("ab_ps", [P, NT, D], F32))
        chain, max_done, exp_done, msg_ready, turned = (
            sem(n) for n in ("chain", "max_done", "exp_done", "msg_ready", "turned"))
        block = ctx.enter_context(nc.Block())
        xv = xT[:, :, :].rearrange("p k (b s) -> p k b s", b=BATCH)
        mv = msg[:, :, :].rearrange("p k (b s) -> p k b s", b=BATCH)

        @block.vector
        def _(dve):
            n_chain = [0]

            def link(ins):
                n_chain[0] += 1
                ins.then_inc(chain, 1)
                dve.wait_ge(chain, n_chain[0])

            for k in range(KD):
                for n in range(BATCH):
                    for m in range(n, BATCH):
                        ins = dve.tensor_tensor_reduce(junk[:], xv[:, k, n, :], xv[:, k, m, :], 1.0, 0.0, ALU.mult,
                                                       ALU.add, sc[:, k, n, m:m + 1])
                        link(ins)
            for n in range(BATCH):
                for m in range(n):
                    ins = dve.tensor_copy(sc[:, :, n, m], sc[:, :, m, n])
            link(ins)
            rows = sc[:, :, :, :].rearrange("p k n m -> p (k n) m")
            link(dve.tensor_reduce(mx[:], rows, AX.X, ALU.max))
            dve.tensor_tensor(ex[:], rows, mx[:].unsqueeze(2).broadcast_to((P, KD * BATCH, BATCH)),
                              ALU.subtract).then_inc(max_done, 1)
            dve.wait_ge(exp_done, 1)
            link(dve.tensor_reduce(sm[:], ex[:], AX.X, ALU.add))
            link(dve.reciprocal(mx[:], sm[:]))
            link(dve.tensor_tensor(ex[:], ex[:], mx[:].unsqueeze(2).broadcast_to((P, KD * BATCH, BATCH)), ALU.mult))
            for k in range(KD):
                for m in range(BATCH):
                    for n in range(BATCH):
                        ins = dve.scalar_tensor_tensor(
                            out=mv[:, k, n, :], in0=xv[:, k, m, :], scalar=ex[:, k * BATCH + n, m:m + 1],
                            in1=xv[:, k, n, :] if m == 0 else mv[:, k, n, :], op0=ALU.mult, op1=ALU.add)
                    if m < BATCH - 1:
                        link(ins)
                ins.then_inc(msg_ready, 1)
            for t in range(NT):
                dve.wait_ge(turned, (KD - 1) * NT + t + 1)
                xt = core.x[:, t, :]
                dve.tensor_tensor(xt, ps[:, t, :], xt, ALU.add)

        @block.scalar
        def _(act):
            act.wait_ge(max_done, 1)
            act.activation(ex[:], ex[:], ACT.Exp, scale=1.0 / float(SEQ) ** 0.5).then_inc(exp_done, 1)

        @block.tensor
        def _(pe):
            for k in range(KD):
                pe.wait_ge(msg_ready, k + 1)
                for t in range(NT):
                    pe.transpose(ps[:, t, k * P:(k + 1) * P], msg[:, k, t * P:(t + 1) * P],
                                 core.ident).then_inc(turned, 1)


def attention_phase(nc, core, name, w_qkv, w_o, kv_heads, causal, b_qkv=None, b_o=None):
    kv_t = kv_heads * HD // P
    KW, VW = kv_t * P, kv_heads * HD
    ALL = D + KW + VW
    QUADS = HPT // 4
    PER_T = KD * QUADS
    JOBS = PER_T * BT
    jobs = [(n // QUADS % KD, n % QUADS, n // PER_T) for n in range(JOBS)]
    pieces = [(t, at, min(HALF, ALL - at)) for t in range(BT) for at in range(0, ALL, HALF)]
    N_PIECES = len(pieces)
    PIECE_AT = {(0, 1, 3, 4, 5, 6)[i]: i for i in range(N_PIECES)}
    TURN_AT, PROJECT_AT = PER_T + 1, PER_T + 2
    BANKS_K = min(kv_t, 2)
    NH = (D + KW) // HD
    n_small = 2 + (2 if b_qkv is not None else 0)
    with ExitStack() as ctx:
        sb = lambda n, shape, dt=F32: ctx.enter_context(nc.sbuf_tensor(name + n, shape, dt))
        pb = lambda n, shape: ctx.enter_context(nc.psum_tensor(name + n, shape, F32))
        sem = phase_semaphores(nc, ctx, name)
        wq = sb("wq", [P, KD, ALL])
        wo = sb("wo", [P, KD, D])
        bq = sb("bq", [P, ALL]) if b_qkv is not None else None
        bo = sb("bo", [P, D]) if b_o is not None else None
        xb = sb("xb", [P, KD, SEQ])
        raw = sb("raw", [P, BT, ALL])
        cosd = sb("cosd", [P, D + KW])
        roped = sb("roped", [P, BT, D + KW])
        v = sb("v", [P, BT, VW])
        qT = sb("qT", [P, KD, SEQ])
        kT = sb("kT", [P, kv_t, HPT, SEQ])
        nm = sb("nm", [P, 2, 4])
        rows = sb("rows", [P, BT, HEADS])
        rec = sb("rec", [P, BT, HEADS])
        pr = sb("pr", [P, 2, 4, SEQ])
        pT = sb("pT", [P, 2, BT, 4, P])
        o = sb("o", [P, D])
        oT = sb("oT", [P, KD, P])
        ps_s = [pb(f"ps_s{i}", [P, 2, HALF]) for i in range(2)]
        ps_p = pb("ps_p", [P, 2, HALF])
        ps_o = pb("ps_o", [P, D])
        ps_x = pb("ps_x", [P, HALF])
        (w_loaded, xb_ready, piece_ready, piece_kept, v_ready, rotated, roped_ready, turned, qT_ready, k_dve, k_act,
         scores_ready, max_ready, probs_ready, pT_ready, pT_kept, pv_done, rec_ready, o_ready, oT_ready, oT_kept,
         out_ready, x_added, biased) = (
            sem(n) for n in ("w_loaded", "xb_ready", "piece_ready", "piece_kept", "v_ready", "rotated",
                             "roped_ready", "turned", "qT_ready", "k_dve", "k_act", "scores_ready", "max_ready",
                             "probs_ready", "pT_ready", "pT_kept", "pv_done", "rec_ready", "o_ready", "oT_ready",
                             "oT_kept", "out_ready", "x_added", "biased"))
        X0 = 1
        block = ctx.enter_context(nc.Block())
        ps_qT = ps_p[:, :, :].rearrange("p a (c s) -> p (a c) s", s=SEQ)
        ps_kT = ps_s[0][:, :, :].rearrange("p a (c s) -> p (a c) s", s=SEQ)

        def batches(eng, body):
            with eng.Fori(0, BATCH - 1) as b:
                body(b, False)
            body(BATCH - 1, True)

        def first(bn):
            return isinstance(bn, int) and bn == 0

        def n_keys(t):
            return t + 1 if causal else BT

        def scores_view(slot, t):
            kw = n_keys(t) * P
            return ps_s[slot][:, :, :].rearrange("p a n -> p (a n)")[:, 0:4 * kw].rearrange("p (h k) -> p h k", k=kw)

        @block.sync
        def _(sp):
            sp.dma_start(wq[:], w_qkv).then_inc(w_loaded, 16)
            sp.dma_start(wo[:], w_o).then_inc(w_loaded, 16)
            if bq is not None:
                sp.dma_start(bq[:], b_qkv.partition_broadcast(P)).then_inc(w_loaded, 16)
                sp.dma_start(bo[:], b_o.partition_broadcast(P)).then_inc(w_loaded, 16)

        @block.tensor
        def _(pe):
            def project(bn, i):
                t, at, width = pieces[i]
                if i == 0:
                    pe.wait_ge(xb_ready, bn + 1)
                    if not first(bn):
                        pe.wait_ge(x_added, X0 + 2 * (bn - 1))
                        pe.wait_ge(piece_kept, N_PIECES * bn)
                else:
                    pe.wait_ge(piece_kept, N_PIECES * bn + i)
                for k in range(KD):
                    ins = pe.matmul(ps_x[:, 0:width], xb[:, k, t * P:(t + 1) * P], wq[:, k, at:at + width],
                                    start=k == 0, stop=k == KD - 1)
                ins.then_inc(piece_ready, 1)

            def turn(bn):
                pe.wait_ge(roped_ready, 2 * bn + 2)
                if not first(bn):
                    pe.wait_ge(probs_ready, JOBS * bn)
                    pe.wait_ge(pT_kept, JOBS * bn)
                for count, dst, at in ((KD, ps_qT, 0), (kv_t, ps_kT, D)):
                    for t in range(BT):
                        for c in range(count):
                            ins = pe.transpose(dst[:, c, t * P:(t + 1) * P],
                                               roped[:, t, at + c * P:at + (c + 1) * P], core.ident)
                    ins.then_inc(turned, 1)

            def turn_sums(b, t, last):
                pe.wait_ge(o_ready, 2 * b + t + 1)
                pe.wait_ge(x_added, X0 + 2 * b + t)
                if t == 0:
                    pe.wait_ge(piece_kept, N_PIECES * (b + (1 if last else 2)))
                for c in range(KD):
                    ins = pe.transpose(ps_x[:, c * P:(c + 1) * P], o[:, c * P:(c + 1) * P], core.ident)
                ins.then_inc(oT_ready, 1)

            def project_sums(b, t):
                pe.wait_ge(oT_kept, 2 * b + t + 1)
                for k in range(KD):
                    ins = pe.matmul(ps_x[:], oT[:, k, :], wo[:, k, :], start=k == 0, stop=k == KD - 1)
                ins.then_inc(out_ready, 1)

            pe.wait_ge(w_loaded, 16 * n_small)
            for i in range(N_PIECES):
                project(0, i)
            turn(0)

            def batch(b, last):
                pe.wait_ge(qT_ready, b + 1)
                pe.wait_ge(k_dve, b + 1)
                if kv_t > BANKS_K:
                    pe.wait_ge(k_act, b + 1)

                def scores(n):
                    c, gq, t = jobs[n]
                    kc = c if kv_t > 1 else 0
                    if n >= 2:
                        pe.wait_ge(probs_ready, JOBS * b + (n - 1))
                    view = scores_view(n % 2, t)
                    q = qT[:, c, t * P:(t + 1) * P]
                    per = HALF // (n_keys(t) * P)
                    for h in range(0, 4, per):
                        if causal:
                            mask = core.tri4[:] if t == 0 else core.tri_right[:].rearrange("p a b c -> p a (b c)")
                            pe.matmul(view[:, h:h + per, :], core.identb[:], mask, start=True, stop=False)
                        ins = pe.matmul(view[:, h:h + per, :], q,
                                        kT[:, kc, 4 * gq + h:4 * gq + h + per, 0:n_keys(t) * P],
                                        start=not causal, stop=True)
                    ins.then_inc(scores_ready, 1)

                scores(0)
                scores(1)
                for n in range(JOBS):
                    c, gq, t = jobs[n]
                    pe.wait_ge(probs_ready, JOBS * b + (n + 1))
                    if n:
                        pe.wait_ge(pT_kept, JOBS * b + n)
                    for kt in range(n_keys(t)):
                        for h in range(4):
                            ins = pe.transpose(ps_p[:, kt, h * P:(h + 1) * P],
                                               pr[:, n % 2, h, kt * P:(kt + 1) * P], core.ident)
                    ins.then_inc(pT_ready, 1)
                    if n + 2 < JOBS:
                        scores(n + 2)
                    if not last and n in PIECE_AT:
                        project(b + 1, PIECE_AT[n])
                    if n == TURN_AT:
                        turn_sums(b, 0, last)
                    if n == PROJECT_AT:
                        project_sums(b, 0)
                    pe.wait_ge(pT_kept, JOBS * b + (n + 1))
                    if n == 0:
                        pe.wait_ge(v_ready, b + 1)
                    if n == PER_T:
                        pe.wait_ge(o_ready, 2 * b + 1)
                    for h in range(4):
                        g = 4 * gq + h
                        head = HPT * c + g
                        kv = head if kv_t > 1 else g
                        for kt in range(n_keys(t)):
                            ins = pe.matmul(ps_o[:, head * HD:(head + 1) * HD], pT[:, n % 2, kt, h, :],
                                            v[:, kt, kv * HD:(kv + 1) * HD], start=kt == 0, stop=kt == n_keys(t) - 1)
                    ins.then_inc(pv_done, 1)
                if not last:
                    turn(b + 1)
                turn_sums(b, 1, last)
                project_sums(b, 1)

            batches(pe, batch)

        @block.vector
        def _(dve):
            def keep_piece(bn, i):
                t, at, width = pieces[i]
                dve.wait_ge(piece_ready, N_PIECES * bn + i + 1)
                if i == 0 and not first(bn):
                    dve.wait_ge(v_ready, bn)
                dve.tensor_tensor(raw[:, t, at:at + width], ps_x[:, 0:width], bq[:, at:at + width],
                                  ALU.add).then_inc(piece_kept, 1)

            def mask_keys(bn):
                dve.wait_ge(turned, 2 * bn + 2)
                for g in range(HPT):
                    ins = dve.tensor_scalar(kT[:, 0:BANKS_K, g, :], ps_kT[:, 0:BANKS_K, :],
                                            core.consts[:, C_HM + g:C_HM + g + 1], None, ALU.mult)
                ins.then_inc(k_dve, 1)

            def normalise(b, t):
                dve.wait_ge(probs_ready, JOBS * b + PER_T * (t + 1))
                dve.reciprocal(rec[:, t, :], rows[:, t, :]).then_inc(rec_ready, 1)
                dve.wait_ge(rec_ready, 2 * b + t + 1)
                dve.wait_ge(pv_done, JOBS * b + PER_T * (t + 1))
                dve.tensor_tensor(o[:, :].rearrange("p (h d) -> p h d", d=HD),
                                  ps_o[:, :].rearrange("p (h d) -> p h d", d=HD),
                                  rec[:, t, :].unsqueeze(2).broadcast_to((P, HEADS, HD)),
                                  ALU.mult).then_inc(o_ready, 1)

            def add_to_residual(b, t):
                dve.wait_ge(out_ready, 2 * b + t + 1)
                xt = core.x[:, 2 * b + t, :]
                dve.tensor_tensor(xt, ps_x[:], xt, ALU.add).then_inc(x_added, 1)

            dve.wait_ge(w_loaded, 16 * n_small)
            if bq is not None:
                for i in range(N_PIECES):
                    keep_piece(0, i)
            mask_keys(0)
            if bo is not None:
                dve.wait_ge(biased, 1)

            def batch(b, last):
                def maximum(n):
                    t = jobs[n][2]
                    dve.wait_ge(scores_ready, JOBS * b + (n + 1))
                    dve.tensor_reduce(nm[:, n % 2, :], scores_view(n % 2, t), AX.X, ALU.max,
                                      negate=True).then_inc(max_ready, 1)

                maximum(0)
                maximum(1)
                for n in range(JOBS):
                    t = jobs[n][2]
                    if n == PER_T:
                        normalise(b, 0)
                    dve.wait_ge(pT_ready, JOBS * b + (n + 1))
                    if n >= 2:
                        dve.wait_ge(pv_done, JOBS * b + (n - 1))
                    kt = n_keys(t)
                    dve.tensor_copy(pT[:, n % 2, 0:kt].rearrange("p k h q -> p k (h q)"),
                                    ps_p[:, 0:kt, :]).then_inc(pT_kept, 1)
                    if n + 2 < JOBS:
                        maximum(n + 2)
                    if not last and bq is not None and n in PIECE_AT:
                        keep_piece(b + 1, PIECE_AT[n])
                    if n == PROJECT_AT:
                        add_to_residual(b, 0)
                normalise(b, 1)
                if not last:
                    mask_keys(b + 1)
                add_to_residual(b, 1)

            batches(dve, batch)

        @block.gpsimd
        def _(pool):
            pool.sem_inc(x_added, X0)
            pool.wait_ge(w_loaded, 16 * n_small)

            def prepare(bn):
                if not first(bn):
                    pool.wait_ge(piece_kept, N_PIECES * bn)
                tok = bass.ts(bn, SEQ)
                pool.tensor_tensor(xb[:], core.xh[:, :, tok], core.xl[:, :, tok], ALU.add).then_inc(xb_ready, 1)
                if first(bn) and bo is not None:
                    for t in range(NT):
                        ins = pool.tensor_tensor(core.x[:, t, :], core.x[:, t, :], bo[:], ALU.add)
                    ins.then_inc(biased, 1)
                for t in range(BT):
                    pool.wait_ge(piece_kept, N_PIECES * bn + N_PIECES // BT * (t + 1))
                    if t or not first(bn):
                        pool.wait_ge(roped_ready, 2 * bn + t)
                    c0, s0 = C_COS + t * HD, C_SIN + t * HD
                    cos = core.consts[:, c0:c0 + HD].unsqueeze(1).broadcast_to((P, NH, HD))
                    pool.tensor_tensor(cosd[:, :].rearrange("p (h d) -> p h d", d=HD),
                                       raw[:, t, 0:D + KW].rearrange("p (h d) -> p h d", d=HD), cos, ALU.mult)
                    r = raw[:, t, 0:D + KW].rearrange("p (h two d) -> p h two d", two=2, d=HD // 2)
                    out = roped[:, t, :].rearrange("p (h two d) -> p h two d", two=2, d=HD // 2)
                    for part in range(2):
                        lo = s0 + part * HD // 2
                        sin = core.consts[:, lo:lo + HD // 2].unsqueeze(1).broadcast_to((P, NH, HD // 2))
                        ins = pool.tensor_tensor(out[:, :, part, :], r[:, :, 1 - part, :], sin, ALU.mult)
                    ins.then_inc(rotated, 1)
                    pool.wait_ge(rotated, 2 * bn + t + 1)
                    pool.tensor_tensor(roped[:, t, :], roped[:, t, :], cosd[:], ALU.add).then_inc(roped_ready, 1)

            prepare(0)
            with pool.Fori(1, BATCH) as bn:
                prepare(bn)

        @block.scalar
        def _(act):
            def keep_piece(bn, i):
                t, at, width = pieces[i]
                act.wait_ge(piece_ready, N_PIECES * bn + i + 1)
                act.activation(raw[:, t, at:at + width], ps_x[:, 0:width], ACT.Copy).then_inc(piece_kept, 1)

            def keep_queries(bn):
                act.wait_ge(turned, 2 * bn + 1)
                act.activation(qT[:], ps_qT, ACT.Copy, scale=1.0 / float(HD) ** 0.5).then_inc(qT_ready, 1)

            def mask_keys_and_keep_values(bn):
                act.wait_ge(turned, 2 * bn + 2)
                act.activation(v[:], raw[:, :, D + KW:], ACT.Copy).then_inc(v_ready, 1)
                if kv_t > BANKS_K:
                    for g in range(HPT):
                        ins = act.activation(kT[:, BANKS_K:, g, :], ps_kT[:, BANKS_K:kv_t, :], ACT.Copy,
                                             scale=core.consts[:, C_HM + g:C_HM + g + 1])
                    ins.then_inc(k_act, 1)

            def keep_sums(b, t):
                act.wait_ge(oT_ready, 2 * b + t + 1)
                act.activation(oT[:], ps_x[:, :].rearrange("p (c q) -> p c q", q=P), ACT.Copy).then_inc(oT_kept, 1)

            if bq is None:
                for i in range(N_PIECES):
                    keep_piece(0, i)
            keep_queries(0)
            mask_keys_and_keep_values(0)

            def batch(b, last):
                for n in range(JOBS):
                    c, gq, t = jobs[n]
                    act.wait_ge(max_ready, JOBS * b + (n + 1))
                    if n >= 2:
                        act.wait_ge(pT_ready, JOBS * b + (n - 1))
                    for h in range(4):
                        head = HPT * c + 4 * gq + h
                        ins = act.activation(pr[:, n % 2, h, 0:n_keys(t) * P], scores_view(n % 2, t)[:, h, :],
                                             ACT.Exp, bias=nm[:, n % 2, h:h + 1],
                                             accum_out=rows[:, t, head:head + 1])
                    ins.then_inc(probs_ready, 1)
                    if not last and bq is None and n - 1 in PIECE_AT:
                        keep_piece(b + 1, PIECE_AT[n - 1])
                    if n - 1 == TURN_AT:
                        keep_sums(b, 0)
                if not last:
                    keep_queries(b + 1)
                keep_sums(b, 1)
                if not last:
                    mask_keys_and_keep_values(b + 1)

            batches(act, batch)


def dt_phase(nc, core, mem, dram):
    with ExitStack() as ctx:
        sb = lambda n, shape, dt=F32: ctx.enter_context(nc.sbuf_tensor("dt_" + n, shape, dt))
        sem = phase_semaphores(nc, ctx, "dt_")
        w = sb("w", [P, KD, MH])
        w_h, w_l = (sb(n, [P, KD, MH], F32R) for n in ("w_h", "w_l"))
        col = sb("col", [P, 3])
        z, e, dtT, dec = (sb(n, [P, TOK]) for n in ("z", "e", "dtT", "dec"))
        ps = ctx.enter_context(nc.psum_tensor("dt_ps", [P, 2, HALF], F32))
        ps_t = ctx.enter_context(nc.psum_tensor("dt_pst", [P, NT, MH], F32))
        loaded, proj, chain, a_exp, minus_abs, log_done, dt_done, decayed, turned = (
            sem(n) for n in ("loaded", "proj", "chain", "a_exp", "minus_abs", "log_done", "dt_done", "decayed",
                             "turned"))
        expd, w_high, w_low = (sem(n) for n in ("expd", "w_high", "w_low"))
        block = ctx.enter_context(nc.Block())

        @block.sync
        def _(sp):
            sp.dma_start(w[:], dram["m_wdt"]).then_inc(loaded, 16)
            sp.dma_start(col[:, 0:1], dram["m_dtb"]).then_inc(loaded, 16)
            sp.dma_start(col[:, 1:2], dram["m_alog"]).then_inc(loaded, 16)
            sp.dma_start(mem.cols[:], dram["m_cols"]).then_inc(loaded, 16)
            sp.wait_ge(loaded, 64)

        @block.tensor
        def _(pe):
            pe.wait_ge(w_low, 1)
            for half in range(2):
                tok = slice(half * HALF, (half + 1) * HALF)
                for k in range(KD):
                    ins = split_product(pe, ps[:, half, :], w_h[:, k, :], w_l[:, k, :], core.xh[:, k, tok],
                                        core.xl[:, k, tok], k == 0, k == KD - 1)
            ins.then_inc(proj, 1)
            pe.wait_ge(dt_done, 1)
            for t in range(NT):
                ins = pe.transpose(ps_t[:, t, :], dtT[:, t * P:(t + 1) * P], core.ident)
            ins.then_inc(turned, 1)

        @block.scalar
        def _(act):
            act.wait_ge(loaded, 64)
            act.activation(w_h[:], w[:], ACT.Copy).then_inc(w_high, 1)
            act.activation(col[:, 2:3], col[:, 1:2], ACT.Exp).then_inc(a_exp, 1)
            act.wait_ge(minus_abs, 1)
            act.activation(e[:], e[:], ACT.Exp).then_inc(expd, 1)
            act.wait_ge(expd, 1)
            act.activation(e[:], e[:], ACT.Ln, bias=1.0).then_inc(log_done, 1)
            act.wait_ge(dt_done, 1)
            act.activation(dec[:], dtT[:], ACT.Exp, scale=col[:, 2:3]).then_inc(decayed, 1)

        @block.vector
        def _(dve):
            n_chain = [0]

            def link(ins):
                n_chain[0] += 1
                ins.then_inc(chain, 1)
                dve.wait_ge(chain, n_chain[0])

            dve.wait_ge(w_high, 1)
            dve.tensor_tensor(w_l[:], w[:], w_h[:], ALU.subtract).then_inc(w_low, 1)
            dve.wait_ge(a_exp, 1)
            link(dve.tensor_scalar(col[:, 2:3], col[:, 2:3], -1.0, None, ALU.mult))
            dve.wait_ge(proj, 1)
            link(dve.tensor_scalar(z[:], ps[:, :, :].rearrange("p a n -> p (a n)"), col[:, 0:1], None, ALU.add))
            dve.scalar_tensor_tensor(out=e[:], in0=z[:], scalar=-1.0, in1=z[:], op0=ALU.mult,
                                     op1=ALU.min).then_inc(minus_abs, 1)
            dve.wait_ge(log_done, 1)
            dve.scalar_tensor_tensor(out=dtT[:], in0=z[:], scalar=0.0, in1=e[:], op0=ALU.max,
                                     op1=ALU.add).then_inc(dt_done, 1)
            dve.wait_ge(decayed, 1)
            link(dve.memset(dec[:, :].rearrange("p (b s) -> p b s", b=BATCH)[:, :, 0:1], 0.0))
            link(dve.tensor_copy(mem.dec[:, 0, :], dec[:]))
            link(dve.tensor_tensor(dec[:], dec[:], mem.dec[:, 0, :], ALU.subtract))
            link(dve.tensor_copy(mem.dec[:, 1, :], dec[:]))
            link(dve.tensor_tensor(dec[:], dec[:], mem.dec[:, 1, :], ALU.subtract))
            dve.tensor_copy(mem.dec[:, 2, :], dec[:])
            link(dve.memset(mem.start[:], 0.0))
            for b in range(2):
                dve.tensor_copy(mem.start[:, b * SEQ:b * SEQ + P], core.ident)
            dve.memset(mem.ones[:], 1.0)
            dve.wait_ge(turned, 1)
            dve.tensor_copy(mem.dt[:], ps_t[:])


def mix_phase(nc, core, mem, dram):
    with ExitStack() as ctx:
        sb = lambda n, shape, dt=F32: ctx.enter_context(nc.sbuf_tensor("mx_" + n, shape, dt))
        pb = lambda n, shape: ctx.enter_context(nc.psum_tensor("mx_" + n, shape, F32))
        sem = phase_semaphores(nc, ctx, "mx_")
        w = sb("w", [P, 2, 2, KD, P])
        w_h, w_l = (sb(n, [P, 2, 2, KD, P], F32R) for n in ("w_h", "w_l"))
        wout = sb("wout", [P, GM, D])
        cols = sb("cols", [P, NCOL])
        sel = sb("sel", [P, GH, P], BF16)
        cacc = sb("cacc", [P, 2, HALF])
        bT, cT = sb("bT", [P, TOK]), sb("cT", [P, TOK])
        G = sb("G", [P, BATCH, SEQ + P])
        hidT = sb("hidT", [P, 2, HALF])
        gateT = sb("gateT", [P, 2, HALF])
        hid = sb("hid", [P, 2, 4, P])
        L = sb("L", [P, 2, 2 * SEQ + 2 * P])
        M = sb("M", [P, 2, 2, 2 * SEQ + 2 * P])
        y2 = sb("y2", [P, HALF])
        yg = sb("yg", [P, 2, HALF])
        yw = sb("yw", [P, GM, TOK])
        sq = sb("sq", [P, 2, HALF])
        sqsum = sb("sqsum", [P, TOK])
        rms = sb("rms", [P, 3, NT])
        ps_hid = [pb(f"ps_hid{i}", [P, HALF]) for i in range(2)]
        ps_gate, ps_turn, ps_y, ps_misc = (pb(n, [P, HALF]) for n in ("ps_gate", "ps_turn", "ps_y", "ps_misc"))
        ps_dec = [pb(f"ps_dec{i}", [P, HALF]) for i in range(2)]
        w_loaded = [sem(f"w_loaded{i}") for i in range(2)]
        AHEAD = {"conv_done": 2, "scanned": 2, "m_ready": 2, "gate_kept": 1, "gate_ready": 3, "values_kept": 1,
                 "y2_done": 2, "yg_done": 2, "yw_done": 2, "sq_added": 2, "out_added": 2, "out_ready": 1,
                 "g_ready": 4, "hidT_ready": 2, "sq_ready": 2, "w_low": 1}
        plain = ("w_high wout_loaded cols_ready hid_ready tap_done conv_chain g_kept turned dec_ready "
                 "y_ready sum_ready var_ready std_ready chain").split()
        s = {n: sem(n) for n in [*plain, *AHEAD]}
        block = ctx.enter_context(nc.Block())
        CONVS = STEPS + 4
        SPLITS = GM + 1
        T1 = TAPS + 1

        def done(name, count):
            return AHEAD.get(name, 0) + count

        def col(i):
            return cols[:, i:i + 1]

        def column(i):
            return cols[:, bass.ds(i, 1)]

        def group_steps(eng, body):
            for q in range(4):
                body(q // 2, q, q)
            with eng.Fori(1, STEPS // 4 - 1) as i:
                for q in range(4):
                    body(2 * i + q // 2, 4 * i + q, q)
            for q in range(4):
                body(GM - 2 + q // 2, STEPS - 4 + q, q)

        def is_first(step):
            return isinstance(step, int) and step == 0

        def is_last(step):
            return isinstance(step, int) and step == STEPS - 1

        @block.sync
        def _(sp):
            with sp.Fori(0, MG) as g:
                sp.wait_ge(s["w_low"], done("w_low", SPLITS * g))
                sp.dma_start(w[:, 1], dram["m_wbc"][g]).then_inc(w_loaded[1], 16)
                with sp.Fori(0, GM // 2) as i:
                    for j in range(2):
                        sp.wait_ge(s["w_low"], done("w_low", SPLITS * g + 2 * i + j))
                        sp.dma_start(w[:, j], dram["m_w"][g, 2 * i + j]).then_inc(w_loaded[j], 16)
                sp.wait_ge(s["out_ready"], done("out_ready", NT * g))
                sp.dma_start(wout[:], dram["m_wout"][g]).then_inc(s["wout_loaded"], 16)

        @block.tensor
        def _(pe):
            with pe.Fori(0, MG) as g:
                def project(ps, slot, which, half):
                    tok = slice(half * HALF, (half + 1) * HALF)
                    for k in range(KD):
                        ins = split_product(pe, ps[:], w_h[:, slot, which, k, :], w_l[:, slot, which, k, :],
                                            core.xh[:, k, tok], core.xl[:, k, tok], k == 0, k == KD - 1)
                    return ins

                pe.wait_ge(s["w_low"], done("w_low", SPLITS * g + 1))
                for n in range(4):
                    pe.wait_ge(s["conv_done"], done("conv_done", CONVS * g + n - 1))
                    project(ps_hid[n % 2], 1, n // 2, n % 2).then_inc(s["hid_ready"], 1)

                def values_and_gate(tile, step, q):
                    half, slot = q % 2, q // 2
                    if half == 0:
                        pe.wait_ge(s["w_low"], done("w_low", SPLITS * g + tile + 2))
                    pe.wait_ge(s["conv_done"], done("conv_done", CONVS * g + 4 + step - 1))
                    project(ps_hid[half], slot, 0, half).then_inc(s["hid_ready"], 1)
                    pe.wait_ge(s["gate_kept"], done("gate_kept", STEPS * g + step))
                    project(ps_gate, slot, 1, half).then_inc(s["gate_ready"], 1)

                def decays(tile, step, q):
                    half = q % 2
                    for hh in range(2):
                        pe.wait_ge(s["scanned"], done("scanned", 2 * (STEPS * g + step - 1) + hh + 1))
                        for part in range(3):
                            ins = pe.matmul(ps_dec[hh][:], sel[:, 2 * tile + hh, :],
                                            mem.dec[:, part, half * HALF:(half + 1) * HALF],
                                            start=part == 0, stop=part == 2)
                        ins.then_inc(s["dec_ready"], 1)

                def turn_values(step, q):
                    half = q % 2
                    pe.wait_ge(s["hidT_ready"], done("hidT_ready", CONVS * g + 4 + step + 1))
                    pe.wait_ge(s["values_kept"], done("values_kept", STEPS * g + step))
                    for t in range(4):
                        ins = pe.transpose(ps_turn[:, t * P:(t + 1) * P], hidT[:, half, t * P:(t + 1) * P],
                                           core.ident)
                    ins.then_inc(s["turned"], 1)

                def sums(step, q):
                    half = q % 2
                    pe.wait_ge(s["m_ready"], done("m_ready", 2 * (STEPS * g + step) + 2))
                    pe.wait_ge(s["values_kept"], done("values_kept", STEPS * g + step + 1))
                    pe.wait_ge(s["y2_done"], done("y2_done", STEPS * g + step))
                    for hh in range(2):
                        rows = slice(hh * MP, (hh + 1) * MP)
                        for b in range(2):
                            pe.matmul(ps_y[rows, b * SEQ:(b + 1) * SEQ], hid[:, half, 2 * b, rows],
                                      M[:, half, hh, b * SEQ:(b + 1) * SEQ], start=True, stop=False)
                            ins = pe.matmul(ps_y[rows, b * SEQ + P:(b + 1) * SEQ], hid[:, half, 2 * b + 1, rows],
                                            M[:, half, hh, 2 * SEQ + b * P:2 * SEQ + (b + 1) * P],
                                            start=False, stop=True)
                    ins.then_inc(s["y_ready"], 1)

                values_and_gate(0, 0, 0)
                pe.wait_ge(s["cols_ready"], g + 1)
                decays(0, 0, 0)
                pe.wait_ge(s["hidT_ready"], done("hidT_ready", CONVS * g + 4))
                pe.wait_ge(s["out_added"], done("out_added", NT * g))
                for b in range(BATCH):
                    if b >= 2:
                        pe.wait_ge(s["g_kept"], BATCH * g + b - 1)
                    ps = (ps_misc, ps_turn)[b % 2]
                    pe.matmul(ps[:, 0:SEQ], bT[:, b * SEQ:b * SEQ + P], cT[:, b * SEQ:(b + 1) * SEQ],
                              start=True, stop=True)
                    pe.matmul(ps[:, SEQ:SEQ + P], bT[:, b * SEQ + P:(b + 1) * SEQ],
                              cT[:, b * SEQ + P:(b + 1) * SEQ], start=True, stop=True).then_inc(s["g_ready"], 1)
                pe.wait_ge(s["g_kept"], BATCH * (g + 1))

                def step_of(tile, step, q):
                    if not is_first(step):
                        sums(step - 1, (q + 3) % 4)
                    turn_values(step, q)
                    if not is_last(step):
                        nxt = (tile if q % 2 == 0 else tile + 1, step + 1, (q + 1) % 4)
                        values_and_gate(*nxt)
                        decays(*nxt)

                group_steps(pe, step_of)
                sums(STEPS - 1, 3)

                pe.wait_ge(s["sq_added"], done("sq_added", STEPS * (g + 1)))
                pe.wait_ge(s["y2_done"], done("y2_done", STEPS * (g + 1)))
                for t in range(NT):
                    ins = pe.matmul(ps_y[:, t:t + 1], sqsum[:, t * P:(t + 1) * P], mem.ones[:], start=True, stop=True)
                ins.then_inc(s["sum_ready"], 1)
                pe.wait_ge(s["wout_loaded"], 16 * (g + 1))
                pe.wait_ge(s["yw_done"], done("yw_done", STEPS * (g + 1)))
                for t in range(NT):
                    pe.wait_ge(s["out_added"], done("out_added", NT * g + t - 1))
                    for m in range(GM):
                        ins = pe.matmul((ps_misc, ps_turn)[t % 2][:], yw[:, m, t * P:(t + 1) * P], wout[:, m, :],
                                        start=m == 0, stop=m == GM - 1)
                    ins.then_inc(s["out_ready"], 1)

        @block.scalar
        def _(act):
            with act.Fori(0, MG) as g:
                def round_weights(slot, loads, gates):
                    act.wait_ge(w_loaded[slot], 16 * loads)
                    act.wait_ge(s["gate_ready"], done("gate_ready", STEPS * g + gates))
                    act.activation(w_h[:, slot], w[:, slot], ACT.Copy).then_inc(s["w_high"], 1)

                round_weights(1, (GM // 2 + 1) * g + 1, 0)
                round_weights(0, (GM // 2) * g + 1, -2)
                act.wait_ge(s["cols_ready"], g + 1)

                def first_tap(tile, unit, half):
                    act.wait_ge(s["hid_ready"], CONVS * g + unit + 1)
                    act.wait_ge(s["hidT_ready"], done("hidT_ready", CONVS * g + unit - 1))
                    act.activation(cacc[:, half, :], ps_hid[half][:], ACT.Identity, scale=col(T1 * tile + TAPS - 1),
                                   bias=col(T1 * tile + TAPS)).then_inc(s["tap_done"], 1)

                def silu_of_conv(out, unit, half):
                    act.wait_ge(s["conv_done"], done("conv_done", CONVS * g + unit + 1))
                    act.activation(out, cacc[:, half, :], ACT.Silu).then_inc(s["hidT_ready"], 1)

                for n in range(4):
                    first_tap(GM + n // 2, n, n % 2)
                    if n:
                        m = n - 1
                        silu_of_conv((bT, cT)[m // 2][:, (m % 2) * HALF:(m % 2 + 1) * HALF], m, m % 2)
                silu_of_conv(cT[:, HALF:], 3, 1)

                def weigh_and_square(tile, step, q):
                    half = q % 2
                    act.wait_ge(s["yg_done"], done("yg_done", STEPS * g + step + 1))
                    act.activation(yw[:, tile, half * HALF:(half + 1) * HALF], yg[:, half, :], ACT.Copy,
                                   scale=col(T1 * (GM + 2) + GM + tile)).then_inc(s["yw_done"], 1)
                    act.wait_ge(s["sq_added"], done("sq_added", STEPS * g + step - 1))
                    act.activation(sq[:, half, :], yg[:, half, :], ACT.Square).then_inc(s["sq_ready"], 1)

                def step_of(tile, step, q):
                    half = q % 2
                    first_tap(tile, 4 + step, half)
                    if is_first(step):
                        for b in range(BATCH):
                            act.wait_ge(s["g_ready"], done("g_ready", BATCH * g + b + 1))
                            act.activation(G[:, b, :], (ps_misc, ps_turn)[b % 2][:, 0:SEQ + P],
                                           ACT.Copy).then_inc(s["g_kept"], 1)
                    act.wait_ge(s["gate_ready"], done("gate_ready", STEPS * g + step + 1))
                    act.wait_ge(s["yg_done"], done("yg_done", STEPS * g + step - 1))
                    act.activation(gateT[:, half, :], ps_gate[:], ACT.Silu).then_inc(s["gate_kept"], 1)
                    silu_of_conv(hidT[:, half, :], 4 + step, half)
                    if not is_first(step):
                        weigh_and_square(tile if q % 2 else tile - 1, step - 1, (q + 3) % 4)

                for step in range(STEPS):
                    nxt = step // 2 + 1
                    if step % 2 == 0 and nxt < GM:
                        round_weights(nxt % 2, (GM // 2 + nxt % 2) * g + nxt // 2 + 1 + nxt % 2, 2 * (nxt - 1))
                    step_of(step // 2, step, step % 4)
                weigh_and_square(GM - 1, STEPS - 1, 3)
                act.wait_ge(s["var_ready"], g + 1)
                act.activation(rms[:, 1, :], rms[:, 0, :], ACT.Sqrt).then_inc(s["std_ready"], 1)

        @block.gpsimd
        def _(pool):
            for name, count in AHEAD.items():
                pool.sem_inc(s[name], count)
            with pool.Fori(0, MG) as g:
                def rest_of_weights(slot, index):
                    pool.wait_ge(s["w_high"], SPLITS * g + index + 1)
                    pool.tensor_tensor(w_l[:, slot], w[:, slot], w_h[:, slot], ALU.subtract).then_inc(s["w_low"], 1)

                rest_of_weights(1, 0)
                rest_of_weights(0, 1)
                pool.wait_ge(s["g_kept"], BATCH * (g + 1))
                pool.wait_ge(s["cols_ready"], g + 1)

                def add_squares(step, q):
                    half = q % 2
                    total = sqsum[:, half * HALF:(half + 1) * HALF]
                    pool.wait_ge(s["sq_ready"], done("sq_ready", STEPS * g + step + 1))
                    pool.wait_ge(s["sq_added"], done("sq_added", STEPS * g + step - 1))
                    pool.tensor_tensor(total, total, sq[:, half, :], ALU.add).then_inc(s["sq_added"], 1)

                def step_of(tile, step, q):
                    half = q % 2
                    if half == 0 and not (isinstance(step, int) and step == STEPS - 2):
                        rest_of_weights(1 - q // 2, tile + 2)
                    for hh in range(2):
                        pool.wait_ge(s["scanned"], done("scanned", 2 * (STEPS * g + step) + hh + 1))
                        for lo, n, g0 in ((0, SEQ, 0), (2 * SEQ, P, SEQ)):
                            ins = pool.tensor_tensor(
                                M[:, half, hh, lo:lo + 2 * n].rearrange("p (b i) -> p b i", b=2),
                                L[:, hh, lo:lo + 2 * n].rearrange("p (b i) -> p b i", b=2),
                                G[:, 2 * half:2 * half + 2, g0:g0 + n], ALU.mult)
                        ins.then_inc(s["m_ready"], 1)
                    if not is_first(step):
                        add_squares(step - 1, (q + 3) % 4)

                group_steps(pool, step_of)
                add_squares(STEPS - 1, 3)

        @block.vector
        def _(dve):
            with dve.Fori(0, MG) as g:
                dve.tensor_copy(cols[:], mem.cols[:, g, :])
                dve.memset(sqsum[:], 0.0)
                dve.tensor_copy(sel[:], core.identb[:, bass.ts(g, GH)].unsqueeze(2).broadcast_to(
                    (P, GH, P))).then_inc(s["cols_ready"], 1)
                dve.wait_ge(s["cols_ready"], g + 1)

                def conv(tile, unit, half):
                    pick = col if isinstance(tile, int) else column
                    acc = cacc[:, half, :].rearrange("p (b s) -> p b s", b=2)
                    src = ps_hid[half][:, :].rearrange("p (b s) -> p b s", b=2)
                    dve.wait_ge(s["tap_done"], CONVS * g + unit + 1)
                    for back in range(1, TAPS):
                        if back > 1:
                            dve.wait_ge(s["conv_chain"], 2 * (CONVS * g + unit) + back - 1)
                        ins = dve.scalar_tensor_tensor(
                            out=acc[:, :, back:], in0=src[:, :, 0:SEQ - back], scalar=pick(T1 * tile + TAPS - 1 - back),
                            in1=acc[:, :, back:], op0=ALU.mult, op1=ALU.add)
                        ins.then_inc(s["conv_chain" if back < TAPS - 1 else "conv_done"], 1)

                for n in range(4):
                    conv(GM + n // 2, n, n % 2)

                def scans(step, q):
                    for hh in range(2):
                        dve.wait_ge(s["dec_ready"], 2 * (STEPS * g + step) + hh + 1)
                        dve.wait_ge(s["m_ready"], done("m_ready", 2 * (STEPS * g + step - 1) + hh + 1))
                        dve.tensor_tensor_scan(L[:, hh, 0:2 * SEQ], ps_dec[hh][:], mem.start[:], 0.0,
                                               ALU.mult, ALU.add)
                        for b in range(2):
                            ins = dve.tensor_tensor_scan(L[:, hh, 2 * SEQ + b * P:2 * SEQ + (b + 1) * P],
                                                         ps_dec[hh][:, b * SEQ + P:(b + 1) * SEQ], core.ident, 0.0,
                                                         ALU.mult, ALU.add)
                        ins.then_inc(s["scanned"], 1)

                def gated(tile, step, q):
                    half = q % 2
                    pick = col if isinstance(tile, int) else column
                    dve.wait_ge(s["y_ready"], STEPS * g + step + 1)
                    dve.wait_ge(s["yg_done"], done("yg_done", STEPS * g + step))
                    dve.scalar_tensor_tensor(out=y2[:], in0=hidT[:, half, :], scalar=pick(T1 * (GM + 2) + tile),
                                             in1=ps_y[:], op0=ALU.mult, op1=ALU.add).then_inc(s["y2_done"], 1)
                    dve.wait_ge(s["y2_done"], done("y2_done", STEPS * g + step + 1))
                    dve.wait_ge(s["gate_kept"], done("gate_kept", STEPS * g + step + 1))
                    dve.wait_ge(s["sq_ready"], done("sq_ready", STEPS * g + step - 1))
                    dve.tensor_tensor(yg[:, half, :], y2[:], gateT[:, half, :], ALU.mult).then_inc(s["yg_done"], 1)

                def keep_values(tile, step, q):
                    half = q % 2
                    dve.wait_ge(s["turned"], STEPS * g + step + 1)
                    dts = mem.dt[:, 4 * half:4 * half + 4, bass.ds(GH * g + 2 * tile, 2)]
                    dve.tensor_tensor(hid[:, half].rearrange("p t (h d) -> p t h d", h=2),
                                      ps_turn[:, :].rearrange("p (t h d) -> p t h d", t=4, h=2),
                                      dts.unsqueeze(3).broadcast_to((P, 4, 2, MP)), ALU.mult).then_inc(
                                          s["values_kept"], 1)

                def step_of(tile, step, q):
                    conv(tile, 4 + step, q % 2)
                    scans(step, q)
                    if not is_first(step):
                        gated(tile if q % 2 else tile - 1, step - 1, (q + 3) % 4)
                    keep_values(tile, step, q)

                group_steps(dve, step_of)
                gated(GM - 1, STEPS - 1, 3)
                dve.wait_ge(s["sum_ready"], g + 1)
                dve.tensor_scalar(rms[:, 0, :], ps_y[:, 0:NT], 1.0 / (GM * P), EPS, ALU.mult,
                                  ALU.add).then_inc(s["var_ready"], 1)
                dve.wait_ge(s["std_ready"], g + 1)
                dve.reciprocal(rms[:, 2, :], rms[:, 1, :]).then_inc(s["chain"], 1)
                dve.wait_ge(s["chain"], g + 1)
                for t in range(NT):
                    dve.wait_ge(s["out_ready"], done("out_ready", NT * g + t + 1))
                    xt = core.x[:, t, :]
                    dve.scalar_tensor_tensor(out=xt, in0=(ps_misc, ps_turn)[t % 2][:], scalar=rms[:, 2, t:t + 1],
                                             in1=xt, op0=ALU.mult, op1=ALU.add).then_inc(s["out_added"], 1)


class MixerArrays:

    def __init__(self, nc, ctx):
        sb = lambda n, shape, dt=F32: ctx.enter_context(nc.sbuf_tensor("m_" + n, shape, dt))
        self.cols = sb("cols", [P, MG, NCOL])
        self.dec = sb("dec", [P, 3, TOK], BF16)
        self.dt = sb("dt", [P, NT, MH])
        self.start = sb("start", [P, 2 * SEQ])
        self.ones = sb("ones", [P, 1])


def mamba_phase(nc, core, dram):
    with ExitStack() as ctx:
        mem = MixerArrays(nc, ctx)
        dt_phase(nc, core, mem, dram)
        mix_phase(nc, core, mem, dram)


def program(nc, dram, out, parts=None):
    with ExitStack() as ctx:
        core = Core(nc, ctx)
        load_phase(nc, core, dram["x"], dram["consts"])
        for part in parts or ("attn0", "ffn0", "mamba", "ffn0", "across", "ffn1", "attn1", "ffn1"):
            if part == "attn0":
                norm_phase(nc, core, "na0")
                attention_phase(nc, core, "a0", dram["a0_w"], dram["a0_wo"], KV_HEADS, True,
                                dram["a0_b"], dram["a0_bo"])
            elif part == "attn1":
                norm_phase(nc, core, "na1")
                attention_phase(nc, core, "a1", dram["a1_w"], dram["a1_wo"], HEADS, False)
            elif part == "ffn0":
                norm_phase(nc, core, f"nf{core.ln_runs}")
                ffn_phase(nc, core, f"f{core.ln_runs}", dram["f0_gu"], dram["f0_down"])
            elif part == "ffn1":
                norm_phase(nc, core, f"nf{core.ln_runs}")
                quant = {k: dram["f1_" + k] for k in ("a", "da", "b", "db", "s_gu", "s_d")}
                quant_ffn_phase(nc, core, f"f{core.ln_runs}", dram["f1_gu"], dram["f1_down"], quant)
            elif part == "across":
                with nc.sbuf_tensor("xT", [P, KD, TOK], F32) as xT:
                    norm_phase(nc, core, "nab", whole=xT)
                    across_batch_phase(nc, core, xT)
            elif part == "mamba":
                norm_phase(nc, core, "nm", add=True, rms_col=dram["m_norm"])
                mamba_phase(nc, core, dram)
        store_phase(nc, core, out)


def rope_tables():
    inv = (1.0 / np.float32(10000.0) ** (np.arange(0, HD, 2, dtype=np.float32) / np.float32(HD))).astype(np.float32)
    ang = np.arange(SEQ, dtype=np.float32)[:, None] * inv[None, :]
    cos, sin = np.cos(ang).astype(np.float32), np.sin(ang).astype(np.float32)
    return np.concatenate([cos, cos], 1), np.concatenate([-sin, sin], 1)


def constants():
    c = np.zeros((P, NCONST), np.float32)
    c[:, C_ID:C_ID + P] = np.eye(P, dtype=np.float32)
    c[:, C_HM:C_HM + HPT] = np.arange(P)[:, None] // HD == np.arange(HPT)[None, :]
    cos, sin = rope_tables()
    c[:, C_COS:C_COS + BT * HD] = cos.reshape(BT, P, HD).transpose(1, 0, 2).reshape(P, BT * HD)
    c[:, C_SIN:C_SIN + BT * HD] = sin.reshape(BT, P, HD).transpose(1, 0, 2).reshape(P, BT * HD)
    c[:, C_TRI:C_TRI + P] = np.where(np.arange(P)[None, :] > np.arange(P)[:, None], MASKED, 0.0)
    return c


def k_major(w):
    return np.ascontiguousarray(w.T.reshape(w.shape[1] // P, P, w.shape[0]).transpose(1, 0, 2))


def pad_to(a, n, axis):
    shape = list(a.shape)
    shape[axis] = n - shape[axis]
    return np.concatenate([a, np.zeros(shape, a.dtype)], axis)


def ffn_tiles(gate, up, down):
    g, u = (pad_to(w, F_PAD, 0).reshape(FT, P, KD, P).transpose(0, 3, 2, 1) for w in (gate, up))
    return (np.ascontiguousarray(np.stack([g, u], 2)),
            np.ascontiguousarray(pad_to(down, F_PAD, 1).T.reshape(FT, P, D)))


def layout(i):
    a = {k: np.asarray(v) for k, v in i.items()}
    d = {"x": a["L0_attn_a_x"].reshape(TOK, D), "consts": constants()}
    w, b = a["L0_attn_a_w_qkv"], a["L0_attn_a_b_qkv"]
    halves = np.concatenate([np.arange(0, HD, 2), np.arange(1, HD, 2)])
    group = HEADS // KV_HEADS
    q_rows = (np.arange(D).reshape(KV_HEADS, group, HD).transpose(1, 0, 2)[:, :, halves]).reshape(-1)
    k_rows = D + np.arange(KV_HEADS * HD).reshape(KV_HEADS, HD)[:, halves].reshape(-1)
    v_rows = D + KV_HEADS * HD + np.arange(KV_HEADS * HD)
    rows = np.concatenate([q_rows, k_rows, v_rows])
    d["a0_w"] = k_major(w[rows])
    d["a0_b"] = b[rows]
    o_cols = np.arange(D).reshape(KV_HEADS, group, HD).transpose(1, 0, 2).reshape(-1)
    d["a0_wo"] = k_major(a["L0_attn_a_w_o"][:, o_cols])
    d["a0_bo"] = a["L0_attn_a_b_o"]
    d["a1_w"] = k_major(np.concatenate([a["L1_attn_b_" + n] for n in ("Wq", "Wk", "Wv")], 0))
    d["a1_wo"] = k_major(a["L1_attn_b_Wo"])
    d["f0_gu"], d["f0_down"] = ffn_tiles(a["L0_ffn_W_gate"], a["L0_ffn_W_up"], a["L0_ffn_W_down"])
    q = {k[7:]: v for k, v in a.items() if k.startswith("L1_ffn_")}
    d["f1_gu"], d["f1_down"] = ffn_tiles(q["gate_q"], q["up_q"], q["down_q"])
    d["f1_a"] = np.ascontiguousarray(
        np.stack([q[n].reshape(KD, P, RANK).transpose(1, 0, 2) for n in ("gate_A", "up_A")], 1))
    d["f1_da"] = np.ascontiguousarray(pad_to(q["down_A"], F_PAD, 0).reshape(FT, P, RANK).transpose(1, 0, 2))
    d["f1_b"] = np.ascontiguousarray(np.stack([pad_to(q[n], F_PAD, 1) for n in ("gate_B", "up_B")], 1))
    d["f1_db"] = q["down_B"]
    d["f1_s_gu"] = np.stack([pad_to(q[n], F_PAD, 0).reshape(FT, P).T for n in ("gate_scale", "up_scale")], 1)
    d["f1_s_d"] = q["down_scale"]
    w = a["L0_attn_b_in_proj_w"]
    gate = w[:D_INNER].reshape(MG, GM, P, KD, P)
    hid = w[D_INNER:2 * D_INNER].reshape(MG, GM, P, KD, P)
    d["m_w"] = np.ascontiguousarray(np.stack([hid, gate], 2).transpose(0, 1, 5, 2, 4, 3))
    bc = w[2 * D_INNER:2 * D_INNER + 2 * MG * MN].reshape(2, MG, P, KD, P)
    d["m_wbc"] = np.ascontiguousarray(bc.transpose(1, 4, 0, 3, 2))
    d["m_wdt"] = k_major(w[2 * D_INNER + 2 * MG * MN:])
    d["m_wout"] = np.ascontiguousarray(a["L0_attn_b_out_proj_w"].T.reshape(MG, GM, P, D).transpose(0, 2, 1, 3))
    taps = np.concatenate([a["L0_attn_b_conv_w"], a["L0_attn_b_conv_b"][:, None]], 1)
    t_hid = taps[:D_INNER].reshape(MG, GM, P, TAPS + 1)
    t_bc = taps[D_INNER:].reshape(2, MG, P, TAPS + 1).transpose(1, 0, 2, 3)
    cols = np.concatenate([t_hid, t_bc], 1).transpose(2, 0, 1, 3).reshape(P, MG, -1)
    per_feature = lambda v: v.reshape(MG, GM, P).transpose(2, 0, 1)
    dp = per_feature(np.repeat(a["L0_attn_b_Dp"], MP))
    d["m_cols"] = np.ascontiguousarray(np.concatenate([cols, dp, per_feature(a["L0_attn_b_gnorm_w"])], 2))
    d["m_dtb"] = a["L0_attn_b_dt_bias"][:, None]
    d["m_alog"] = a["L0_attn_b_A_log"][:, None]
    d["m_norm"] = np.ascontiguousarray(a["L0_attn_b_norm_w"].reshape(KD, P).T)
    return {k: np.ascontiguousarray(v) for k, v in d.items()}


def kernel(**inputs):
    import concourse.bacc as _bacc
    from concourse.bass_utils import run_bass_kernel_spmd as _run

    nc = _bacc.Bacc("TRN2", target_bir_lowering=False, num_devices=1)
    arrays = layout(inputs)
    dram = {k: nc.dram_tensor(f"in_{k}", v.shape, mybir.dt.from_np(v.dtype), kind="ExternalInput").ap()
            for k, v in arrays.items()}
    out = nc.dram_tensor("out_x", (TOK, D), F32, kind="ExternalOutput").ap()
    program(nc, dram, out)
    r = _run(nc, [{f"in_{k}": v for k, v in arrays.items()}], core_ids=[0])
    return r.results[0]["out_x"].reshape(BATCH, SEQ, D)
```

```python
from contextlib import ExitStack

import numpy as np

import concourse.bass as bass
from concourse import mybir

F32 = mybir.dt.float32
F32R = mybir.dt.float32r
BF16 = mybir.dt.bfloat16
I32 = mybir.dt.int32
ALU = mybir.AluOpType
ACT = mybir.ActivationFunctionType
AX = mybir.AxisListType

P = 128
BATCH, SEQ, D = 4, 256, 512
TOK = BATCH * SEQ
NT = TOK // P
KD = D // P
BT = SEQ // P
HALF = 512
EPS = 1e-5

HEADS, KV_HEADS, HD = 32, 8, 16
HPT = P // HD
F_FF = 1376
FT = -(-F_FF // P)
F_PAD = FT * P
RANK = 32
Q_ZERO, Q_STEP, LR_SCALE = 7.5, 0.005, 0.02

MH, MP, MG, MN, TAPS = 128, 64, 8, 128, 4
D_INNER = MH * MP
GF = D_INNER // MG
GM = GF // P
GH = MH // MG
STEPS = 2 * GM
NCOL = (GM + 2) * (TAPS + 1) + 2 * GM
MASKED = -1e20

C_ID, C_HM, C_COS, C_SIN, C_TRI = 0, P, P + HPT, P + HPT + BT * HD, P + HPT + 2 * BT * HD
NCONST = C_TRI + P


class Core:

    def __init__(self, nc, ctx):
        self.nc = nc
        sb = lambda name, shape, dt=F32: ctx.enter_context(nc.sbuf_tensor(name, shape, dt))
        self.x = sb("x_res", [P, NT, D])
        self.xh = sb("xh", [P, KD, TOK], F32R)
        self.xl = sb("xl", [P, KD, TOK], F32R)
        self.consts = sb("consts", [P, NCONST])
        self.ident = self.consts[:, C_ID:C_ID + P]
        sem = lambda name: ctx.enter_context(nc.semaphore(name))
        self.ln = {n: sem("ln_" + n) for n in ("chain", "var", "std", "xn", "turned", "evac", "added")}
        self.ln_runs = 0
        self.ln_links = 0
        self.ln_std = 0


def phase_semaphores(nc, ctx, prefix):
    taken = []

    def clear():
        nc.clear_and_free_semaphores(taken)
        nc.all_engine_barrier(sem_only=True)

    ctx.callback(clear)

    def sem(name):
        taken.append(nc.alloc_semaphore(prefix + name))
        return taken[-1]

    return sem


def load_phase(nc, core, x_dram, const_dram):
    with ExitStack() as ctx:
        loaded = ctx.enter_context(nc.semaphore("in_loaded"))
        block = ctx.enter_context(nc.Block())

        @block.sync
        def _(sp):
            sp.dma_start(core.x[:], x_dram.rearrange("(t p) d -> p t d", p=P)).then_inc(loaded, 16)
            sp.dma_start(core.consts[:], const_dram).then_inc(loaded, 16)
            sp.wait_ge(loaded, 32)


def store_phase(nc, core, out_dram):
    with ExitStack() as ctx:
        stored = ctx.enter_context(nc.semaphore("stored"))
        block = ctx.enter_context(nc.Block())

        @block.sync
        def _(sp):
            sp.dma_start(out_dram.rearrange("(t p) d -> p t d", p=P), core.x[:]).then_inc(stored, 16)
            sp.wait_ge(stored, 16)


def split_product(pe, out, wh, wl, xh, xl, start, stop):
    pe.matmul(out, wh, xh, start=start, stop=False, skip_group_check=True)
    ins = pe.matmul(out, wh, xl, start=False, stop=stop and wl is None, skip_group_check=True)
    if wl is not None:
        ins = pe.matmul(out, wl, xh, start=False, stop=stop, skip_group_check=True)
    return ins


def norm_phase(nc, core, name, add=False, rms_col=None, whole=None, sync=None, scalar=None,
               gpsimd=None):
    run, s = core.ln_runs, core.ln
    core.ln_runs += 1
    links = [core.ln_links]
    with ExitStack() as ctx:
        sb = lambda n, shape, dt=F32: ctx.enter_context(nc.sbuf_tensor(name + n, shape, dt))
        st = sb("st", [P, NT, 6])
        v = sb("v", [P, 10, NT])
        xn = sb("xn", [P, NT, D])
        hn = sb("hn", [P, NT, D]) if rms_col is not None else xn
        wcol = sb("wcol", [P, KD]) if rms_col is not None else None
        ps = ctx.enter_context(nc.psum_tensor(name + "ps", [P, 2, KD, HALF], F32))
        wsem = ctx.enter_context(nc.semaphore(name + "w")) if rms_col is not None else None
        block = ctx.enter_context(nc.Block())
        n_std = 2 if rms_col is not None else 1

        high = whole if whole is not None else core.xh

        def low_parts(half):
            tok = slice(half * HALF, (half + 1) * HALF)
            for f in range(KD):
                nc.vector.wait_ge(s["evac"], 2 * KD * run + KD * half + f + 1)
                src, hi, out = ps[:, half, f, :], core.xh[:, f, tok], core.xl[:, f, tok]
                if wcol is None:
                    nc.vector.tensor_tensor(out, src, hi, ALU.subtract)
                else:
                    nc.vector.scalar_tensor_tensor(out=out, in0=src, scalar=wcol[:, f:f + 1], in1=hi, op0=ALU.mult,
                                             op1=ALU.subtract)

        @block.sync
        def _(sp):
            if wcol is not None:
                sp.dma_start(wcol[:], rms_col).then_inc(wsem, 16)
            if sync:
                sync(sp)

        @block.vector
        def _(dve):
            def link(ins):
                links[0] += 1
                ins.then_inc(s["chain"], 1)
                dve.wait_ge(s["chain"], links[0])

            def values(half):
                return (v[:, i, half * 4:half * 4 + 4] for i in range(10))

            def statistics(half):
                for t in range(4 * half, 4 * half + 4):
                    ins = dve.bn_stats(st[:, t, :], core.x[:, t, :])
                link(ins)
                h = st[:, half * 4:half * 4 + 4, :]
                MEAN2, DIFF, VSUM, DSQ, VAR, MEAN, STD, RSTD, MS, RMS = values(half)
                dve.tensor_tensor(DIFF, h[:, :, 1], h[:, :, 4], ALU.subtract)
                dve.tensor_tensor(VSUM, h[:, :, 2], h[:, :, 5], ALU.add)
                link(dve.tensor_tensor(MEAN2, h[:, :, 1], h[:, :, 4], ALU.add))
                dve.tensor_scalar(MEAN, MEAN2, 0.5, None, ALU.mult)
                link(dve.scalar_tensor_tensor(out=DSQ, in0=DIFF, scalar=0.25, in1=DIFF, op0=ALU.mult, op1=ALU.mult))
                link(dve.scalar_tensor_tensor(out=VAR, in0=VSUM, scalar=1.0 / D, in1=DSQ, op0=ALU.mult,
                                              op1=ALU.add))
                dve.tensor_scalar(DSQ, VAR, EPS, None, ALU.add).then_inc(s["var"], 1)

            def normalise(half):
                MEAN2, DIFF, VSUM, DSQ, VAR, MEAN, STD, RSTD, MS, RMS = values(half)
                dve.wait_ge(s["std"], core.ln_std + n_std * half + 1)
                link(dve.reciprocal(RSTD, STD))
                if n_std == 2:
                    link(dve.tensor_tensor(MS, RSTD, RSTD, ALU.mult))
                    link(dve.tensor_tensor(MS, MS, VAR, ALU.mult))
                    dve.tensor_scalar(DSQ, MS, EPS, None, ALU.add).then_inc(s["var"], 1)
                    dve.wait_ge(s["std"], core.ln_std + 2 * half + 2)
                    link(dve.reciprocal(RMS, STD))
                for i in range(4):
                    t = 4 * half + i
                    ins = dve.tensor_scalar(xn[:, t, :], core.x[:, t, :], MEAN[:, i:i + 1], RSTD[:, i:i + 1],
                                            ALU.subtract, ALU.mult)
                    if n_std == 2:
                        link(ins)
                        ins = dve.tensor_scalar(hn[:, t, :], xn[:, t, :], RMS[:, i:i + 1], None, ALU.mult)
                    ins.then_inc(s["xn"], 1)

            for half in range(2):
                statistics(half)
                normalise(half)
            if whole is None:
                for half in range(2):
                    low_parts(half)

        @block.gpsimd
        def _(pool):
            if gpsimd:
                gpsimd(pool)
            if add:
                for t in range(NT):
                    pool.wait_ge(s["xn"], NT * run + t + 1)
                    pool.tensor_tensor(core.x[:, t, :], core.x[:, t, :], xn[:, t, :], ALU.add)

        @block.scalar
        def _(act):
            def roots(half):
                STD, DSQ = (v[:, row, half * 4:half * 4 + 4] for row in (6, 3))
                for i in range(n_std):
                    act.wait_ge(s["var"], core.ln_std + n_std * half + i + 1)
                    act.activation(STD, DSQ, ACT.Sqrt).then_inc(s["std"], 1)

            def high_parts(half, tiles):
                act.wait_ge(s["turned"], NT * run + 4 * (half + 1))
                for f in tiles:
                    act.activation(high[:, f, half * HALF:(half + 1) * HALF], ps[:, half, f, :], ACT.Copy,
                                   scale=1.0 if wcol is None else wcol[:, f:f + 1]).then_inc(s["evac"], 1)

            roots(0)
            if scalar:
                scalar(act)
            if wcol is not None:
                act.wait_ge(wsem, 16)
            high_parts(0, (0, 1))
            roots(1)
            high_parts(0, (2, 3))
            high_parts(1, range(KD))

        @block.tensor
        def _(pe):
            for t in range(NT):
                pe.wait_ge(s["xn"], NT * run + t + 1)
                for f in range(KD):
                    ins = pe.transpose(ps[:, t // 4, f, (t % 4) * P:(t % 4 + 1) * P],
                                       hn[:, t, f * P:(f + 1) * P], core.ident)
                ins.then_inc(s["turned"], 1)
    core.ln_links = links[0]
    core.ln_std += 2 * n_std


def slice_steps(eng, half, body):
    for f in range(2):
        body(f, FT * half + f, (half * FT + f) % 2)
    with eng.Fori(0, (FT - 2) // 2) as i:
        for j in range(2):
            body(2 + 2 * i + j, FT * half + 2 + 2 * i + j, (half * FT + j) % 2)
    for f in range(FT - FT % 2, FT):
        body(f, FT * half + f, (half * FT + f) % 2)


def early(step, n):
    return isinstance(step, int) and step < n


def landed(step, slot):
    return 8 * (step - slot) + 16


def ffn_phase(nc, core, name, w_gu, w_down):
    LAST = 2 * FT
    with ExitStack() as ctx:
        sb = lambda n, shape, dt=F32: ctx.enter_context(nc.sbuf_tensor(name + n, shape, dt))
        pb = lambda n, shape: ctx.enter_context(nc.psum_tensor(name + n, shape, F32))
        sem = phase_semaphores(nc, ctx, name)
        wgu = sb("wgu", [P, 2, 2, KD, P])
        wd = sb("wd", [P, 2, D])
        wgu_h, wgu_l = (sb(n, [P, 2, 2, KD, P], F32R) for n in ("wgu_h", "wgu_l"))
        wd_h, wd_l = (sb(n, [P, 2, D], F32R) for n in ("wd_h", "wd_l"))
        sil = sb("sil", [P, 2, HALF])
        hT = sb("hT", [P, 2, HALF])
        hT_h, hT_l = (sb(n, [P, 2, HALF], F32R) for n in ("hT_h", "hT_l"))
        gu_loaded = [sem(f"gu_loaded{i}") for i in range(2)]
        d_loaded = [sem(f"d_loaded{i}") for i in range(2)]
        (gu_high, gu_low, d_high, d_low, gate_ready, up_ready, silu_done, h_ready, h_high, h_low, down_done,
         acc_added) = (sem(n) for n in ("gu_high", "gu_low", "d_high", "d_low", "gate_ready", "up_ready", "silu_done",
                                        "h_ready", "h_high", "h_low", "down_done", "acc_added"))

        def first_loads(sp):
            for f in range(2):
                sp.dma_start(wgu[:, f], w_gu[f]).then_inc(gu_loaded[f], 16)
                sp.dma_start(wd[:, f], w_down[f]).then_inc(d_loaded[f], 16)

        def round_gate_up(act, step, slot):
            act.wait_ge(gu_loaded[slot], landed(step, slot))
            if not early(step, 2):
                act.wait_ge(up_ready, step - 1)
            act.activation(wgu_h[:, slot], wgu[:, slot], ACT.Copy).then_inc(gu_high, 1)

        def rest_of_gate_up(pool, step, slot):
            pool.wait_ge(gu_high, step + 1)
            pool.tensor_tensor(wgu_l[:, slot], wgu[:, slot], wgu_h[:, slot], ALU.subtract).then_inc(gu_low, 1)

        norm_phase(nc, core, name + "n", sync=first_loads, scalar=lambda act: round_gate_up(act, 0, 0),
                   gpsimd=lambda pool: rest_of_gate_up(pool, 0, 0))
        ps_gu = pb("psgu", [P, 2, HALF])
        acc = pb("acc", [P, 4, D])
        block = ctx.enter_context(nc.Block())

        @block.sync
        def _(sp):
            for half in range(2):
                def load(f, step, slot):
                    if early(step, 2):
                        return
                    sp.wait_ge(gu_low, step - 1)
                    sp.dma_start(wgu[:, slot], w_gu[f]).then_inc(gu_loaded[slot], 16)
                    sp.wait_ge(d_low, step - 1)
                    sp.dma_start(wd[:, slot], w_down[f]).then_inc(d_loaded[slot], 16)
                slice_steps(sp, half, load)

        @block.tensor
        def _(pe):
            for half in range(2):
                tok = slice(half * HALF, (half + 1) * HALF)

                def gate_up(step, slot):
                    pe.wait_ge(gu_low, step + 1)
                    for w, ready, used in ((0, gate_ready, silu_done), (1, up_ready, h_ready)):
                        if not early(step, 1):
                            pe.wait_ge(used, step)
                        for k in range(KD):
                            ins = split_product(pe, ps_gu[:, w, :], wgu_h[:, slot, w, k, :], wgu_l[:, slot, w, k, :],
                                                core.xh[:, k, tok], core.xl[:, k, tok], k == 0, k == KD - 1)
                        ins.then_inc(ready, 1)

                def down(step, slot, first, last):
                    pe.wait_ge(d_low, step + 1)
                    if first and half:
                        pe.wait_ge(acc_added, 4)
                    pe.wait_ge(h_high, step + 1)
                    for t in range(4):
                        hi = hT_h[:, slot, t * P:(t + 1) * P]
                        pe.matmul(acc[:, t, :], hi, wd_h[:, slot, :], start=first, stop=False, skip_group_check=True)
                        pe.matmul(acc[:, t, :], hi, wd_l[:, slot, :], start=False, stop=False, skip_group_check=True)
                    pe.wait_ge(h_low, step + 1)
                    for t in range(4):
                        ins = pe.matmul(acc[:, t, :], hT_l[:, slot, t * P:(t + 1) * P], wd_h[:, slot, :],
                                        start=False, stop=last, skip_group_check=True)
                    ins.then_inc(down_done, 1)

                def both(f, step, slot):
                    gate_up(step, slot)
                    if not early(f, 1):
                        down(step - 1, 1 - slot, early(f, 2), False)

                slice_steps(pe, half, both)
                down(FT * (half + 1) - 1, (FT * (half + 1) - 1) % 2, False, True)

        @block.scalar
        def _(act):
            def silu_and_round(step, slot):
                act.wait_ge(gate_ready, step + 1)
                if not early(step, 2):
                    act.wait_ge(h_ready, step - 1)
                act.activation(sil[:, slot, :], ps_gu[:, 0, :], ACT.Silu).then_inc(silu_done, 1)
                act.wait_ge(h_ready, step + 1)
                act.activation(hT_h[:, slot, :], hT[:, slot, :], ACT.Copy).then_inc(h_high, 1)

            def work(f, step, slot):
                if not early(step, 1):
                    round_gate_up(act, step, slot)
                    silu_and_round(step - 1, 1 - slot)
                act.wait_ge(d_loaded[slot], landed(step, slot))
                if not early(step, 2):
                    act.wait_ge(down_done, step - 1)
                act.activation(wd_h[:, slot], wd[:, slot], ACT.Copy).then_inc(d_high, 1)

            for half in range(2):
                slice_steps(act, half, work)
            silu_and_round(LAST - 1, (LAST - 1) % 2)

        @block.gpsimd
        def _(pool):
            def rests(f, step, slot):
                if not early(step, 1):
                    rest_of_gate_up(pool, step, slot)
                pool.wait_ge(d_high, step + 1)
                pool.tensor_tensor(wd_l[:, slot], wd[:, slot], wd_h[:, slot], ALU.subtract).then_inc(d_low, 1)

            for half in range(2):
                slice_steps(pool, half, rests)

        @block.vector
        def _(dve):
            def product(step, slot):
                dve.wait_ge(silu_done, step + 1)
                dve.wait_ge(up_ready, step + 1)
                if not early(step, 2):
                    dve.wait_ge(down_done, step - 1)
                dve.tensor_tensor(hT[:, slot, :], ps_gu[:, 1, :], sil[:, slot, :], ALU.mult).then_inc(h_ready, 1)
                dve.wait_ge(h_high, step + 1)
                dve.tensor_tensor(hT_l[:, slot, :], hT[:, slot, :], hT_h[:, slot, :],
                                  ALU.subtract).then_inc(h_low, 1)

            for half in range(2):
                slice_steps(dve, half, lambda f, step, slot: product(step, slot))
                dve.wait_ge(down_done, FT * (half + 1))
                for t in range(4):
                    xt = core.x[:, 4 * half + t, :]
                    dve.tensor_tensor(xt, acc[:, t, :], xt, ALU.add).then_inc(acc_added, 1)


def quant_ffn_phase(nc, core, name, w_gu, w_down, small):
    LAST = 2 * FT
    with ExitStack() as ctx:
        sb = lambda n, shape, dt=F32: ctx.enter_context(nc.sbuf_tensor(name + n, shape, dt))
        pb = lambda n, shape: ctx.enter_context(nc.psum_tensor(name + n, shape, F32))
        sem = phase_semaphores(nc, ctx, name)
        codes_gu = sb("codes_gu", [P, 2, 2, KD, P], I32)
        codes_d = sb("codes_d", [P, 2, D], I32)
        cgu = sb("cgu", [P, 2, 2, KD, P], F32R)
        cd = sb("cd", [P, 2, D], F32R)
        low_in = sb("low_in", [P, KD, P])
        low_in_h, low_in_l = (sb(n, [P, KD, P], F32R) for n in ("low_in_h", "low_in_l"))
        low_da = sb("low_da", [P, FT, RANK])
        low_b = sb("low_b", [2 * RANK, 2, F_PAD])
        low_db = sb("low_db", [RANK, D])
        scale_gu = sb("scale_gu", [P, 2, FT])
        scale_d = sb("scale_d", [P, D])
        b_slot_h, b_slot_l = (sb(n, [2 * RANK, 2, 2, P], F32R) for n in ("b_slot_h", "b_slot_l"))
        da_slot = sb("da_slot", [P, 2, RANK])
        lowx_h, lowx_l = (sb(n, [2 * RANK, TOK], F32R) for n in ("lowx_h", "lowx_l"))
        lowh = sb("lowh", [RANK, HALF])
        low = sb("low", [P, 2, HALF])
        gate = sb("gate", [P, HALF])
        up = sb("up", [P, HALF])
        sil = sb("sil", [P, HALF])
        hT = sb("hT", [P, 2, HALF])
        hT_h, hT_l = (sb(n, [P, 2, HALF], F32R) for n in ("hT_h", "hT_l"))
        scaled_acc = sb("scaled_acc", [P, 4, D])
        gu_loaded = [sem(f"gu_loaded{i}") for i in range(2)]
        d_loaded = [sem(f"d_loaded{i}") for i in range(2)]
        (small_loaded, scaled, in_high, in_low, lowx_ready, lowx_high, lowx_low, gu_ready, d_ready, b_high,
         b_low, gate_ready, up_ready, low_ready, low_kept, gate_kept, up_kept, silu_done, h_ready, h_high,
         h_low, down_done, lowh_kept, acc_scaled, rank_ready, x_added, acc_added) = (
            sem(n) for n in ("small_loaded scaled in_high in_low lowx_ready lowx_high lowx_low gu_ready "
                             "d_ready b_high b_low gate_ready up_ready low_ready low_kept gate_kept up_kept "
                             "silu_done h_ready h_high h_low down_done lowh_kept acc_scaled rank_ready x_added "
                             "acc_added").split())

        def first_loads(sp):
            for dst, src in ((low_in, small["a"]), (low_da, small["da"]), (low_b, small["b"]),
                             (low_db, small["db"]), (scale_gu, small["s_gu"])):
                sp.dma_start(dst[:], src).then_inc(small_loaded, 16)
            sp.dma_start(scale_d[:], small["s_d"].partition_broadcast(P)).then_inc(small_loaded, 16)
            for f in range(2):
                sp.dma_start(codes_gu[:, f], w_gu[f]).then_inc(gu_loaded[f], 16)
                sp.dma_start(codes_d[:, f], w_down[f]).then_inc(d_loaded[f], 16)

        def round_low_in(act):
            act.wait_ge(small_loaded, 16 * 6)
            act.activation(low_in_h[:], low_in[:], ACT.Copy).then_inc(in_high, 1)

        def rest_of_low_in(pool):
            pool.wait_ge(in_high, 1)
            pool.tensor_tensor(low_in_l[:], low_in[:], low_in_h[:], ALU.subtract).then_inc(in_low, 1)

        norm_phase(nc, core, name + "n", sync=first_loads, scalar=round_low_in, gpsimd=rest_of_low_in)
        ps_gu = pb("psgu", [P, 2, HALF])
        ps_low = pb("pslow", [P, HALF])
        ps_lowh = pb("pslowh", [P, HALF])
        acc = pb("acc", [P, 4, D])
        block = ctx.enter_context(nc.Block())

        @block.sync
        def _(sp):
            for half in range(2):
                def load(f, step, slot):
                    if early(step, 2):
                        return
                    sp.wait_ge(gu_ready, step - 1)
                    sp.dma_start(codes_gu[:, slot], w_gu[f]).then_inc(gu_loaded[slot], 16)
                    sp.wait_ge(d_ready, step - 1)
                    sp.dma_start(codes_d[:, slot], w_down[f]).then_inc(d_loaded[slot], 16)
                slice_steps(sp, half, load)

        @block.tensor
        def _(pe):
            pe.wait_ge(in_low, 1)
            for half in range(2):
                tok = slice(half * HALF, (half + 1) * HALF)
                for k in range(KD):
                    ins = split_product(pe, (ps_low, ps_lowh)[half][:], low_in_h[:, k, :], low_in_l[:, k, :],
                                        core.xh[:, k, tok], core.xl[:, k, tok], k == 0, k == KD - 1)
                ins.then_inc(lowx_ready, 1)
            pe.wait_ge(lowx_low, 2)
            for half in range(2):
                tok = slice(half * HALF, (half + 1) * HALF)

                def codes_and_low(w, step, slot, ready, kept):
                    if w or not early(step, 1):
                        pe.wait_ge(low_kept, 2 * step + w)
                    split_product(pe, ps_low[:], b_slot_h[:, slot, w, :], b_slot_l[:, slot, w, :], lowx_h[:, tok],
                                  lowx_l[:, tok], True, True).then_inc(low_ready, 1)
                    if not early(step, 1):
                        pe.wait_ge(kept, step)
                    for k in range(KD):
                        ins = split_product(pe, ps_gu[:, w, :], cgu[:, slot, w, k, :], None, core.xh[:, k, tok],
                                            core.xl[:, k, tok], k == 0, k == KD - 1)
                    ins.then_inc(ready, 1)

                def down(step, slot, first, last):
                    pe.wait_ge(d_ready, step + 1)
                    pe.wait_ge(h_ready, step + 1)
                    if first and half:
                        pe.wait_ge(acc_added, 4)
                    pe.matmul(ps_lowh[0:RANK, :], da_slot[:, slot, :], hT[:, slot, :], start=first, stop=last,
                              skip_group_check=True)
                    pe.wait_ge(h_high, step + 1)
                    for t in range(4):
                        pe.matmul(acc[:, t, :], hT_h[:, slot, t * P:(t + 1) * P], cd[:, slot, :], start=first,
                                  stop=False, skip_group_check=True)
                    pe.wait_ge(h_low, step + 1)
                    for t in range(4):
                        ins = pe.matmul(acc[:, t, :], hT_l[:, slot, t * P:(t + 1) * P], cd[:, slot, :], start=False,
                                        stop=last, skip_group_check=True)
                    ins.then_inc(down_done, 1)

                def both(f, step, slot):
                    pe.wait_ge(gu_ready, step + 1)
                    pe.wait_ge(b_low, step + 1)
                    codes_and_low(0, step, slot, gate_ready, gate_kept)
                    if not early(f, 1):
                        down(step - 1, 1 - slot, early(f, 2), False)
                    codes_and_low(1, step, slot, up_ready, up_kept)

                slice_steps(pe, half, both)
                down(FT * (half + 1) - 1, (FT * (half + 1) - 1) % 2, False, True)
                pe.wait_ge(lowh_kept, half + 1)
                for t in range(4):
                    pe.wait_ge(acc_scaled, 4 * half + t + 1)
                    pe.matmul(acc[:, t, :], lowh[:, t * P:(t + 1) * P], low_db[:], start=True,
                              stop=True).then_inc(rank_ready, 1)

        @block.scalar
        def _(act):
            def copy_b(f, slot):
                act.activation(b_slot_h[:, slot, :, :], low_b[:, :, bass.ts(f, P)], ACT.Copy).then_inc(b_high, 1)

            copy_b(0, 0)
            for half in range(2):
                act.wait_ge(lowx_ready, half + 1)
                act.activation(lowx_h[:, half * HALF:(half + 1) * HALF], (ps_low, ps_lowh)[half][0:2 * RANK, :],
                               ACT.Copy, scale=LR_SCALE).then_inc(lowx_high, 1)

            def keep_low(w, step):
                act.wait_ge(low_ready, 2 * step + w + 1)
                if not early(step, 1):
                    act.wait_ge((gate_kept, up_kept)[w], step)
                act.activation(low[:, w, :], ps_low[:], ACT.Copy).then_inc(low_kept, 1)

            def round_h(step, slot):
                act.wait_ge(h_ready, step + 1)
                act.activation(hT_h[:, slot, :], hT[:, slot, :], ACT.Copy).then_inc(h_high, 1)

            def work(f, step, slot):
                if isinstance(step, int) and step == FT:
                    round_h(step - 1, 1 - slot)
                    keep_lowh(0)
                    keep_low(0, step)
                else:
                    keep_low(0, step)
                    if not early(step, 1):
                        round_h(step - 1, 1 - slot)
                if isinstance(f, int) and f == FT - 1:
                    if step < LAST - 1:
                        copy_b(0, 1 - slot)
                else:
                    copy_b(f + 1, 1 - slot)
                act.wait_ge(gate_kept, step + 1)
                act.activation(sil[:], gate[:], ACT.Silu).then_inc(silu_done, 1)
                keep_low(1, step)

            def keep_lowh(half):
                act.wait_ge(down_done, FT * (half + 1))
                act.activation(lowh[:], ps_lowh[0:RANK, :], ACT.Copy, scale=LR_SCALE).then_inc(lowh_kept, 1)

            for half in range(2):
                slice_steps(act, half, work)
            round_h(LAST - 1, (LAST - 1) % 2)
            keep_lowh(1)

        @block.gpsimd
        def _(pool):
            def hidden(step, slot):
                pool.wait_ge(h_high, step + 1)
                pool.tensor_tensor(hT_l[:, slot, :], hT[:, slot, :], hT_h[:, slot, :],
                                   ALU.subtract).then_inc(h_low, 1)

            for half in range(2):
                slice_steps(pool, half, lambda f, step, slot: hidden(step, slot))

        @block.vector
        def _(dve):
            dve.wait_ge(small_loaded, 16 * 6)
            dve.tensor_scalar(scale_gu[:], scale_gu[:], Q_STEP, None, ALU.mult).then_inc(scaled, 1)
            dve.tensor_scalar(scale_d[:], scale_d[:], Q_STEP, None, ALU.mult).then_inc(scaled, 1)
            dve.wait_ge(scaled, 2)

            def rest_of_b(f, step, slot):
                f = bass.ts(f, P) if not isinstance(f, int) else slice(f * P, (f + 1) * P)
                dve.wait_ge(b_high, step + 1)
                dve.tensor_tensor(b_slot_l[:, slot], low_b[:, :, f], b_slot_h[:, slot],
                                  ALU.subtract).then_inc(b_low, 1)

            rest_of_b(0, 0, 0)
            for half in range(2):
                tok = slice(half * HALF, (half + 1) * HALF)
                dve.wait_ge(lowx_high, half + 1)
                dve.scalar_tensor_tensor(out=lowx_l[:, tok], in0=(ps_low, ps_lowh)[half][0:2 * RANK, :],
                                         scalar=LR_SCALE, in1=lowx_h[:, tok], op0=ALU.mult,
                                         op1=ALU.subtract).then_inc(lowx_low, 1)

            def scale_and_add(w, f, step, dst):
                dve.wait_ge(low_kept, 2 * step + w + 1)
                col = scale_gu[:, w, f:f + 1] if isinstance(f, int) else scale_gu[:, w, bass.ds(f, 1)]
                return dve.scalar_tensor_tensor(out=dst[:], in0=ps_gu[:, w, :], scalar=col, in1=low[:, w, :],
                                                op0=ALU.mult, op1=ALU.add)

            def keep_gate(f, step):
                dve.wait_ge(gate_ready, step + 1)
                if not early(step, 1):
                    dve.wait_ge(silu_done, step)
                scale_and_add(0, f, step, gate).then_inc(gate_kept, 1)

            def keep_up_and_multiply(f, step, slot):
                dve.wait_ge(up_ready, step + 1)
                scale_and_add(1, f, step, up).then_inc(up_kept, 1)
                dve.wait_ge(up_kept, step + 1)
                dve.wait_ge(silu_done, step + 1)
                if not early(step, 2):
                    dve.wait_ge(down_done, step - 1)
                dve.tensor_tensor(hT[:, slot, :], up[:], sil[:], ALU.mult).then_inc(h_ready, 1)

            def centre(f, step, slot):
                dve.wait_ge(gu_loaded[slot], landed(step, slot))
                if not early(step, 2):
                    dve.wait_ge(up_ready, step - 1)
                dve.tensor_scalar(cgu[:, slot], codes_gu[:, slot], -Q_ZERO, None, ALU.add).then_inc(gu_ready, 1)

            def work(f, step, slot):
                if early(step, 1):
                    centre(f, step, slot)
                dve.wait_ge(d_loaded[slot], landed(step, slot))
                if not early(step, 2):
                    dve.wait_ge(down_done, step - 1)
                dve.tensor_copy(da_slot[:, slot, :], low_da[:, f, :])
                dve.tensor_scalar(cd[:, slot, :], codes_d[:, slot, :], -Q_ZERO, None, ALU.add).then_inc(d_ready, 1)
                keep_gate(f, step)
                if not (isinstance(step, int) and step == LAST - 1):
                    centre(f, step + 1, 1 - slot)
                    rest_of_b(0 if isinstance(f, int) and f == FT - 1 else f + 1, step + 1, 1 - slot)
                keep_up_and_multiply(f, step, slot)

            for half in range(2):
                slice_steps(dve, half, work)
                dve.wait_ge(down_done, FT * (half + 1))
                for t in range(4):
                    dve.tensor_tensor(scaled_acc[:, t, :], acc[:, t, :], scale_d[:],
                                      ALU.mult).then_inc(acc_scaled, 1)
                for t in range(4):
                    xt = core.x[:, 4 * half + t, :]
                    dve.wait_ge(acc_scaled, 4 * half + t + 1)
                    dve.tensor_tensor(xt, scaled_acc[:, t, :], xt, ALU.add).then_inc(x_added, 1)
                for t in range(4):
                    xt = core.x[:, 4 * half + t, :]
                    dve.wait_ge(x_added, 4 * half + t + 1)
                    dve.wait_ge(rank_ready, 4 * half + t + 1)
                    dve.tensor_tensor(xt, acc[:, t, :], xt, ALU.add).then_inc(acc_added, 1)


def across_batch_phase(nc, core, xT):
    B2 = BATCH * BATCH
    with ExitStack() as ctx:
        sb = lambda n, shape, dt=F32: ctx.enter_context(nc.sbuf_tensor("ab_" + n, shape, dt))
        sem = phase_semaphores(nc, ctx, "ab_")
        sc = sb("sc", [P, KD, BATCH, BATCH])
        junk = sb("junk", [P, 4, SEQ])
        mx = sb("mx", [P, KD * BATCH])
        ex = sb("ex", [P, KD * BATCH, BATCH])
        sm = sb("sm", [P, KD * BATCH])
        msg = sb("msg", [P, KD, TOK])
        ps = ctx.enter_context(nc.psum_tensor("ab_ps", [P, NT, D], F32))
        chain, dotted, max_done, exp_done, probs_ready, begun, msg_ready, turned = (
            sem(n) for n in ("chain", "dotted", "max_done", "exp_done", "probs_ready", "begun", "msg_ready",
                             "turned"))
        block = ctx.enter_context(nc.Block())
        xv = xT[:, :, :].rearrange("p k (b s) -> p k b s", b=BATCH)
        mv = msg[:, :, :].rearrange("p k (b s) -> p k b s", b=BATCH)

        @block.vector
        def _(dve):
            n_chain = [0]

            def link(ins):
                n_chain[0] += 1
                ins.then_inc(chain, 1)
                dve.wait_ge(chain, n_chain[0])

            pairs = [(k, n, m) for k in range(KD) for n in range(BATCH) for m in range(n, BATCH)]
            for i, (k, n, m) in enumerate(pairs):
                if i >= 4:
                    dve.wait_ge(dotted, i - 3)
                dve.tensor_tensor_reduce(junk[:, i % 4, :], xv[:, k, n, :], xv[:, k, m, :], 1.0, 0.0, ALU.mult,
                                         ALU.add, sc[:, k, n, m:m + 1]).then_inc(dotted, 1)
            dve.wait_ge(dotted, len(pairs))
            for n in range(BATCH):
                for m in range(n):
                    ins = dve.tensor_copy(sc[:, :, n, m], sc[:, :, m, n])
            link(ins)
            rows = sc[:, :, :, :].rearrange("p k n m -> p (k n) m")
            link(dve.tensor_reduce(mx[:], rows, AX.X, ALU.max))
            dve.tensor_tensor(ex[:], rows, mx[:].unsqueeze(2).broadcast_to((P, KD * BATCH, BATCH)),
                              ALU.subtract).then_inc(max_done, 1)
            dve.wait_ge(exp_done, 1)
            link(dve.tensor_reduce(sm[:], ex[:], AX.X, ALU.add))
            link(dve.reciprocal(mx[:], sm[:]))
            link(dve.tensor_tensor(ex[:], ex[:], mx[:].unsqueeze(2).broadcast_to((P, KD * BATCH, BATCH)), ALU.mult))
            for n in range(BATCH):
                own = ex[:, :, n].rearrange("p (k n) -> p k n", n=BATCH)[:, :, n]
                ins = dve.tensor_scalar(own, own, 1.0, None, ALU.add)
            ins.then_inc(probs_ready, 1)
            dve.wait_ge(probs_ready, 1)
            for k in range(KD):
                for m in range(1, BATCH):
                    for n in range(BATCH):
                        if m == 1:
                            dve.wait_ge(begun, BATCH * k + n + 1)
                        ins = dve.scalar_tensor_tensor(
                            out=mv[:, k, n, :], in0=xv[:, k, m, :], scalar=ex[:, k * BATCH + n, m:m + 1],
                            in1=mv[:, k, n, :], op0=ALU.mult, op1=ALU.add)
                    if m < BATCH - 1:
                        link(ins)
                ins.then_inc(msg_ready, 1)
            for t in range(NT):
                dve.wait_ge(turned, (KD - 1) * NT + t + 1)
                xt = core.x[:, t, :]
                dve.tensor_tensor(xt, ps[:, t, :], xt, ALU.add)

        @block.scalar
        def _(act):
            act.wait_ge(max_done, 1)
            act.activation(ex[:], ex[:], ACT.Exp, scale=1.0 / float(SEQ) ** 0.5).then_inc(exp_done, 1)
            act.wait_ge(probs_ready, 1)
            for k in range(KD):
                for n in range(BATCH):
                    act.activation(mv[:, k, n, :], xv[:, k, 0, :], ACT.Copy,
                                   scale=ex[:, k * BATCH + n, 0:1]).then_inc(begun, 1)

        @block.tensor
        def _(pe):
            for k in range(KD):
                pe.wait_ge(msg_ready, k + 1)
                for t in range(NT):
                    pe.transpose(ps[:, t, k * P:(k + 1) * P], msg[:, k, t * P:(t + 1) * P],
                                 core.ident).then_inc(turned, 1)


def attention_phase(nc, core, name, w_qkv, w_o, kv_heads, causal, b_qkv=None, b_o=None):
    kv_t = kv_heads * HD // P
    KW, VW = kv_t * P, kv_heads * HD
    ALL = D + KW + VW
    QUADS = HPT // 4
    PER_T = KD * QUADS
    JOBS = PER_T * BT
    jobs = [(n // QUADS % KD, n % QUADS, n // PER_T) for n in range(JOBS)]
    pieces = [(t, at, min(HALF, ALL - at)) for t in range(BT) for at in range(0, ALL, HALF)]
    N_PIECES = len(pieces)
    PIECE_AT = {(0, 1, 3, 4, 5, 6)[i]: i for i in range(N_PIECES)}
    TURN_AT, PROJECT_AT = JOBS - 3, JOBS - 2
    BANKS_K = min(kv_t, 2)
    NH = (D + KW) // HD
    n_small = 2 + (2 if b_qkv is not None else 0)
    with ExitStack() as ctx:
        sb = lambda n, shape, dt=F32: ctx.enter_context(nc.sbuf_tensor(name + n, shape, dt))
        pb = lambda n, shape: ctx.enter_context(nc.psum_tensor(name + n, shape, F32))
        sem = phase_semaphores(nc, ctx, name)
        wq = sb("wq", [P, KD, ALL])
        wo = sb("wo", [P, KD, D])
        if causal:
            identb = sb("identb", [P, P], BF16)
            tri4 = sb("tri4", [P, 4, P], BF16)
            tri_right = sb("tri_right", [P, 2, 2, P], BF16)
        bq = sb("bq", [P, ALL]) if b_qkv is not None else None
        bo = sb("bo", [P, D]) if b_o is not None else None
        xb = sb("xb", [P, KD, SEQ])
        raw = sb("raw", [P, BT, ALL])
        cosd = sb("cosd", [P, D + KW])
        roped = sb("roped", [P, BT, D + KW])
        v = sb("v", [P, BT, VW])
        qT = sb("qT", [P, KD, SEQ])
        kT = sb("kT", [P, kv_t, HPT, SEQ])
        nm = sb("nm", [P, 2, 4])
        rows = sb("rows", [P, BT, HEADS])
        rec = sb("rec", [P, BT, HEADS])
        pr = sb("pr", [P, 2, 4, SEQ])
        pT = sb("pT", [P, 2, BT, 4, P])
        o = sb("o", [P, D])
        oT = sb("oT", [P, KD, P])
        (w_loaded, xb_ready, piece_ready, piece_kept, v_ready, rotated, roped_ready, turned, qT_ready, k_dve, k_act,
         scores_ready, max_ready, probs_ready, pT_ready, pT_kept, pv_done, rec_ready, o_ready, oT_ready, oT_kept,
         out_ready, x_added, biased, tri_made) = (
            sem(n) for n in ("w_loaded", "xb_ready", "piece_ready", "piece_kept", "v_ready", "rotated",
                             "roped_ready", "turned", "qT_ready", "k_dve", "k_act", "scores_ready", "max_ready",
                             "probs_ready", "pT_ready", "pT_kept", "pv_done", "rec_ready", "o_ready", "oT_ready",
                             "oT_kept", "out_ready", "x_added", "biased",
                             "tri_made"))
        X0 = 1

        def loads(sp):
            sp.dma_start(wq[:], w_qkv).then_inc(w_loaded, 16)
            if bq is not None:
                sp.dma_start(bq[:], b_qkv.partition_broadcast(P)).then_inc(w_loaded, 16)
                sp.dma_start(bo[:], b_o.partition_broadcast(P)).then_inc(w_loaded, 16)
            sp.dma_start(wo[:], w_o).then_inc(w_loaded, 16)

        norm_phase(nc, core, name + "n", sync=loads)
        ps_s = [pb(f"ps_s{i}", [P, 2, HALF]) for i in range(2)]
        ps_p = pb("ps_p", [P, 2, HALF])
        ps_o = pb("ps_o", [P, D])
        ps_x = pb("ps_x", [P, HALF])
        block = ctx.enter_context(nc.Block())
        ps_qT = ps_s[1][:, :, :].rearrange("p a (c s) -> p (a c) s", s=SEQ)
        ps_kT = ps_p[:, :, :].rearrange("p a (c s) -> p (a c) s", s=SEQ)

        def batches(eng, body):
            with eng.Fori(0, BATCH - 1) as b:
                body(b, False)
            body(BATCH - 1, True)

        def first(bn):
            return isinstance(bn, int) and bn == 0

        def piece_bank(bn, i):
            return (ps_x, ps_o)[i % 2 if first(bn) else 0]

        def rotate(eng, bn, t):
            eng.wait_ge(piece_kept, N_PIECES * bn + N_PIECES // BT * (t + 1))
            if t or not first(bn):
                eng.wait_ge(roped_ready, 2 * bn + t)
            c0, s0 = C_COS + t * HD, C_SIN + t * HD
            cos = core.consts[:, c0:c0 + HD].unsqueeze(1).broadcast_to((P, NH, HD))
            eng.tensor_tensor(cosd[:, :].rearrange("p (h d) -> p h d", d=HD),
                              raw[:, t, 0:D + KW].rearrange("p (h d) -> p h d", d=HD), cos, ALU.mult)
            r = raw[:, t, 0:D + KW].rearrange("p (h two d) -> p h two d", two=2, d=HD // 2)
            out = roped[:, t, :].rearrange("p (h two d) -> p h two d", two=2, d=HD // 2)
            for part in range(2):
                lo = s0 + part * HD // 2
                sin = core.consts[:, lo:lo + HD // 2].unsqueeze(1).broadcast_to((P, NH, HD // 2))
                ins = eng.tensor_tensor(out[:, :, part, :], r[:, :, 1 - part, :], sin, ALU.mult)
            ins.then_inc(rotated, 1)
            eng.wait_ge(rotated, 2 * bn + t + 1)
            eng.tensor_tensor(roped[:, t, :], roped[:, t, :], cosd[:], ALU.add).then_inc(roped_ready, 1)

        def copy_tokens(eng, bn):
            tok = bass.ts(bn, SEQ)
            eng.tensor_tensor(xb[:], core.xh[:, :, tok], core.xl[:, :, tok], ALU.add).then_inc(xb_ready, 1)

        def n_keys(t):
            return t + 1 if causal else BT

        def scores_view(slot, t):
            kw = n_keys(t) * P
            return ps_s[slot][:, :, :].rearrange("p a n -> p (a n)")[:, 0:4 * kw].rearrange("p (h k) -> p h k", k=kw)

        @block.tensor
        def _(pe):
            def project(bn, i):
                t, at, width = pieces[i]
                if i == 0:
                    pe.wait_ge(xb_ready, bn + 1)
                    if not first(bn):
                        pe.wait_ge(x_added, X0 + 2 * (bn - 1))
                        pe.wait_ge(piece_kept, N_PIECES * bn)
                elif not first(bn):
                    pe.wait_ge(piece_kept, N_PIECES * bn + i)
                elif i > 1:
                    pe.wait_ge(piece_kept, i - 1)
                for k in range(KD):
                    ins = pe.matmul(piece_bank(bn, i)[:, 0:width], xb[:, k, t * P:(t + 1) * P], wq[:, k, at:at + width],
                                    start=k == 0, stop=k == KD - 1)
                ins.then_inc(piece_ready, 1)

            def turn(bn, dst, count, at):
                for t in range(BT):
                    for c in range(count):
                        ins = pe.transpose(dst[:, c, t * P:(t + 1) * P],
                                           roped[:, t, at + c * P:at + (c + 1) * P], core.ident)
                ins.then_inc(turned, 1)

            def turn_queries(bn):
                pe.wait_ge(roped_ready, 2 * bn + 2)
                turn(bn, ps_qT, KD, 0)

            def turn_keys(bn):
                turn(bn, ps_kT, kv_t, D)

            def turn_sums(b, t, last):
                pe.wait_ge(o_ready, 2 * b + t + 1)
                pe.wait_ge(x_added, X0 + 2 * b + t)
                if t == 0:
                    pe.wait_ge(piece_kept, N_PIECES * (b + (1 if last else 2)))
                for c in range(KD):
                    ins = pe.transpose(ps_x[:, c * P:(c + 1) * P], o[:, c * P:(c + 1) * P], core.ident)
                ins.then_inc(oT_ready, 1)

            def project_sums(b, t):
                pe.wait_ge(oT_kept, 2 * b + t + 1)
                for k in range(KD):
                    ins = pe.matmul(ps_x[:], oT[:, k, :], wo[:, k, :], start=k == 0, stop=k == KD - 1)
                ins.then_inc(out_ready, 1)

            pe.wait_ge(w_loaded, 16 * n_small)
            for i in range(N_PIECES):
                project(0, i)
            if causal:
                pe.wait_ge(tri_made, 1)
            turn_queries(0)
            turn_keys(0)

            def batch(b, last):
                pe.wait_ge(qT_ready, b + 1)

                def scores(n):
                    c, gq, t = jobs[n]
                    kc = c if kv_t > 1 else 0
                    if n % QUADS == 0 and n < PER_T:
                        if kc < BANKS_K:
                            pe.wait_ge(k_dve, BANKS_K * b + kc + 1)
                        else:
                            pe.wait_ge(k_act, b + 1)
                    if n >= 2:
                        pe.wait_ge(probs_ready, JOBS * b + (n - 1))
                    view = scores_view(n % 2, t)
                    q = qT[:, c, t * P:(t + 1) * P]
                    per = HALF // (n_keys(t) * P)
                    for h in range(0, 4, per):
                        if causal:
                            mask = tri4[:] if t == 0 else tri_right[:].rearrange("p a b c -> p a (b c)")
                            pe.matmul(view[:, h:h + per, :], identb[:], mask, start=True, stop=False)
                        ins = pe.matmul(view[:, h:h + per, :], q,
                                        kT[:, kc, 4 * gq + h:4 * gq + h + per, 0:n_keys(t) * P],
                                        start=not causal, stop=True)
                    ins.then_inc(scores_ready, 1)

                scores(0)
                scores(1)
                for n in range(JOBS):
                    c, gq, t = jobs[n]
                    pe.wait_ge(probs_ready, JOBS * b + (n + 1))
                    if n:
                        pe.wait_ge(pT_kept, JOBS * b + n)
                    else:
                        pe.wait_ge(k_dve, BANKS_K * (b + 1))
                        if kv_t > BANKS_K:
                            pe.wait_ge(k_act, b + 1)
                    for kt in range(n_keys(t)):
                        for h in range(4):
                            ins = pe.transpose(ps_p[:, kt, h * P:(h + 1) * P],
                                               pr[:, n % 2, h, kt * P:(kt + 1) * P], core.ident)
                    ins.then_inc(pT_ready, 1)
                    if n + 2 < JOBS:
                        scores(n + 2)
                    if not last and n in PIECE_AT:
                        project(b + 1, PIECE_AT[n])
                    if n == TURN_AT:
                        turn_sums(b, 0, last)
                    if n == PROJECT_AT:
                        project_sums(b, 0)
                    if n == JOBS - 1 and not last:
                        turn_queries(b + 1)
                    pe.wait_ge(pT_kept, JOBS * b + (n + 1))
                    if n == 0:
                        pe.wait_ge(v_ready, b + 1)
                    if n == PER_T:
                        pe.wait_ge(o_ready, 2 * b + 1)
                    for h in range(4):
                        g = 4 * gq + h
                        head = HPT * c + g
                        kv = head if kv_t > 1 else g
                        for kt in range(n_keys(t)):
                            ins = pe.matmul(ps_o[:, head * HD:(head + 1) * HD], pT[:, n % 2, kt, h, :],
                                            v[:, kt, kv * HD:(kv + 1) * HD], start=kt == 0, stop=kt == n_keys(t) - 1)
                    ins.then_inc(pv_done, 1)
                if not last:
                    turn_keys(b + 1)
                turn_sums(b, 1, last)
                project_sums(b, 1)

            batches(pe, batch)

        @block.vector
        def _(dve):
            def keep_piece(bn, i):
                t, at, width = pieces[i]
                dve.wait_ge(piece_ready, N_PIECES * bn + i + 1)
                if i == 0 and not first(bn):
                    dve.wait_ge(v_ready, bn)
                dve.tensor_tensor(raw[:, t, at:at + width], piece_bank(bn, i)[:, 0:width], bq[:, at:at + width],
                                  ALU.add).then_inc(piece_kept, 1)

            def mask_keys(bn):
                dve.wait_ge(turned, 2 * bn + 2)
                heads = core.consts[:, C_HM:C_HM + HPT].unsqueeze(2).broadcast_to((P, HPT, SEQ))
                for c in range(BANKS_K):
                    dve.tensor_tensor(kT[:, c], ps_kT[:, c, :].unsqueeze(1).broadcast_to((P, HPT, SEQ)), heads,
                                      ALU.mult).then_inc(k_dve, 1)

            def normalise(b, t):
                dve.wait_ge(probs_ready, JOBS * b + PER_T * (t + 1))
                dve.reciprocal(rec[:, t, :], rows[:, t, :]).then_inc(rec_ready, 1)
                dve.wait_ge(rec_ready, 2 * b + t + 1)
                dve.wait_ge(pv_done, JOBS * b + PER_T * (t + 1))
                dve.tensor_tensor(o[:, :].rearrange("p (h d) -> p h d", d=HD),
                                  ps_o[:, :].rearrange("p (h d) -> p h d", d=HD),
                                  rec[:, t, :].unsqueeze(2).broadcast_to((P, HEADS, HD)),
                                  ALU.mult).then_inc(o_ready, 1)

            def add_to_residual(b, t):
                dve.wait_ge(out_ready, 2 * b + t + 1)
                xt = core.x[:, 2 * b + t, :]
                dve.tensor_tensor(xt, ps_x[:], xt, ALU.add).then_inc(x_added, 1)

            if causal:
                tri = core.consts[:, C_TRI:C_TRI + P]
                dve.tensor_copy(identb[:], core.ident)
                dve.tensor_copy(tri4[:], tri.unsqueeze(1).broadcast_to((P, 4, P)))
                dve.memset(tri_right[:, :, 0, :], 0.0)
                dve.tensor_copy(tri_right[:, :, 1, :], tri.unsqueeze(1).broadcast_to((P, 2, P))).then_inc(tri_made, 1)
            dve.wait_ge(w_loaded, 16 * n_small)
            copy_tokens(dve, 0)
            for t in range(BT):
                if bq is not None:
                    for i in range(N_PIECES // BT * t, N_PIECES // BT * (t + 1)):
                        keep_piece(0, i)
                rotate(dve, 0, t)
            mask_keys(0)
            if bo is not None:
                dve.wait_ge(biased, 1)

            def batch(b, last):
                def maximum(n):
                    t = jobs[n][2]
                    dve.wait_ge(scores_ready, JOBS * b + (n + 1))
                    dve.tensor_reduce(nm[:, n % 2, :], scores_view(n % 2, t), AX.X, ALU.max,
                                      negate=True).then_inc(max_ready, 1)

                maximum(0)
                maximum(1)
                for n in range(JOBS):
                    t = jobs[n][2]
                    if n == PER_T:
                        normalise(b, 0)
                    dve.wait_ge(pT_ready, JOBS * b + (n + 1))
                    if n >= 2:
                        dve.wait_ge(pv_done, JOBS * b + (n - 1))
                    kt = n_keys(t)
                    dve.tensor_copy(pT[:, n % 2, 0:kt].rearrange("p k h q -> p k (h q)"),
                                    ps_p[:, 0:kt, :]).then_inc(pT_kept, 1)
                    if n + 2 < JOBS:
                        maximum(n + 2)
                    if not last and bq is not None and n in PIECE_AT:
                        keep_piece(b + 1, PIECE_AT[n])
                    if n == PROJECT_AT:
                        add_to_residual(b, 0)
                normalise(b, 1)
                if not last:
                    mask_keys(b + 1)
                add_to_residual(b, 1)

            batches(dve, batch)

        @block.gpsimd
        def _(pool):
            pool.sem_inc(x_added, X0)
            pool.wait_ge(w_loaded, 16 * n_small)

            def prepare(bn):
                pool.wait_ge(piece_kept, N_PIECES * bn)
                copy_tokens(pool, bn)
                for t in range(BT):
                    rotate(pool, bn, t)

            if bo is not None:
                for t in range(NT):
                    ins = pool.tensor_tensor(core.x[:, t, :], core.x[:, t, :], bo[:], ALU.add)
                ins.then_inc(biased, 1)
            with pool.Fori(1, BATCH) as bn:
                prepare(bn)

        @block.scalar
        def _(act):
            def keep_piece(bn, i):
                t, at, width = pieces[i]
                act.wait_ge(piece_ready, N_PIECES * bn + i + 1)
                act.activation(raw[:, t, at:at + width], piece_bank(bn, i)[:, 0:width],
                               ACT.Copy).then_inc(piece_kept, 1)

            def keep_queries(bn):
                act.wait_ge(turned, 2 * bn + 1)
                act.activation(qT[:], ps_qT, ACT.Copy, scale=1.0 / float(HD) ** 0.5).then_inc(qT_ready, 1)

            def mask_keys_and_keep_values(bn):
                act.wait_ge(turned, 2 * bn + 2)
                act.activation(v[:], raw[:, :, D + KW:], ACT.Copy).then_inc(v_ready, 1)
                if kv_t > BANKS_K:
                    for g in range(HPT):
                        ins = act.activation(kT[:, BANKS_K:, g, :], ps_kT[:, BANKS_K:kv_t, :], ACT.Copy,
                                             scale=core.consts[:, C_HM + g:C_HM + g + 1])
                    ins.then_inc(k_act, 1)

            def keep_sums(b, t):
                act.wait_ge(oT_ready, 2 * b + t + 1)
                act.activation(oT[:], ps_x[:, :].rearrange("p (c q) -> p c q", q=P), ACT.Copy).then_inc(oT_kept, 1)

            if bq is None:
                for i in range(N_PIECES):
                    keep_piece(0, i)
            keep_queries(0)
            mask_keys_and_keep_values(0)

            def batch(b, last):
                for n in range(JOBS):
                    c, gq, t = jobs[n]
                    act.wait_ge(max_ready, JOBS * b + (n + 1))
                    if n >= 2:
                        act.wait_ge(pT_ready, JOBS * b + (n - 1))
                    for h in range(4):
                        head = HPT * c + 4 * gq + h
                        ins = act.activation(pr[:, n % 2, h, 0:n_keys(t) * P], scores_view(n % 2, t)[:, h, :],
                                             ACT.Exp, bias=nm[:, n % 2, h:h + 1],
                                             accum_out=rows[:, t, head:head + 1])
                    ins.then_inc(probs_ready, 1)
                    if not last and bq is None and n - 1 in PIECE_AT:
                        keep_piece(b + 1, PIECE_AT[n - 1])
                    if n - 1 == TURN_AT:
                        keep_sums(b, 0)
                if not last:
                    keep_queries(b + 1)
                keep_sums(b, 1)
                if not last:
                    mask_keys_and_keep_values(b + 1)

            batches(act, batch)


def dt_phase(nc, core, mem, dram):
    with ExitStack() as ctx:
        sb = lambda n, shape, dt=F32: ctx.enter_context(nc.sbuf_tensor("dt_" + n, shape, dt))
        sem = phase_semaphores(nc, ctx, "dt_")
        w = sb("w", [P, KD, MH])
        w_h, w_l = (sb(n, [P, KD, MH], F32R) for n in ("w_h", "w_l"))
        col = sb("col", [P, 3])
        z, e, dtT, dec = (sb(n, [P, TOK]) for n in ("z", "e", "dtT", "dec"))
        loaded, proj, chain, a_exp, minus_abs, log_done, dt_done, decayed, turned = (
            sem(n) for n in ("loaded", "proj", "chain", "a_exp", "minus_abs", "log_done", "dt_done", "decayed",
                             "turned"))
        expd, w_high, w_low = (sem(n) for n in ("expd", "w_high", "w_low"))

        def loads(sp):
            sp.dma_start(w[:], dram["m_wdt"]).then_inc(loaded, 16)
            sp.dma_start(col[:, 0:1], dram["m_dtb"]).then_inc(loaded, 16)
            sp.dma_start(col[:, 1:2], dram["m_alog"]).then_inc(loaded, 16)
            sp.dma_start(mem.cols[:], dram["m_cols"]).then_inc(loaded, 16)
            sp.dma_start(mem.w[:, 1], dram["m_first"][0, 0]).then_inc(mem.w_loaded[1], 16)
            sp.dma_start(mem.w[:, 0], dram["m_first"][0, 1]).then_inc(mem.w_loaded[0], 16)

        def round_weights(act):
            act.wait_ge(loaded, 64)
            act.activation(w_h[:], w[:], ACT.Copy).then_inc(w_high, 1)
            for slot in (1, 0):
                act.wait_ge(mem.w_loaded[slot], 16)
                act.activation(mem.w_h[:, slot], mem.w[:, slot], ACT.Copy).then_inc(mem.w_high, 1)

        def rest_of_weights(pool):
            pool.wait_ge(w_high, 1)
            pool.tensor_tensor(w_l[:], w[:], w_h[:], ALU.subtract).then_inc(w_low, 1)

        norm_phase(nc, core, "nm", add=True, rms_col=dram["m_norm"], sync=loads, scalar=round_weights,
                   gpsimd=rest_of_weights)
        ps = ctx.enter_context(nc.psum_tensor("dt_ps", [P, 2, HALF], F32))
        ps_t = ctx.enter_context(nc.psum_tensor("dt_pst", [P, NT, MH], F32))
        block = ctx.enter_context(nc.Block())

        @block.gpsimd
        def _(pool):
            for i, slot in enumerate((1, 0)):
                pool.wait_ge(mem.w_high, i + 1)
                pool.tensor_tensor(mem.w_l[:, slot], mem.w[:, slot], mem.w_h[:, slot],
                                   ALU.subtract).then_inc(mem.w_low, 1)

        @block.tensor
        def _(pe):
            pe.wait_ge(w_low, 1)
            for half in range(2):
                tok = slice(half * HALF, (half + 1) * HALF)
                for k in range(KD):
                    ins = split_product(pe, ps[:, half, :], w_h[:, k, :], w_l[:, k, :], core.xh[:, k, tok],
                                        core.xl[:, k, tok], k == 0, k == KD - 1)
            ins.then_inc(proj, 1)
            pe.wait_ge(dt_done, 1)
            for t in range(NT):
                ins = pe.transpose(ps_t[:, t, :], dtT[:, t * P:(t + 1) * P], core.ident)
            ins.then_inc(turned, 1)

        @block.scalar
        def _(act):
            act.activation(col[:, 2:3], col[:, 1:2], ACT.Exp).then_inc(a_exp, 1)
            act.wait_ge(minus_abs, 1)
            act.activation(e[:], e[:], ACT.Exp).then_inc(expd, 1)
            act.wait_ge(expd, 1)
            act.activation(e[:], e[:], ACT.Ln, bias=1.0).then_inc(log_done, 1)
            act.wait_ge(dt_done, 1)
            act.activation(dec[:], dtT[:], ACT.Exp, scale=col[:, 2:3]).then_inc(decayed, 1)
            act.wait_ge(turned, 1)
            act.activation(mem.dt[:], ps_t[:], ACT.Copy)

        @block.vector
        def _(dve):
            n_chain = [0]

            def link(ins):
                n_chain[0] += 1
                ins.then_inc(chain, 1)
                dve.wait_ge(chain, n_chain[0])

            link(dve.memset(mem.start[:], 0.0))
            for b in range(2):
                dve.tensor_copy(mem.start[:, b * SEQ:b * SEQ + P], core.ident)
            dve.memset(mem.ones[:], 1.0)
            dve.wait_ge(a_exp, 1)
            link(dve.tensor_scalar(col[:, 2:3], col[:, 2:3], -1.0, None, ALU.mult))
            dve.wait_ge(proj, 1)
            link(dve.tensor_scalar(z[:], ps[:, :, :].rearrange("p a n -> p (a n)"), col[:, 0:1], None, ALU.add))
            dve.scalar_tensor_tensor(out=e[:], in0=z[:], scalar=-1.0, in1=z[:], op0=ALU.mult,
                                     op1=ALU.min).then_inc(minus_abs, 1)
            dve.wait_ge(log_done, 1)
            dve.scalar_tensor_tensor(out=dtT[:], in0=z[:], scalar=0.0, in1=e[:], op0=ALU.max,
                                     op1=ALU.add).then_inc(dt_done, 1)
            dve.wait_ge(decayed, 1)
            link(dve.memset(dec[:, :].rearrange("p (b s) -> p b s", b=BATCH)[:, :, 0:1], 0.0))
            link(dve.tensor_copy(mem.dec_h[:], dec[:]))
            dve.tensor_tensor(mem.dec_l[:], dec[:], mem.dec_h[:], ALU.subtract)


def mix_phase(nc, core, mem, dram):
    with ExitStack() as ctx:
        sb = lambda n, shape, dt=F32: ctx.enter_context(nc.sbuf_tensor("mx_" + n, shape, dt))
        pb = lambda n, shape: ctx.enter_context(nc.psum_tensor("mx_" + n, shape, F32))
        sem = phase_semaphores(nc, ctx, "mx_")
        w, w_h, w_l, w_loaded = mem.w, mem.w_h, mem.w_l, mem.w_loaded
        wout_h, wout_l = (sb(n, [P, GM, D], F32R) for n in ("wout_h", "wout_l"))
        yw_h, yw_l = (sb(n, [P, 2, 2, P], F32R) for n in ("yw_h", "yw_l"))
        cols = sb("cols", [P, NCOL])
        sel = sb("sel", [P, 2, 2, P], F32R)
        cacc = sb("cacc", [P, 2, HALF])
        G = sb("G", [P, BATCH, SEQ + P])
        hidT = sb("hidT", [P, 2, HALF])
        gateT = sb("gateT", [P, 2, HALF])
        hid = sb("hid", [P, 2, 4, P])
        L = sb("L", [P, 2, 2 * SEQ + 2 * P])
        M = sb("M", [P, 2, 2, 2 * SEQ + 2 * P])
        yg = sb("yg", [P, 2, HALF])
        yw = sb("yw", [P, GM, TOK])
        sqsum = sb("sqsum", [P, TOK])
        rms = sb("rms", [P, 3, NT])
        ps_hid = [pb(f"ps_hid{i}", [P, HALF]) for i in range(2)]
        ps_gate, ps_turn, ps_y, ps_misc = (pb(n, [P, HALF]) for n in ("ps_gate", "ps_turn", "ps_y", "ps_misc"))
        ps_dec = [pb(f"ps_dec{i}", [P, HALF]) for i in range(2)]
        flat_M = M[:, :, :, :].rearrange("p a b n -> p (a b n)")
        bT, cT = flat_M[:, 0:TOK], flat_M[:, TOK:2 * TOK]
        AHEAD = {"conv_done": 2, "scanned": 2, "m_ready": 2, "gate_kept": 1, "gate_ready": 3, "values_kept": 1,
                 "y2_done": 2, "yg_done": 2, "yw_done": 2, "sq_added": 2, "out_added": 4, "out_ready": 1,
                 "g_ready": 4, "hidT_ready": 2, "sq_ready": 2, "w_low": 1, "var_ready": 1}
        plain = ("sel_ready part_high part_low part_used cols_ready hid_ready tap_done conv_chain g_kept turned "
                 "dec_ready y_ready sum_ready std_ready chain").split()
        s = {n: sem(n) for n in [*plain, *AHEAD] if n != "w_low"}
        s.update(w_high=mem.w_high, w_low=mem.w_low)
        block = ctx.enter_context(nc.Block())
        CONVS = STEPS + 4
        PAIRS = GM // 2
        SPLITS = 1 + GM + PAIRS
        LOADS = (SPLITS // 2, SPLITS - SPLITS // 2)
        N_FIRST = PAIRS - 1
        units = ([(0, j) for j in range(N_FIRST)] + [(1, j) for j in range(N_FIRST)]
                 + [(0, PAIRS - 1), (1, PAIRS - 1)] + [(t, j) for t in range(2, NT) for j in range(PAIRS)])
        UNITS = len(units)
        SUMS_AT, ROOT_AT = 2 * PAIRS, 2 * PAIRS + 2
        T1 = TAPS + 1

        def done(name, count):
            return AHEAD.get(name, 0) + count

        bc_banks = (*ps_hid, ps_gate, ps_y)
        out_banks = (ps_misc, ps_turn, *ps_dec)

        def conv_bank(unit, half):
            return bc_banks[unit] if isinstance(unit, int) and unit < 4 else ps_hid[half]

        def col(i):
            return cols[:, i:i + 1]

        def column(i):
            return cols[:, bass.ds(i, 1)]

        def group_steps(eng, body):
            for q in range(4):
                body(q // 2, q, q)
            with eng.Fori(1, STEPS // 4 - 1) as i:
                for q in range(4):
                    body(2 * i + q // 2, 4 * i + q, q)
            for q in range(4):
                body(GM - 2 + q // 2, STEPS - 4 + q, q)

        def is_first(step):
            return isinstance(step, int) and step == 0

        def is_last(step):
            return isinstance(step, int) and step == STEPS - 1

        @block.sync
        def _(sp):
            with sp.Fori(0, MG) as g:
                def load_tile(tile):
                    sp.wait_ge(s["w_low"], done("w_low", SPLITS * g + tile))
                    sp.dma_start(w[:, tile % 2], dram["m_w"][g, tile - 1]).then_inc(w_loaded[tile % 2], 16)

                for tile in range(1, GM):
                    load_tile(tile)
                for j in range(PAIRS):
                    sp.wait_ge(s["w_low"], done("w_low", SPLITS * g + GM + j))
                    sp.dma_start(w[:, j % 2].rearrange("p a k n -> p a (k n)"),
                                 dram["m_wout"][g, :, 2 * j:2 * j + 2]).then_inc(w_loaded[j % 2], 16)
                for i in range(2):
                    sp.wait_ge(s["w_low"], done("w_low", SPLITS * (g + 1)))
                    sp.dma_start(w[:, 1 - i], dram["m_first"][g + 1, i]).then_inc(w_loaded[1 - i], 16)

        @block.tensor
        def _(pe):
            with pe.Fori(0, MG) as g:
                def output_units(span):
                    for p in span:
                        t, j = units[p]
                        if j == 0:
                            pe.wait_ge(s["out_added"], done("out_added", NT * g + t - 3))
                        pe.wait_ge(s["part_low"], UNITS * g + p + 1)
                        if t == 0:
                            pe.wait_ge(s["w_low"], done("w_low", SPLITS * g + 1 + GM + j + 1))
                        for m in range(2):
                            ins = split_product(pe, out_banks[t % 4][:], yw_h[:, p % 2, m, :], yw_l[:, p % 2, m, :],
                                                wout_h[:, 2 * j + m, :], wout_l[:, 2 * j + m, :],
                                                j == 0 and m == 0, j == PAIRS - 1 and m == 1)
                        ins.then_inc(s["out_ready"] if j == PAIRS - 1 else s["part_used"], 1)

                def project(ps, slot, which, half):
                    tok = slice(half * HALF, (half + 1) * HALF)
                    for k in range(KD):
                        ins = split_product(pe, ps[:], w_h[:, slot, which, k, :], w_l[:, slot, which, k, :],
                                            core.xh[:, k, tok], core.xl[:, k, tok], k == 0, k == KD - 1)
                    return ins

                pe.wait_ge(s["w_low"], done("w_low", SPLITS * g + 1))
                pe.wait_ge(s["conv_done"], done("conv_done", CONVS * g))
                pe.wait_ge(s["gate_kept"], done("gate_kept", STEPS * g))
                pe.wait_ge(s["var_ready"], done("var_ready", g))
                for n in range(4):
                    project(bc_banks[n], 1, n // 2, n % 2).then_inc(s["hid_ready"], 1)

                def values_and_gate(tile, step, q):
                    half, slot = q % 2, q // 2
                    if half == 0:
                        pe.wait_ge(s["w_low"], done("w_low", SPLITS * g + tile + 2))
                    pe.wait_ge(s["conv_done"], done("conv_done", CONVS * g + 4 + step - 1))
                    project(ps_hid[half], slot, 0, half).then_inc(s["hid_ready"], 1)
                    pe.wait_ge(s["gate_kept"], done("gate_kept", STEPS * g + step))
                    project(ps_gate, slot, 1, half).then_inc(s["gate_ready"], 1)

                def decays(tile, step, q):
                    half = q % 2
                    if half == 0:
                        pe.wait_ge(s["sel_ready"], GM * g + tile + 1)
                    tok = slice(half * HALF, (half + 1) * HALF)
                    for hh in range(2):
                        pe.wait_ge(s["scanned"], done("scanned", 2 * (STEPS * g + step - 1) + hh + 1))
                        pe.matmul(ps_dec[hh][:], sel[:, q // 2, hh, :], mem.dec_h[:, tok], start=True, stop=False)
                        ins = pe.matmul(ps_dec[hh][:], sel[:, q // 2, hh, :], mem.dec_l[:, tok], start=False,
                                        stop=True)
                        ins.then_inc(s["dec_ready"], 1)

                def turn_values(step, q):
                    half = q % 2
                    pe.wait_ge(s["hidT_ready"], done("hidT_ready", CONVS * g + 4 + step + 1))
                    pe.wait_ge(s["values_kept"], done("values_kept", STEPS * g + step))
                    for t in range(4):
                        ins = pe.transpose(ps_turn[:, t * P:(t + 1) * P], hidT[:, half, t * P:(t + 1) * P],
                                           core.ident)
                    ins.then_inc(s["turned"], 1)

                def sums(step, q):
                    half = q % 2
                    pe.wait_ge(s["m_ready"], done("m_ready", 2 * (STEPS * g + step) + 2))
                    pe.wait_ge(s["values_kept"], done("values_kept", STEPS * g + step + 1))
                    pe.wait_ge(s["y2_done"], done("y2_done", STEPS * g + step))
                    for hh in range(2):
                        rows = slice(hh * MP, (hh + 1) * MP)
                        for b in range(2):
                            pe.matmul(ps_y[rows, b * SEQ:(b + 1) * SEQ], hid[:, half, 2 * b, rows],
                                      M[:, half, hh, b * SEQ:(b + 1) * SEQ], start=True, stop=False)
                            ins = pe.matmul(ps_y[rows, b * SEQ + P:(b + 1) * SEQ], hid[:, half, 2 * b + 1, rows],
                                            M[:, half, hh, 2 * SEQ + b * P:2 * SEQ + (b + 1) * P],
                                            start=False, stop=True)
                    ins.then_inc(s["y_ready"], 1)

                values_and_gate(0, 0, 0)
                pe.wait_ge(s["out_added"], done("out_added", NT * g))
                decays(0, 0, 0)
                pe.wait_ge(s["hidT_ready"], done("hidT_ready", CONVS * g + 4))
                for b in range(BATCH):
                    if b >= 2:
                        pe.wait_ge(s["g_kept"], BATCH * g + b - 1)
                    ps = (ps_misc, ps_turn)[b % 2]
                    pe.matmul(ps[:, 0:SEQ], bT[:, b * SEQ:b * SEQ + P], cT[:, b * SEQ:(b + 1) * SEQ],
                              start=True, stop=True)
                    pe.matmul(ps[:, SEQ:SEQ + P], bT[:, b * SEQ + P:(b + 1) * SEQ],
                              cT[:, b * SEQ + P:(b + 1) * SEQ], start=True, stop=True).then_inc(s["g_ready"], 1)
                pe.wait_ge(s["g_kept"], BATCH * (g + 1))

                def step_of(tile, step, q):
                    if not is_first(step):
                        sums(step - 1, (q + 3) % 4)
                    turn_values(step, q)
                    if not is_last(step):
                        nxt = (tile if q % 2 == 0 else tile + 1, step + 1, (q + 1) % 4)
                        values_and_gate(*nxt)
                        decays(*nxt)

                group_steps(pe, step_of)
                output_units(range(N_FIRST))
                sums(STEPS - 1, 3)
                output_units(range(N_FIRST, SUMS_AT))

                pe.wait_ge(s["sq_added"], done("sq_added", STEPS * (g + 1)))
                pe.wait_ge(s["y2_done"], done("y2_done", STEPS * (g + 1)))
                for t in range(NT):
                    ins = pe.matmul(ps_y[:, t:t + 1], sqsum[:, t * P:(t + 1) * P], mem.ones[:], start=True, stop=True)
                ins.then_inc(s["sum_ready"], 1)
                output_units(range(SUMS_AT, UNITS))

        @block.scalar
        def _(act):
            def round_weights(slot, loads, gates):
                act.wait_ge(w_loaded[slot], 16 * loads)
                act.wait_ge(s["gate_ready"], done("gate_ready", gates))
                act.activation(w_h[:, slot], w[:, slot], ACT.Copy).then_inc(s["w_high"], 1)

            with act.Fori(0, MG) as g:
                act.wait_ge(s["cols_ready"], g + 1)

                def first_tap(tile, unit, half):
                    act.wait_ge(s["hid_ready"], CONVS * g + unit + 1)
                    act.wait_ge(s["hidT_ready"], done("hidT_ready", CONVS * g + unit - 1))
                    act.activation(cacc[:, half, :], conv_bank(unit, half)[:], ACT.Identity,
                                   scale=col(T1 * tile + TAPS - 1),
                                   bias=col(T1 * tile + TAPS)).then_inc(s["tap_done"], 1)

                def silu_of_conv(out, unit, half):
                    act.wait_ge(s["conv_done"], done("conv_done", CONVS * g + unit + 1))
                    act.activation(out, cacc[:, half, :], ACT.Silu).then_inc(s["hidT_ready"], 1)

                for n in range(4):
                    first_tap(GM + n // 2, n, n % 2)
                    if n:
                        m = n - 1
                        silu_of_conv((bT, cT)[m // 2][:, (m % 2) * HALF:(m % 2 + 1) * HALF], m, m % 2)
                silu_of_conv(cT[:, HALF:], 3, 1)

                def round_pair(j):
                    act.wait_ge(w_loaded[j % 2], 16 * (LOADS[j % 2] * g + (GM // 2 + j % 2) + j // 2 + 1))
                    act.wait_ge(s["out_ready"], done("out_ready", NT * g))
                    act.activation(wout_h[:, 2 * j:2 * j + 2, :], w[:, j % 2].rearrange("p a k n -> p a (k n)"),
                                   ACT.Copy).then_inc(s["w_high"], 1)

                def unit_used(p):
                    lasts = [j == PAIRS - 1 for _, j in units[:p + 1]]
                    if lasts[-1]:
                        act.wait_ge(s["out_ready"], done("out_ready", NT * g + sum(lasts)))
                    else:
                        act.wait_ge(s["part_used"], (UNITS - NT) * g + lasts.count(False))

                def round_unit(p):
                    t, j = units[p]
                    if t == 0:
                        act.wait_ge(s["yw_done"], done("yw_done", STEPS * g + 4 * (j + 1)))
                    if p >= 2:
                        unit_used(p - 2)
                    act.activation(yw_h[:, p % 2], yw[:, 2 * j:2 * j + 2, t * P:(t + 1) * P],
                                   ACT.Copy).then_inc(s["part_high"], 1)

                def weigh_and_square(tile, step, q):
                    half = q % 2
                    act.wait_ge(s["yg_done"], done("yg_done", STEPS * g + step + 1))
                    act.activation(yw[:, tile, half * HALF:(half + 1) * HALF], yg[:, half, :], ACT.Copy,
                                   scale=col(T1 * (GM + 2) + GM + tile)).then_inc(s["yw_done"], 1)
                    act.wait_ge(s["yw_done"], done("yw_done", STEPS * g + step + 1))
                    act.activation(yg[:, half, :], yg[:, half, :], ACT.Square).then_inc(s["sq_ready"], 1)

                def step_of(tile, step, q):
                    half = q % 2
                    first_tap(tile, 4 + step, half)
                    act.wait_ge(s["gate_ready"], done("gate_ready", STEPS * g + step + 1))
                    act.wait_ge(s["yg_done"], done("yg_done", STEPS * g + step - 1))
                    act.activation(gateT[:, half, :], ps_gate[:], ACT.Silu).then_inc(s["gate_kept"], 1)
                    silu_of_conv(hidT[:, half, :], 4 + step, half)
                    if is_first(step):
                        for b in range(BATCH):
                            act.wait_ge(s["g_ready"], done("g_ready", BATCH * g + b + 1))
                            act.activation(G[:, b, :], (ps_misc, ps_turn)[b % 2][:, 0:SEQ + P],
                                           ACT.Copy).then_inc(s["g_kept"], 1)
                    nxt = tile + 1
                    if half == 0 and nxt < GM:
                        round_weights(nxt % 2, LOADS[nxt % 2] * g + nxt // 2 + 1 + nxt % 2,
                                      STEPS * g + 2 * (nxt - 1))
                    if step == STEPS - 1:
                        round_unit(0)
                        round_unit(1)
                    if step >= STEPS - PAIRS:
                        round_pair(step - (STEPS - PAIRS))
                    if step == STEPS - 1:
                        round_unit(2)
                    if not is_first(step):
                        weigh_and_square(tile if q % 2 else tile - 1, step - 1, (q + 3) % 4)

                for step in range(STEPS):
                    step_of(step // 2, step, step % 4)
                for p in range(3, 2 * N_FIRST):
                    round_unit(p)
                weigh_and_square(GM - 1, STEPS - 1, 3)
                for p in range(2 * N_FIRST, ROOT_AT):
                    round_unit(p)
                act.wait_ge(s["var_ready"], done("var_ready", g + 1))
                act.activation(rms[:, 1, :], rms[:, 0, :], ACT.Sqrt).then_inc(s["std_ready"], 1)
                for u in range(ROOT_AT, UNITS):
                    round_unit(u)
                    if u in (UNITS // 2, UNITS // 2 + PAIRS):
                        i = int(u > UNITS // 2)
                        round_weights(1 - i, LOADS[1 - i] * (g + 1) + 1, STEPS * (g + 1))

        @block.gpsimd
        def _(pool):
            for name, count in AHEAD.items():
                pool.sem_inc(s[name], count)
            def rest_of_weights(slot, g, index):
                pool.wait_ge(s["w_high"], SPLITS * g + index + 1)
                pool.tensor_tensor(w_l[:, slot], w[:, slot], w_h[:, slot], ALU.subtract).then_inc(s["w_low"], 1)

            with pool.Fori(0, MG) as g:
                pool.wait_ge(s["g_kept"], BATCH * (g + 1))
                pool.wait_ge(s["cols_ready"], g + 1)

                def add_squares(step, q):
                    half = q % 2
                    total = sqsum[:, half * HALF:(half + 1) * HALF]
                    pool.wait_ge(s["sq_ready"], done("sq_ready", STEPS * g + step + 1))
                    pool.wait_ge(s["sq_added"], done("sq_added", STEPS * g + step - 1))
                    pool.tensor_tensor(total, total, yg[:, half, :], ALU.add).then_inc(s["sq_added"], 1)

                def step_of(tile, step, q):
                    half = q % 2
                    for hh in range(2):
                        pool.wait_ge(s["scanned"], done("scanned", 2 * (STEPS * g + step) + hh + 1))
                        for lo, n, g0 in ((0, SEQ, 0), (2 * SEQ, P, SEQ)):
                            ins = pool.tensor_tensor(
                                M[:, half, hh, lo:lo + 2 * n].rearrange("p (b i) -> p b i", b=2),
                                L[:, hh, lo:lo + 2 * n].rearrange("p (b i) -> p b i", b=2),
                                G[:, 2 * half:2 * half + 2, g0:g0 + n], ALU.mult)
                        ins.then_inc(s["m_ready"], 1)
                    if half == 0 and not (isinstance(step, int) and step == STEPS - 2):
                        rest_of_weights(1 - q // 2, g, tile + 2)
                    if not is_first(step):
                        add_squares(step - 1, (q + 3) % 4)

                group_steps(pool, step_of)
                add_squares(STEPS - 1, 3)
                rest_of_weights(1, g + 1, 0)
                rest_of_weights(0, g + 1, 1)

        @block.vector
        def _(dve):
            with dve.Fori(0, MG) as g:
                def pick_heads(tile, slot):
                    dve.tensor_copy(sel[:, slot], core.consts[:, bass.ds(C_ID + GH * g + 2 * tile, 2)].unsqueeze(
                        2).broadcast_to((P, 2, P))).then_inc(s["sel_ready"], 1)

                pick_heads(0, 0)
                dve.tensor_copy(cols[:], mem.cols[:, g, :])
                dve.memset(sqsum[:], 0.0).then_inc(s["cols_ready"], 1)
                dve.wait_ge(s["cols_ready"], g + 1)

                def conv(tile, unit, half):
                    pick = col if isinstance(tile, int) else column
                    acc = cacc[:, half, :].rearrange("p (b s) -> p b s", b=2)
                    src = conv_bank(unit, half)[:, :].rearrange("p (b s) -> p b s", b=2)
                    dve.wait_ge(s["tap_done"], CONVS * g + unit + 1)
                    for back in range(1, TAPS):
                        if back > 1:
                            dve.wait_ge(s["conv_chain"], 2 * (CONVS * g + unit) + back - 1)
                        ins = dve.scalar_tensor_tensor(
                            out=acc[:, :, back:], in0=src[:, :, 0:SEQ - back], scalar=pick(T1 * tile + TAPS - 1 - back),
                            in1=acc[:, :, back:], op0=ALU.mult, op1=ALU.add)
                        ins.then_inc(s["conv_chain" if back < TAPS - 1 else "conv_done"], 1)

                for n in range(4):
                    conv(GM + n // 2, n, n % 2)

                def scans(step, q):
                    for hh in range(2):
                        dve.wait_ge(s["dec_ready"], 2 * (STEPS * g + step) + hh + 1)
                        dve.wait_ge(s["m_ready"], done("m_ready", 2 * (STEPS * g + step - 1) + hh + 1))
                        dve.tensor_tensor_scan(L[:, hh, 0:2 * SEQ], ps_dec[hh][:], mem.start[:], 0.0,
                                               ALU.mult, ALU.add)
                        for b in range(2):
                            ins = dve.tensor_tensor_scan(L[:, hh, 2 * SEQ + b * P:2 * SEQ + (b + 1) * P],
                                                         ps_dec[hh][:, b * SEQ + P:(b + 1) * SEQ], core.ident, 0.0,
                                                         ALU.mult, ALU.add)
                        ins.then_inc(s["scanned"], 1)

                def gated(tile, step, q):
                    half = q % 2
                    pick = col if isinstance(tile, int) else column
                    dve.wait_ge(s["y_ready"], STEPS * g + step + 1)
                    dve.wait_ge(s["sq_added"], done("sq_added", STEPS * g + step - 1))
                    dve.scalar_tensor_tensor(out=yg[:, half, :], in0=hidT[:, half, :],
                                             scalar=pick(T1 * (GM + 2) + tile), in1=ps_y[:], op0=ALU.mult,
                                             op1=ALU.add).then_inc(s["y2_done"], 1)
                    dve.wait_ge(s["y2_done"], done("y2_done", STEPS * g + step + 1))
                    dve.wait_ge(s["gate_kept"], done("gate_kept", STEPS * g + step + 1))
                    dve.tensor_tensor(yg[:, half, :], yg[:, half, :], gateT[:, half, :],
                                      ALU.mult).then_inc(s["yg_done"], 1)

                def keep_values(tile, step, q):
                    half = q % 2
                    dve.wait_ge(s["turned"], STEPS * g + step + 1)
                    dts = mem.dt[:, 4 * half:4 * half + 4, bass.ds(GH * g + 2 * tile, 2)]
                    dve.tensor_tensor(hid[:, half].rearrange("p t (h d) -> p t h d", h=2),
                                      ps_turn[:, :].rearrange("p (t h d) -> p t h d", t=4, h=2),
                                      dts.unsqueeze(3).broadcast_to((P, 4, 2, MP)), ALU.mult).then_inc(
                                          s["values_kept"], 1)

                def rest_of_pair(j):
                    dve.wait_ge(s["w_low"], done("w_low", SPLITS * g + 1 + GM + j))
                    dve.wait_ge(s["w_high"], SPLITS * g + 1 + GM + j + 1)
                    dve.tensor_tensor(wout_l[:, 2 * j:2 * j + 2, :], w[:, j % 2].rearrange("p a k n -> p a (k n)"),
                                      wout_h[:, 2 * j:2 * j + 2, :], ALU.subtract).then_inc(s["w_low"], 1)

                def rest_of_unit(p):
                    t, j = units[p]
                    dve.wait_ge(s["part_high"], UNITS * g + p + 1)
                    dve.tensor_tensor(yw_l[:, p % 2], yw[:, 2 * j:2 * j + 2, t * P:(t + 1) * P], yw_h[:, p % 2],
                                      ALU.subtract).then_inc(s["part_low"], 1)

                def add_to_residual(t):
                    dve.wait_ge(s["out_ready"], done("out_ready", NT * g + t + 1))
                    xt = core.x[:, t, :]
                    dve.scalar_tensor_tensor(out=xt, in0=out_banks[t % 4][:], scalar=rms[:, 2, t:t + 1],
                                             in1=xt, op0=ALU.mult, op1=ALU.add).then_inc(s["out_added"], 1)

                def step_of(tile, step, q):
                    if q % 2 == 0 and not (isinstance(step, int) and step == STEPS - 2):
                        pick_heads(tile + 1, 1 - q // 2)
                    conv(tile, 4 + step, q % 2)
                    scans(step, q)
                    at_end = isinstance(step, int) and step == STEPS - 1
                    if at_end:
                        rest_of_unit(0)
                        rest_of_unit(1)
                        rest_of_pair(2)
                    if not is_first(step):
                        gated(tile if q % 2 else tile - 1, step - 1, (q + 3) % 4)
                    if at_end:
                        rest_of_unit(2)
                    keep_values(tile, step, q)
                    if isinstance(step, int) and STEPS - PAIRS < step < STEPS - 1:
                        rest_of_pair(step - (STEPS - PAIRS + 1))

                group_steps(dve, step_of)
                for p in range(3, 2 * N_FIRST - 1):
                    rest_of_unit(p)
                rest_of_pair(PAIRS - 1)
                gated(GM - 1, STEPS - 1, 3)
                for p in range(2 * N_FIRST - 1, ROOT_AT):
                    rest_of_unit(p)
                dve.wait_ge(s["sum_ready"], g + 1)
                dve.tensor_scalar(rms[:, 0, :], ps_y[:, 0:NT], 1.0 / (GM * P), EPS, ALU.mult,
                                  ALU.add).then_inc(s["var_ready"], 1)
                dve.wait_ge(s["std_ready"], g + 1)
                dve.reciprocal(rms[:, 2, :], rms[:, 1, :]).then_inc(s["chain"], 1)
                dve.wait_ge(s["chain"], g + 1)
                for p in range(ROOT_AT, UNITS):
                    rest_of_unit(p)
                    if p < ROOT_AT + 2:
                        add_to_residual(p - ROOT_AT)
                    elif p % PAIRS == 1:
                        add_to_residual(p // PAIRS - 1)
                add_to_residual(NT - 1)


class MixerArrays:

    def __init__(self, nc, ctx):
        sem = phase_semaphores(nc, ctx, "m_")
        self.w_loaded = [sem(f"w_loaded{i}") for i in range(2)]
        self.w_high, self.w_low = sem("w_high"), sem("w_low")
        sb = lambda n, shape, dt=F32: ctx.enter_context(nc.sbuf_tensor("m_" + n, shape, dt))
        self.cols = sb("cols", [P, MG, NCOL])
        self.dec_h, self.dec_l = (sb(n, [P, TOK], F32R) for n in ("dec_h", "dec_l"))
        self.dt = sb("dt", [P, NT, MH])
        self.start = sb("start", [P, 2 * SEQ])
        self.ones = sb("ones", [P, 1])
        self.w = sb("w", [P, 2, 2, KD, P])
        self.w_h, self.w_l = (sb(n, [P, 2, 2, KD, P], F32R) for n in ("w_h", "w_l"))


def mamba_phase(nc, core, dram):
    with ExitStack() as ctx:
        mem = MixerArrays(nc, ctx)
        dt_phase(nc, core, mem, dram)
        mix_phase(nc, core, mem, dram)


def program(nc, dram, out, parts=None):
    with ExitStack() as ctx:
        core = Core(nc, ctx)
        load_phase(nc, core, dram["x"], dram["consts"])
        for part in parts or ("attn0", "ffn0", "mamba", "ffn0", "across", "ffn1", "attn1", "ffn1"):
            if part == "attn0":
                attention_phase(nc, core, "a0", dram["a0_w"], dram["a0_wo"], KV_HEADS, True,
                                dram["a0_b"], dram["a0_bo"])
            elif part == "attn1":
                attention_phase(nc, core, "a1", dram["a1_w"], dram["a1_wo"], HEADS, False)
            elif part == "ffn0":
                ffn_phase(nc, core, f"f{core.ln_runs}", dram["f0_gu"], dram["f0_down"])
            elif part == "ffn1":
                quant = {k: dram["f1_" + k] for k in ("a", "da", "b", "db", "s_gu", "s_d")}
                quant_ffn_phase(nc, core, f"f{core.ln_runs}", dram["f1_gu"], dram["f1_down"], quant)
            elif part == "across":
                with nc.sbuf_tensor("xT", [P, KD, TOK], F32) as xT:
                    norm_phase(nc, core, "nab", whole=xT)
                    across_batch_phase(nc, core, xT)
            elif part == "mamba":
                mamba_phase(nc, core, dram)
        store_phase(nc, core, out)


def rope_tables():
    inv = (1.0 / np.float32(10000.0) ** (np.arange(0, HD, 2, dtype=np.float32) / np.float32(HD))).astype(np.float32)
    ang = np.arange(SEQ, dtype=np.float32)[:, None] * inv[None, :]
    cos, sin = np.cos(ang).astype(np.float32), np.sin(ang).astype(np.float32)
    return np.concatenate([cos, cos], 1), np.concatenate([-sin, sin], 1)


def constants():
    c = np.zeros((P, NCONST), np.float32)
    c[:, C_ID:C_ID + P] = np.eye(P, dtype=np.float32)
    c[:, C_HM:C_HM + HPT] = np.arange(P)[:, None] // HD == np.arange(HPT)[None, :]
    cos, sin = rope_tables()
    c[:, C_COS:C_COS + BT * HD] = cos.reshape(BT, P, HD).transpose(1, 0, 2).reshape(P, BT * HD)
    c[:, C_SIN:C_SIN + BT * HD] = sin.reshape(BT, P, HD).transpose(1, 0, 2).reshape(P, BT * HD)
    c[:, C_TRI:C_TRI + P] = np.where(np.arange(P)[None, :] > np.arange(P)[:, None], MASKED, 0.0)
    return c


def k_major(w):
    return np.ascontiguousarray(w.T.reshape(w.shape[1] // P, P, w.shape[0]).transpose(1, 0, 2))


def pad_to(a, n, axis):
    shape = list(a.shape)
    shape[axis] = n - shape[axis]
    return np.concatenate([a, np.zeros(shape, a.dtype)], axis)


def ffn_tiles(gate, up, down):
    g, u = (pad_to(w, F_PAD, 0).reshape(FT, P, KD, P).transpose(0, 3, 2, 1) for w in (gate, up))
    return (np.ascontiguousarray(np.stack([g, u], 2)),
            np.ascontiguousarray(pad_to(down, F_PAD, 1).T.reshape(FT, P, D)))


def layout(i):
    a = {k: np.asarray(v) for k, v in i.items()}
    d = {"x": a["L0_attn_a_x"].reshape(TOK, D), "consts": constants()}
    w, b = a["L0_attn_a_w_qkv"], a["L0_attn_a_b_qkv"]
    halves = np.concatenate([np.arange(0, HD, 2), np.arange(1, HD, 2)])
    group = HEADS // KV_HEADS
    q_rows = (np.arange(D).reshape(KV_HEADS, group, HD).transpose(1, 0, 2)[:, :, halves]).reshape(-1)
    k_rows = D + np.arange(KV_HEADS * HD).reshape(KV_HEADS, HD)[:, halves].reshape(-1)
    v_rows = D + KV_HEADS * HD + np.arange(KV_HEADS * HD)
    rows = np.concatenate([q_rows, k_rows, v_rows])
    d["a0_w"] = k_major(w[rows])
    d["a0_b"] = b[rows]
    o_cols = np.arange(D).reshape(KV_HEADS, group, HD).transpose(1, 0, 2).reshape(-1)
    d["a0_wo"] = k_major(a["L0_attn_a_w_o"][:, o_cols])
    d["a0_bo"] = a["L0_attn_a_b_o"]
    d["a1_w"] = k_major(np.concatenate([a["L1_attn_b_" + n] for n in ("Wq", "Wk", "Wv")], 0))
    d["a1_wo"] = k_major(a["L1_attn_b_Wo"])
    d["f0_gu"], d["f0_down"] = ffn_tiles(a["L0_ffn_W_gate"], a["L0_ffn_W_up"], a["L0_ffn_W_down"])
    q = {k[7:]: v for k, v in a.items() if k.startswith("L1_ffn_")}
    d["f1_gu"], d["f1_down"] = ffn_tiles(q["gate_q"], q["up_q"], q["down_q"])
    ab = np.concatenate([q["gate_A"], q["up_A"]], 1)
    d["f1_a"] = np.ascontiguousarray(pad_to(ab, P, 1).reshape(KD, P, P).transpose(1, 0, 2))
    d["f1_da"] = np.ascontiguousarray(pad_to(q["down_A"], F_PAD, 0).reshape(FT, P, RANK).transpose(1, 0, 2))
    g_b, u_b = (pad_to(q[n], F_PAD, 1) for n in ("gate_B", "up_B"))
    d["f1_b"] = np.stack([np.concatenate([g_b, np.zeros_like(g_b)], 0), np.concatenate([np.zeros_like(u_b), u_b], 0)],
                         1)
    d["f1_db"] = q["down_B"]
    d["f1_s_gu"] = np.stack([pad_to(q[n], F_PAD, 0).reshape(FT, P).T for n in ("gate_scale", "up_scale")], 1)
    d["f1_s_d"] = q["down_scale"]
    w = a["L0_attn_b_in_proj_w"]
    gate = w[:D_INNER].reshape(MG, GM, P, KD, P)
    hid = w[D_INNER:2 * D_INNER].reshape(MG, GM, P, KD, P)
    tiles = np.stack([hid, gate], 2).transpose(0, 1, 5, 2, 4, 3)
    d["m_w"] = np.ascontiguousarray(tiles[:, 1:])
    bc = w[2 * D_INNER:2 * D_INNER + 2 * MG * MN].reshape(2, MG, P, KD, P)
    first = np.stack([bc.transpose(1, 4, 0, 3, 2), tiles[:, 0]], 1)
    d["m_first"] = np.concatenate([first, first[:1]], 0)
    d["m_wdt"] = k_major(w[2 * D_INNER + 2 * MG * MN:])
    d["m_wout"] = np.ascontiguousarray(a["L0_attn_b_out_proj_w"].T.reshape(MG, GM, P, D).transpose(0, 2, 1, 3))
    taps = np.concatenate([a["L0_attn_b_conv_w"], a["L0_attn_b_conv_b"][:, None]], 1)
    t_hid = taps[:D_INNER].reshape(MG, GM, P, TAPS + 1)
    t_bc = taps[D_INNER:].reshape(2, MG, P, TAPS + 1).transpose(1, 0, 2, 3)
    cols = np.concatenate([t_hid, t_bc], 1).transpose(2, 0, 1, 3).reshape(P, MG, -1)
    per_feature = lambda v: v.reshape(MG, GM, P).transpose(2, 0, 1)
    dp = per_feature(np.repeat(a["L0_attn_b_Dp"], MP))
    d["m_cols"] = np.ascontiguousarray(np.concatenate([cols, dp, per_feature(a["L0_attn_b_gnorm_w"])], 2))
    d["m_dtb"] = a["L0_attn_b_dt_bias"][:, None]
    d["m_alog"] = a["L0_attn_b_A_log"][:, None]
    d["m_norm"] = np.ascontiguousarray(a["L0_attn_b_norm_w"].reshape(KD, P).T)
    return {k: np.ascontiguousarray(v) for k, v in d.items()}


def kernel(**inputs):
    import concourse.bacc as _bacc
    from concourse.bass_utils import run_bass_kernel_spmd as _run

    nc = _bacc.Bacc("TRN2", target_bir_lowering=False, num_devices=1)
    arrays = layout(inputs)
    dram = {k: nc.dram_tensor(f"in_{k}", v.shape, mybir.dt.from_np(v.dtype), kind="ExternalInput").ap()
            for k, v in arrays.items()}
    out = nc.dram_tensor("out_x", (TOK, D), F32, kind="ExternalOutput").ap()
    program(nc, dram, out)
    r = _run(nc, [{f"in_{k}": v for k, v in arrays.items()}], core_ids=[0])
    return r.results[0]["out_x"].reshape(BATCH, SEQ, D)
```
